# Optimizing a Trainium2 kernel written in Bass

```python
import numpy as np
import jax
import jax.numpy as jnp

def _softmax(x, axis=-1):
    return jax.nn.softmax(x, axis=axis)

def _gelu(x):
    return jax.nn.gelu(x, approximate=True)

def _silu(x):
    return jax.nn.silu(x)

def _sigmoid(x):
    return jax.nn.sigmoid(x)

def _layernorm(x, axis=-1, eps=1e-05):
    m = jnp.mean(x, axis=axis, keepdims=True)
    v = jnp.var(x, axis=axis, keepdims=True)
    return (x - m) / jnp.sqrt(v + eps)

def _scatter_add(tgt, idx, src, axis=0):
    return tgt.at[idx].add(src)

def _segment_sum(src, seg, n):
    return jax.ops.segment_sum(src, seg, n)
kernel_name = 'mk_gps_d1_gnn_r32_78bc09'

def setup_inputs(seed: int=0):
    np.random.seed(seed)
    _w = jnp.asarray

    def _rec_inputs():
        import jax
        import jax.numpy as jnp
        _gk = jax.random.key(seed)
        x = -8.776e-05 + 1 * jax.random.normal(jax.random.fold_in(_gk, 1), (3125, 256), jnp.float32)
        src = jax.random.randint(jax.random.fold_in(_gk, 2), (50000,), 0, 3125, jnp.int32)
        dst = jnp.minimum((3125 * jax.random.uniform(jax.random.fold_in(_gk, 3), (50000,)) ** 2.0).astype(jnp.int32), 99999)
        _o = jnp.argsort(dst, stable=True)
        src = src[_o]
        dst = dst[_o]
        edge_type_3 = jax.random.randint(jax.random.fold_in(_gk, 12), (50000,), 0, 3, jnp.int32)
        return (x, src, dst, edge_type_3)
    x, src, dst, edge_type_3 = _rec_inputs()

    def _L0_gnn_setup():
        import jax, jax.numpy as jnp
        import numpy as np
        H = 4
        DH = 64
        HID = 256
        EPS = 1e-05
        N_NODES = 625
        N_EDGES = 10000
        N_LAYERS = 3

        def _layer_norm(x, g, b):
            mu = jnp.mean(x, axis=-1, keepdims=True)
            var = jnp.mean((x - mu) ** 2, axis=-1, keepdims=True)
            return (x - mu) * jax.lax.rsqrt(var + EPS) * g + b

        def _message_passing(h, src, tgt, et, Wq, bq, Wk, bk, Wv, bv, Ee, Wo, bo, n_nodes):
            Q = (h @ Wq.T + bq).reshape(-1, H, DH)
            K = (h @ Wk.T + bk).reshape(-1, H, DH)
            V = (h @ Wv.T + bv).reshape(-1, H, DH)
            scores = jnp.einsum('ehd,egd->ehg', Q[src], K[tgt]) / jnp.sqrt(jnp.float32(DH))
            attn = jax.nn.softmax(scores, axis=-1)
            msg = jnp.einsum('ehg,egd->ehd', attn, V[tgt]).reshape(-1, HID)
            msg = msg + Ee[et]
            proj = msg @ Wo.T + bo
            return jax.ops.segment_sum(proj, src, num_segments=n_nodes)
        key = jax.random.key(seed)
        ks = jax.random.split(key, 16)

        def w(k, shape, s=0.05):
            return jax.random.normal(k, shape, jnp.float32) * s
        return {'x': jax.random.normal(ks[0], (N_NODES, HID), jnp.float32), 'edges': jax.random.randint(ks[1], (N_EDGES, 2), 0, N_NODES), 'edge_types': jax.random.randint(ks[2], (N_EDGES,), 0, 3), 'Win': w(ks[3], (HID, HID)), 'b_in': jnp.zeros((HID,), jnp.float32), 'Wq': w(ks[4], (N_LAYERS, HID, HID)), 'bq': jnp.zeros((N_LAYERS, HID), jnp.float32), 'Wk': w(ks[5], (N_LAYERS, HID, HID)), 'bk': jnp.zeros((N_LAYERS, HID), jnp.float32), 'Wv': w(ks[6], (N_LAYERS, HID, HID)), 'bv': jnp.zeros((N_LAYERS, HID), jnp.float32), 'Eemb': w(ks[7], (N_LAYERS, 3, HID)), 'Wo': w(ks[8], (N_LAYERS, HID, HID)), 'bo': jnp.zeros((N_LAYERS, HID), jnp.float32), 'ln_g': jnp.ones((N_LAYERS, HID), jnp.float32), 'ln_b': jnp.zeros((N_LAYERS, HID), jnp.float32), 'W1': w(ks[9], (HID, HID)), 'b1': jnp.zeros((HID,), jnp.float32), 'W2': w(ks[10], (HID, HID)), 'b2': jnp.zeros((HID,), jnp.float32)}
    _L0_gnn_all = _L0_gnn_setup()
    _L0_gnn_in = {k: v for k, v in _L0_gnn_all.items() if k in ('Win', 'b_in', 'Wq', 'bq', 'Wk', 'bk', 'Wv', 'bv', 'Eemb', 'Wo', 'bo', 'ln_g', 'ln_b', 'W1', 'b1', 'W2', 'b2')}
    del _L0_gnn_all

    def _L0_mix_setup():
        import jax, jax.numpy as jnp
        import numpy as np
        B, S, D = (8, 64, 256)
        H, KD = (8, 256)
        M = 256
        EPS_LN = 1e-06
        EPS_ATT = 1e-06

        def _layernorm(x, g, b):
            mu = jnp.mean(x, axis=-1, keepdims=True)
            var = jnp.mean(jnp.square(x - mu), axis=-1, keepdims=True)
            return (x - mu) * jax.lax.rsqrt(var + EPS_LN) * g + b

        def _phi(x, proj):
            u = jnp.einsum('bshd,md->bshm', x, proj)
            sq = 0.5 * jnp.sum(jnp.square(x), axis=-1, keepdims=True)
            return jnp.exp(u - sq) * (1.0 / np.sqrt(M)) + EPS_ATT
        key = jax.random.key(seed)
        ks = jax.random.split(key, 16)
        sd = lambda *s: 1.0 / np.sqrt(s[0])
        return {'inputs': jax.random.normal(ks[0], (B, S, D), dtype=jnp.float32), 'Wq': jax.random.normal(ks[1], (D, H, KD), jnp.float32) * sd(D), 'bq': jnp.zeros((H, KD), jnp.float32), 'Wk': jax.random.normal(ks[2], (D, H, KD), jnp.float32) * sd(D), 'bk': jnp.zeros((H, KD), jnp.float32), 'Wv': jax.random.normal(ks[3], (D, H, KD), jnp.float32) * sd(D), 'bv': jnp.zeros((H, KD), jnp.float32), 'Wo': jax.random.normal(ks[4], (H, KD, D), jnp.float32) * sd(H * KD), 'bo': jnp.zeros((D,), jnp.float32), 'proj': jax.random.normal(ks[5], (M, KD), jnp.float32), 'W1': jax.random.normal(ks[6], (D, D), jnp.float32) * sd(D), 'bias1': jnp.zeros((D,), jnp.float32), 'W2': jax.random.normal(ks[7], (D, D), jnp.float32) * sd(D), 'bias2': jnp.zeros((D,), jnp.float32), 'g1': jnp.ones((D,), jnp.float32), 'beta1': jnp.zeros((D,), jnp.float32), 'g2': jnp.ones((D,), jnp.float32), 'beta2': jnp.zeros((D,), jnp.float32)}
    _L0_mix_all = _L0_mix_setup()
    _L0_mix_in = {k: v for k, v in _L0_mix_all.items() if k in ('Wq', 'bq', 'Wk', 'bk', 'Wv', 'bv', 'Wo', 'bo', 'proj', 'W1', 'bias1', 'W2', 'bias2', 'g1', 'beta1', 'g2', 'beta2')}
    del _L0_mix_all

    def _L0_ffn_setup():
        import jax, jax.numpy as jnp
        import numpy as np
        B, S, D = (8, 128, 256)
        H = 4 * D
        CAPACITY = 0.5
        key = jax.random.key(seed)
        ks = jax.random.split(key, 6)
        x = jax.random.normal(ks[0], (B, S, D), dtype=jnp.float32)
        attention_mask = jnp.zeros((B, 1, 1, S), dtype=jnp.float32)
        wr = jax.random.normal(ks[1], (D, 1), dtype=jnp.float32) * 0.02
        br = jnp.zeros((1,), dtype=jnp.float32)
        w1 = jax.random.normal(ks[2], (D, H), dtype=jnp.float32) * 0.02
        b1 = jnp.zeros((H,), dtype=jnp.float32)
        w2 = jax.random.normal(ks[3], (H, D), dtype=jnp.float32) * 0.02
        b2 = jnp.zeros((D,), dtype=jnp.float32)
        return {'x': x, 'attention_mask': attention_mask, 'wr': wr, 'br': br, 'w1': w1, 'b1': b1, 'w2': w2, 'b2': b2}
    _L0_ffn_all = _L0_ffn_setup()
    _L0_ffn_in = {k: v for k, v in _L0_ffn_all.items() if k in ('attention_mask', 'wr', 'br', 'w1', 'b1', 'w2', 'b2')}
    del _L0_ffn_all
    return {'x': x, 'src': src, 'dst': dst, 'edge_type_3': edge_type_3, 'L0_gnn_Win': _L0_gnn_in['Win'], 'L0_gnn_b_in': _L0_gnn_in['b_in'], 'L0_gnn_Wq': _L0_gnn_in['Wq'], 'L0_gnn_bq': _L0_gnn_in['bq'], 'L0_gnn_Wk': _L0_gnn_in['Wk'], 'L0_gnn_bk': _L0_gnn_in['bk'], 'L0_gnn_Wv': _L0_gnn_in['Wv'], 'L0_gnn_bv': _L0_gnn_in['bv'], 'L0_gnn_Eemb': _L0_gnn_in['Eemb'], 'L0_gnn_Wo': _L0_gnn_in['Wo'], 'L0_gnn_bo': _L0_gnn_in['bo'], 'L0_gnn_ln_g': _L0_gnn_in['ln_g'], 'L0_gnn_ln_b': _L0_gnn_in['ln_b'], 'L0_gnn_W1': _L0_gnn_in['W1'], 'L0_gnn_b1': _L0_gnn_in['b1'], 'L0_gnn_W2': _L0_gnn_in['W2'], 'L0_gnn_b2': _L0_gnn_in['b2'], 'L0_mix_Wq': _L0_mix_in['Wq'], 'L0_mix_bq': _L0_mix_in['bq'], 'L0_mix_Wk': _L0_mix_in['Wk'], 'L0_mix_bk': _L0_mix_in['bk'], 'L0_mix_Wv': _L0_mix_in['Wv'], 'L0_mix_bv': _L0_mix_in['bv'], 'L0_mix_Wo': _L0_mix_in['Wo'], 'L0_mix_bo': _L0_mix_in['bo'], 'L0_mix_proj': _L0_mix_in['proj'], 'L0_mix_W1': _L0_mix_in['W1'], 'L0_mix_bias1': _L0_mix_in['bias1'], 'L0_mix_W2': _L0_mix_in['W2'], 'L0_mix_bias2': _L0_mix_in['bias2'], 'L0_mix_g1': _L0_mix_in['g1'], 'L0_mix_beta1': _L0_mix_in['beta1'], 'L0_mix_g2': _L0_mix_in['g2'], 'L0_mix_beta2': _L0_mix_in['beta2'], 'L0_ffn_attention_mask': _L0_ffn_in['attention_mask'], 'L0_ffn_wr': _L0_ffn_in['wr'], 'L0_ffn_br': _L0_ffn_in['br'], 'L0_ffn_w1': _L0_ffn_in['w1'], 'L0_ffn_b1': _L0_ffn_in['b1'], 'L0_ffn_w2': _L0_ffn_in['w2'], 'L0_ffn_b2': _L0_ffn_in['b2']}

def reference(x, src, dst, edge_type_3, L0_gnn_Win, L0_gnn_b_in, L0_gnn_Wq, L0_gnn_bq, L0_gnn_Wk, L0_gnn_bk, L0_gnn_Wv, L0_gnn_bv, L0_gnn_Eemb, L0_gnn_Wo, L0_gnn_bo, L0_gnn_ln_g, L0_gnn_ln_b, L0_gnn_W1, L0_gnn_b1, L0_gnn_W2, L0_gnn_b2, L0_mix_Wq, L0_mix_bq, L0_mix_Wk, L0_mix_bk, L0_mix_Wv, L0_mix_bv, L0_mix_Wo, L0_mix_bo, L0_mix_proj, L0_mix_W1, L0_mix_bias1, L0_mix_W2, L0_mix_bias2, L0_mix_g1, L0_mix_beta1, L0_mix_g2, L0_mix_beta2, L0_ffn_attention_mask, L0_ffn_wr, L0_ffn_br, L0_ffn_w1, L0_ffn_b1, L0_ffn_w2, L0_ffn_b2):
    import jax
    import jax.numpy as jnp

    def _L0_gnn_ref(x, edges, edge_types, Win, b_in, Wq, bq, Wk, bk, Wv, bv, Eemb, Wo, bo, ln_g, ln_b, W1, b1, W2, b2):
        import jax, jax.numpy as jnp
        import numpy as np
        H = 4
        DH = 64
        HID = 256
        EPS = 1e-05
        N_NODES = 625
        N_EDGES = 10000
        N_LAYERS = 3

        def _layer_norm(x, g, b):
            mu = jnp.mean(x, axis=-1, keepdims=True)
            var = jnp.mean((x - mu) ** 2, axis=-1, keepdims=True)
            return (x - mu) * jax.lax.rsqrt(var + EPS) * g + b

        def _message_passing(h, src, tgt, et, Wq, bq, Wk, bk, Wv, bv, Ee, Wo, bo, n_nodes):
            Q = (h @ Wq.T + bq).reshape(-1, H, DH)
            K = (h @ Wk.T + bk).reshape(-1, H, DH)
            V = (h @ Wv.T + bv).reshape(-1, H, DH)
            scores = jnp.einsum('ehd,egd->ehg', Q[src], K[tgt]) / jnp.sqrt(jnp.float32(DH))
            attn = jax.nn.softmax(scores, axis=-1)
            msg = jnp.einsum('ehg,egd->ehd', attn, V[tgt]).reshape(-1, HID)
            msg = msg + Ee[et]
            proj = msg @ Wo.T + bo
            return jax.ops.segment_sum(proj, src, num_segments=n_nodes)
        n_nodes = x.shape[0]
        src, tgt = (edges[:, 0], edges[:, 1])
        hidden = x @ Win.T + b_in
        for l in range(N_LAYERS):
            m = _message_passing(hidden, src, tgt, edge_types, Wq[l], bq[l], Wk[l], bk[l], Wv[l], bv[l], Eemb[l], Wo[l], bo[l], n_nodes)
            hidden = jax.nn.relu(_layer_norm(hidden + m, ln_g[l], ln_b[l]))
        adjustment = jax.nn.relu(hidden @ W1.T + b1) @ W2.T + b2
        return x + adjustment

    def _L0_mix_ref(inputs, Wq, bq, Wk, bk, Wv, bv, Wo, bo, proj, W1, bias1, W2, bias2, g1, beta1, g2, beta2):
        import jax, jax.numpy as jnp
        import numpy as np
        B, S, D = (8, 64, 256)
        H, KD = (8, 256)
        M = 256
        EPS_LN = 1e-06
        EPS_ATT = 1e-06

        def _layernorm(x, g, b):
            mu = jnp.mean(x, axis=-1, keepdims=True)
            var = jnp.mean(jnp.square(x - mu), axis=-1, keepdims=True)
            return (x - mu) * jax.lax.rsqrt(var + EPS_LN) * g + b

        def _phi(x, proj):
            u = jnp.einsum('bshd,md->bshm', x, proj)
            sq = 0.5 * jnp.sum(jnp.square(x), axis=-1, keepdims=True)
            return jnp.exp(u - sq) * (1.0 / np.sqrt(M)) + EPS_ATT
        scale = KD ** (-0.25)
        q = (jnp.einsum('bsd,dhk->bshk', inputs, Wq) + bq) * scale
        k = (jnp.einsum('bsd,dhk->bshk', inputs, Wk) + bk) * scale
        v = jnp.einsum('bsd,dhk->bshk', inputs, Wv) + bv
        phi_q = _phi(q, proj)
        phi_k = _phi(k, proj)
        kv = jnp.einsum('bshm,bshk->bhmk', phi_k, v)
        z = jnp.einsum('bshm,bhm->bsh', phi_q, phi_k.sum(axis=1))
        attn = jnp.einsum('bshm,bhmk->bshk', phi_q, kv) / z[..., None]
        attn_out = jnp.einsum('bshk,hkd->bsd', attn, Wo) + bo
        out1 = _layernorm(inputs + attn_out, g1, beta1)
        h = jax.nn.relu(out1 @ W1 + bias1)
        ffn_out = h @ W2 + bias2
        return _layernorm(out1 + ffn_out, g2, beta2)

    def _L0_ffn_ref(x, attention_mask, wr, br, w1, b1, w2, b2):
        import jax, jax.numpy as jnp
        import numpy as np
        B, S, D = (8, 128, 256)
        H = 4 * D
        CAPACITY = 0.5
        b, s, d = x.shape
        weights = (jnp.einsum('bsd,do->bso', x, wr) + br)[..., 0]
        k = max(1, int(CAPACITY * s))
        kk = k - 1 if k > 1 else 1
        _, idx = jax.lax.top_k(weights, k)
        sel_idx = idx[:, :kk]
        sel = jnp.take_along_axis(x, sel_idx[:, :, None], axis=1)
        h = jax.nn.gelu(jnp.einsum('bkd,dh->bkh', sel, w1) + b1)
        y = jnp.einsum('bkh,hd->bkd', h, w2) + b2
        w_sel = jnp.take_along_axis(weights, sel_idx, axis=1)
        y = y * w_sel[..., None]
        batch_idx = jnp.arange(b)[:, None]
        processed = jnp.zeros_like(x).at[batch_idx, sel_idx].set(y)
        return processed + x
    edge_index_t = jnp.stack([src, dst], axis=1)
    xn = _layernorm(x, axis=-1)
    x = x + _L0_gnn_ref(xn, edge_index_t, edge_type_3, L0_gnn_Win, L0_gnn_b_in, L0_gnn_Wq, L0_gnn_bq, L0_gnn_Wk, L0_gnn_bk, L0_gnn_Wv, L0_gnn_bv, L0_gnn_Eemb, L0_gnn_Wo, L0_gnn_bo, L0_gnn_ln_g, L0_gnn_ln_b, L0_gnn_W1, L0_gnn_b1, L0_gnn_W2, L0_gnn_b2) + _L0_mix_ref(xn[None], L0_mix_Wq, L0_mix_bq, L0_mix_Wk, L0_mix_bk, L0_mix_Wv, L0_mix_bv, L0_mix_Wo, L0_mix_bo, L0_mix_proj, L0_mix_W1, L0_mix_bias1, L0_mix_W2, L0_mix_bias2, L0_mix_g1, L0_mix_beta1, L0_mix_g2, L0_mix_beta2)[0]
    x = x + _L0_ffn_ref(_layernorm(x, axis=-1)[None], L0_ffn_attention_mask, L0_ffn_wr, L0_ffn_br, L0_ffn_w1, L0_ffn_b1, L0_ffn_w2, L0_ffn_b2)[0]
    return x

_drawn_inputs = setup_inputs


def setup_inputs(seed=0):
    import zlib

    import numpy as np

    out = dict(_drawn_inputs(seed))
    spreads = {'L0_gnn_b_in': (0.0, 0.305),
     'L0_gnn_bq': (0.0, 0.8),
     'L0_gnn_bk': (0.0, 0.8),
     'L0_gnn_bv': (0.0, 0.1),
     'L0_gnn_bo': (0.0, 0.1),
     'L0_gnn_ln_g': (1.0, 0.2),
     'L0_gnn_ln_b': (0.0, 0.474),
     'L0_gnn_b1': (0.0, 0.464),
     'L0_gnn_b2': (0.0, 0.1),
     'L0_mix_bq': (0.0, 0.345),
     'L0_mix_bk': (0.0, 0.357),
     'L0_mix_bv': (0.0, 0.1),
     'L0_mix_bo': (0.0, 0.1),
     'L0_mix_bias1': (0.0, 0.394),
     'L0_mix_bias2': (0.0, 0.285),
     'L0_mix_g1': (1.0, 0.2),
     'L0_mix_beta1': (0.0, 0.1),
     'L0_mix_g2': (1.0, 0.2),
     'L0_mix_beta2': (0.0, 0.1),
     'L0_ffn_b1': (0.0, 0.8),
     'L0_ffn_b2': (0.0, 0.8)}
    factors = {'L0_gnn_Win': 4.808, 'L0_ffn_wr': 6.864, 'L0_ffn_w1': 7.699, 'L0_ffn_w2': 7.21}
    for name, (base, spread) in spreads.items():
        noise = np.random.default_rng([zlib.crc32(name.encode()), seed]).standard_normal(out[name].shape)
        drawn = base * np.exp(spread * noise) if base else spread * noise
        out[name] = jnp.asarray(drawn.astype(out[name].dtype))
    for name, factor in factors.items():
        out[name] = (out[name] * factor).astype(out[name].dtype)
    return out
```

```python
from contextlib import ExitStack

import concourse.bass as bass
from concourse import mybir

F32 = mybir.dt.float32
I32 = mybir.dt.int32
BF16 = mybir.dt.bfloat16
ALU = mybir.AluOpType
ACT = mybir.ActivationFunctionType
AX = mybir.AxisListType

N_NODES = 3125
D = 256
P = 128
TN = 125
NT = N_NODES // TN
KC = D // P
N_EDGES = 50000
EC = 391
N_PADDED = P * EC
ET_MAX = (N_EDGES + NT * (P - 1)) // P
GRP = 4
ETILES = -(-ET_MAX // (2 * GRP)) * 2 * GRP
TRASH = ETILES * P
TCOLS = ETILES + -(-EC // P)
NODE_BITS = 12
EMPTY = 127 << NODE_BITS
N_ET = 3
LAYERS = 3
GH, GD = 4, 64
MH = 8
HM = MH * D
PARTS = 3
AUG = PARTS * (MH + 1)
MSCALE = 0.25
FF = 4 * D
TOPK = N_NODES // 2 - 1
CNT_T = 23
CNT_G = EC // CNT_T


class Steps:

    def __init__(self, eng, sem, base=0):
        self.eng, self.sem, self.base, self.n = eng, sem, base, 0

    def done(self, ins):
        self.n += 1
        return ins.then_inc(self.sem, 1)

    def wait(self):
        self.eng.wait_ge(self.sem, self.base + self.n)

    def link(self, ins):
        self.done(ins)
        self.wait()


def paired(eng, n, step):
    with eng.Fori(0, n // 2) as i:
        step(2 * i, 0)
        step(2 * i + 1, 1)
    if n % 2:
        step(n - 1, 0)


def hold(eng, go, sem, value):
    eng.wait_ge(sem, value)
    eng.sem_inc(go, 1)


def row(ap, n):
    return ap.rearrange("(o d) -> o d", o=1).to_broadcast([n, ap.shape[0]])


def flipped(eng, n, first, step):
    with eng.Fori(0, n // 2) as i:
        step(2 * i, first)
        step(2 * i + 1, 1 - first)
    step(n - 1, first)


class Norm:

    def __init__(self, k, name):
        self.stats = k.sb(name + "_stats", [TN, NT, 6])
        self.mean = k.sb(name + "_mean", [TN, NT])
        self.rstd = k.sb(name + "_rstd", [TN, NT])
        self.var = k.sb(name + "_var", [TN, NT])
        self.tmp = k.sb(name + "_tmp", [TN, NT])
        self.bits = k.sb(name + "_bits", [TN, NT], I32)
        self.s_done = k.sem(name + "_done")

    def moments(self, v, c, x, eps):
        with v.Fori(0, NT) as t:
            v.bn_stats(self.stats[:, bass.ds(t, 1), :], x[:, bass.ds(t, 1), 0:D]).then_inc(c.sem, 1)
        c.n += NT
        c.wait()
        even, odd = self.stats[:, :, 1], self.stats[:, :, 4]
        var, tmp, y = self.var[:, :], self.tmp[:, :], self.rstd[:, :]
        c.done(v.tensor_tensor(self.mean[:, :], even, odd, ALU.add))
        c.done(v.tensor_tensor(tmp, even, odd, ALU.subtract))
        c.link(v.tensor_tensor(var, self.stats[:, :, 2], self.stats[:, :, 5], ALU.add))
        c.done(v.tensor_scalar(self.mean[:, :], self.mean[:, :], 0.5, None, ALU.mult))
        c.link(v.scalar_tensor_tensor(out=tmp, in0=tmp, scalar=D / 4.0, in1=tmp, op0=ALU.mult, op1=ALU.mult))
        c.link(v.tensor_tensor(var, var, tmp, ALU.add))
        c.link(v.tensor_scalar(var, var, 1.0 / D, eps, ALU.mult, ALU.add))
        c.link(v.tensor_scalar(self.bits[:, :], var.bitcast(I32), 1, None, ALU.logical_shift_right))
        c.link(v.tensor_scalar(y.bitcast(I32), self.bits[:, :], -1.0, float(0x5F3759DF), ALU.mult, ALU.add))
        c.link(v.tensor_scalar(var, var, -0.5, None, ALU.mult))
        for _ in range(4):
            c.wait()
            c.link(v.tensor_tensor(tmp, y, y, ALU.mult))
            c.link(v.tensor_tensor(tmp, tmp, var, ALU.mult))
            c.done(v.scalar_tensor_tensor(out=y, in0=tmp, scalar=1.5, in1=y, op0=ALU.add, op1=ALU.mult))
        hold(v, self.s_done, c.sem, c.base + c.n)

    def apply(self, v, out, x, t):
        return v.tensor_scalar(out, x, self.mean[:, bass.ds(t, 1)], self.rstd[:, bass.ds(t, 1)],
                               ALU.subtract, ALU.mult)


class Kit:

    def __init__(self, nc, ctx):
        self.nc, self.ctx = nc, ctx

    def sb(self, name, shape, dt=F32):
        return self.ctx.enter_context(self.nc.sbuf_tensor(name, shape, dt))

    def ps(self, name, shape=(P, 512), dt=F32):
        return self.ctx.enter_context(self.nc.psum_tensor(name, list(shape), dt))

    def sem(self, name):
        return self.ctx.enter_context(self.nc.semaphore(name))


def prepare(nc, a, g, scr):
    with ExitStack() as ctx:
        k = Kit(nc, ctx)
        src_i = k.sb("src_i", [P, EC], I32)
        dst_i = k.sb("dst_i", [P, EC], I32)
        et_i = k.sb("et_i", [P, EC], I32)
        src_f = k.sb("src_f", [P, EC])
        dst_f = k.sb("dst_f", [P, EC])
        et_f = k.sb("et_f", [P, EC])
        ge = k.sb("ge", [P, NT + 1, EC], BF16)
        boh = k.sb("boh", [P, NT, EC], BF16)
        eoh = k.sb("eoh", [P, N_ET, EC], BF16)
        run = k.sb("run", [P, NT * EC])
        runb = run[:, :].rearrange("p (b t) -> p b t", b=NT)
        local = k.sb("local", [P, EC])
        iota_e = k.sb("iota_e", [P, TCOLS])
        tri = k.sb("tri", [P, P])
        ones = k.sb("ones", [P, P])
        last = k.sb("last", [P, NT + 1])
        cnt = k.sb("cnt", [P, NT])
        cnt_i = k.sb("cnt_i", [P, NT], I32)
        tiles = k.sb("tiles", [P, NT])
        tend = k.sb("tend", [P, NT])
        off = k.sb("off", [P, NT])
        pos, pos_i, lo_i, hi_i = et_f, src_i, dst_i, et_i
        fill = k.sb("fill", [P, TCOLS], I32)
        bucket = k.sb("bucket", [1, ETILES])
        be = k.sb("be", [P, NT, N_ET, CNT_T], BF16)
        roh = k.sb("roh", [P, CNT_T, TN], BF16)
        counts = k.sb("counts", [NT * N_ET, TN])
        norm_x = Norm(k, "nx")
        stage = k.sb("stage", [TN, 2, D])
        p_tr = [k.ps(f"p_tr{i}") for i in range(2)]
        p_scan = k.ps("p_scan")
        p_cnt = k.ps("p_cnt")

        s_x = k.sem("pr_x")
        s_const = k.sem("pr_const")
        s_edges = k.sem("pr_edges")
        s_dve = k.sem("pr_dve")
        s_xn = k.sem("pr_xn")
        s_tr = k.sem("pr_tr")
        s_xnt = k.sem("pr_xnt")
        s_c = k.sem("pr_c")
        s_off = k.sem("pr_off")
        s_oh = k.sem("pr_oh")
        s_ohu = k.sem("pr_ohu")
        s_cout = k.sem("pr_cout")
        s_fill = k.sem("pr_fill")
        s_out = k.sem("pr_out")
        block = ctx.enter_context(nc.Block())

        @block.sync
        def _(sp):
            sp.dma_start(g["xacc"][:, :, :], a["x"].rearrange("(t p) d -> p t d", p=TN)).then_inc(s_x, 16)
            sp.dma_start(src_i[:, :], a["src"]).then_inc(s_edges, 16)
            sp.dma_start(dst_i[:, :], a["dst"]).then_inc(s_edges, 16)
            sp.dma_start(et_i[:, :], a["et"]).then_inc(s_edges, 16)
            sp.dma_start(g["ident"][:, :], a["c_ident"]).then_inc(s_const, 16)
            sp.dma_start(tri[:, :], a["c_tri"]).then_inc(s_const, 16)
            sp.dma_start(g["iota_n"][:, :], a["c_iota_n"]).then_inc(s_const, 16)
            sp.dma_start(iota_e[:, :], a["c_iota_e"]).then_inc(s_const, 16)
            sp.wait_ge(s_fill, 1)
            sp.dma_start(scr["table"].rearrange("(p c) o -> p (c o)", p=P), fill[:, :]).then_inc(s_out, 16)
            sp.wait_ge(s_cout, 1)
            sp.dma_start(scr["counts"], counts[:, :]).then_inc(s_out, 16)
            sp.wait_ge(s_out, 32)

        @block.scalar
        def _(act):
            act.sem_inc(s_xnt, 2)

            def step(t, slot):
                act.wait_ge(s_tr, t + 1)
                act.copy(g["xn_t"][:, :, bass.ds(t * TN, TN)],
                         p_tr[slot][:, 0:KC * TN].rearrange("p (c n) -> p c n", c=KC)).then_inc(s_xnt, 1)
            paired(act, NT, step)

        @block.tensor
        def _(pe):
            pe.wait_ge(s_const, 64)

            def step(t, slot):
                pe.wait_ge(s_xn, t + 1)
                pe.wait_ge(s_xnt, t + 1)
                for c in range(KC):
                    ins = pe.transpose(p_tr[slot][:, c * TN:(c + 1) * TN],
                                       stage[:, slot, c * P:(c + 1) * P], g["ident"][0:TN, 0:TN])
                ins.then_inc(s_tr, 1)
            paired(pe, NT, step)
            pe.wait_ge(s_c, 1)
            pe.matmul(p_scan[:, 0:NT], tri[:, :], cnt[:, :], start=True, stop=True)
            pe.matmul(p_scan[:, NT:2 * NT], ones[:, :], cnt[:, :], start=True, stop=True).then_inc(s_off, 1)
            pe.sem_inc(s_ohu, 1)
            with pe.Fori(0, CNT_G) as i:
                pe.wait_ge(s_oh, i + 1)
                for j in range(CNT_T):
                    ins = pe.matmul(p_cnt[0:NT * N_ET, 0:TN], be[:, :, :, j].rearrange("p b e -> p (b e)"),
                                    roh[:, j, :], start=False, stop=False, skip_group_check=True)
                ins.then_inc(s_ohu, 1)

        @block.gpsimd
        def _(pool):
            pool.memset(fill[:, :], EMPTY).then_inc(s_fill, 1)
            pool.wait_ge(s_xn, NT)
            pool.tensor_tensor(g["xacc"][:, :, :], g["xacc"][:, :, :], g["xn"][:, :, 0:D], ALU.add)

        @block.vector
        def _(v):
            c = Steps(v, s_dve)
            v.memset(ones[:, :], 1.0)
            v.memset(last[:, 0:1], 0.0)
            v.memset(g["xn"][:, :, D:D + 1], 1.0)
            v.wait_ge(s_x, 16)
            norm_x.moments(v, c, g["xacc"], 1e-5)

            def norm(t, slot):
                v.wait_ge(s_xnt, t + 1)
                norm_x.apply(v, g["xn"][:, bass.ds(t, 1), 0:D], g["xacc"][:, bass.ds(t, 1), :], t)
                norm_x.apply(v, stage[:, slot, :], g["xacc"][:, bass.ds(t, 1), :], t).then_inc(s_xn, 1)
            paired(v, NT, norm)
            v.wait_ge(s_edges, 48)
            v.wait_ge(s_const, 64)
            v.tensor_copy(g["ident_b"][:, :], g["ident"][:, :])
            c.done(v.tensor_copy(src_f[:, :], src_i[:, :]))
            c.done(v.tensor_copy(dst_f[:, :], dst_i[:, :]))
            c.link(v.tensor_copy(et_f[:, :], et_i[:, :]))
            for b in range(NT + 1):
                c.done(v.tensor_scalar(ge[:, b, :], src_f[:, :], float(TN * b), None, ALU.is_ge))
            for e in range(N_ET):
                c.done(v.tensor_scalar(eoh[:, e, :], et_f[:, :], float(e), None, ALU.is_equal))
            c.wait()
            c.done(v.tensor_tensor(boh[:, :, :], ge[:, 0:NT, :], ge[:, 1:NT + 1, :], ALU.subtract))
            c.link(v.tensor_reduce(local[:, :], ge[:, 1:NT, :].rearrange("p b t -> p t b"), AX.X, ALU.add))
            c.done(v.scalar_tensor_tensor(out=local[:, :], in0=local[:, :], scalar=-float(TN), in1=src_f[:, :],
                                          op0=ALU.mult, op1=ALU.add))
            flat = boh[:, :, :].rearrange("p b t -> p (b t)")
            c.link(v.tensor_tensor_scan(run[:, :], flat, flat, 0.0, ALU.add, ALU.max))
            c.link(v.tensor_copy(last[:, 1:NT + 1], runb[:, :, EC - 1]))
            c.link(v.tensor_tensor(cnt[:, :], last[:, 1:NT + 1], last[:, 0:NT], ALU.subtract))
            v.nop().then_inc(s_c, 1)
            v.wait_ge(s_off, 1)
            c.link(v.tensor_scalar(cnt_i[:, :], p_scan[:, NT:2 * NT], float(P - 1), None, ALU.add))
            c.link(v.tensor_scalar(cnt_i[:, :], cnt_i[:, :], 7, None, ALU.logical_shift_right))
            c.link(v.tensor_copy(tiles[:, :], cnt_i[:, :]))
            c.link(v.tensor_tensor_scan(tend[:, :], tiles[:, :], tiles[:, :], 0.0, ALU.add, ALU.max))
            c.link(v.tensor_tensor(off[:, :], tend[:, :], tiles[:, :], ALU.subtract))
            c.link(v.tensor_scalar(off[:, :], off[:, :], float(P), -1.0, ALU.mult, ALU.add))
            c.link(v.tensor_tensor(off[:, :], off[:, :], p_scan[:, 0:NT], ALU.add))
            c.link(v.tensor_tensor(off[:, :], off[:, :], last[:, 0:NT], ALU.subtract))
            c.link(v.tensor_tensor(runb, runb, off[:, :].rearrange("p (b o) -> p b o", o=1).to_broadcast([P, NT, EC]), ALU.add))
            c.link(v.tensor_tensor(runb, runb, boh[:, :, :], ALU.mult))
            c.link(v.tensor_reduce(pos[:, :], runb.rearrange("p b t -> p t b"), AX.X, ALU.add))
            c.link(v.scalar_tensor_tensor(out=src_f[:, :], in0=iota_e[:, 0:EC], scalar=float(TRASH), in1=ge[:, NT, :],
                                          op0=ALU.add, op1=ALU.mult))
            c.link(v.tensor_tensor(pos_i[:, :], pos[:, :], src_f[:, :], ALU.add))
            c.done(v.tensor_scalar(lo_i[:, :], pos_i[:, :], P - 1, None, ALU.bitwise_and))
            c.link(v.tensor_scalar(hi_i[:, :], pos_i[:, :], 7, None, ALU.logical_shift_right))
            c.done(v.scalar_tensor_tensor(out=g["scat_idx"][:, :], in0=lo_i[:, :], scalar=float(TCOLS), in1=hi_i[:, :],
                                          op0=ALU.mult, op1=ALU.add))
            c.done(v.scalar_tensor_tensor(out=g["record"][:, :], in0=local[:, :], scalar=float(1 << NODE_BITS),
                                          in1=dst_f[:, :], op0=ALU.mult, op1=ALU.add))
            cmp = run[0:1, 0:ETILES * NT // 2].rearrange("p (j b) -> p j b", b=NT)
            half = ETILES // 2
            for h in range(2):
                c.link(v.tensor_tensor(cmp, iota_e[0:1, h * half:(h + 1) * half].rearrange("p (j o) -> p j o", o=1).to_broadcast([1, half, NT]),
                                       tend[0:1, :].rearrange("p (o b) -> p o b", o=1).to_broadcast([1, half, NT]), ALU.is_ge))
                c.link(v.tensor_reduce(bucket[0:1, h * half:(h + 1) * half], cmp, AX.X, ALU.add))
            c.link(v.tensor_scalar(bucket[:, :], bucket[:, :], float(NT - 1), None, ALU.min))
            b4 = bucket[:, :].rearrange("p (g j) -> p g j", j=GRP)
            for j in range(1, GRP):
                c.link(v.scalar_tensor_tensor(out=b4[:, :, 0] if j < GRP - 1 else g["tab"][:, :], in0=b4[:, :, j],
                                              scalar=float(32 ** j), in1=b4[:, :, 0], op0=ALU.mult, op1=ALU.add))
            c.link(v.memset(p_cnt[:, :], 0.0))
            with v.Fori(0, CNT_G) as i:
                v.wait_ge(s_ohu, i + 1)
                cols = bass.ds(i * CNT_T, CNT_T)
                v.tensor_tensor(be[:, :, :, :],
                                boh[:, :, cols].rearrange("p (b o) t -> p b o t", o=1).to_broadcast([P, NT, N_ET, CNT_T]),
                                eoh[:, :, cols].rearrange("p (o e) t -> p o e t", o=1).to_broadcast([P, NT, N_ET, CNT_T]),
                                ALU.mult)
                v.tensor_tensor(roh[:, :, :],
                                local[:, cols].rearrange("p (t o) -> p t o", o=1).to_broadcast([P, CNT_T, TN]),
                                g["iota_n"][:, :].rearrange("p (o n) -> p o n", o=1).to_broadcast([P, CNT_T, TN]),
                                ALU.is_equal).then_inc(s_oh, 1)
            v.wait_ge(s_ohu, CNT_G + 1)
            v.tensor_copy(counts[:, :], p_cnt[0:NT * N_ET, 0:TN]).then_inc(s_cout, 1)


def mix(nc, a, g, scr):
    with ExitStack() as ctx:
        k = Kit(nc, ctx)
        NB = 2 * MH
        NW = HM // (2 * D)
        WCOLS = 4 * D + KC
        wring = k.sb("wring", [P, 2, WCOLS])
        pb = k.sb("pb", [P, KC, D + NB])
        bsq = k.sb("bsq", [P, KC, NB])
        ones = k.sb("mones", [P, P])
        eones = k.sb("eones", [P, P])
        wp = k.sb("wp", [P, 2, KC, HM])
        w2 = k.sb("w2", [P, KC, NB])
        crow = k.sb("crow", [NB, D])
        cpart = k.sb("cpart", [NB, PARTS, D], BF16)
        augw = k.sb("augw", [AUG, 2, HM], BF16)
        augx = k.sb("augx", [AUG, 2, N_NODES], BF16)
        c0 = k.sb("c0", [TN, NB])
        sq = k.sb("sq", [TN, NT * NB])
        sqp = k.sb("sqp", [TN, NT * NB])
        s54 = k.sb("s54", [TN, NT, 2 * AUG], BF16)
        s54s = k.sb("s54s", [TN, 2, 2 * AUG], BF16)
        junk = k.sb("junk", [TN, 2, 2, D])
        xs = k.sb("xs", [P, 2, KC, TN])
        augs = k.sb("augs", [AUG, 2, TN], BF16)
        ek = k.sb("ek", [TN, 2, 2 * D])
        csum = k.sb("csum", [P, D + 1])
        gs = k.sb("gs", [P, 4, D + 1])
        gt = k.sb("gt", [P, KC, D])
        kst = k.sb("kst", [1, D])
        wvo = k.sb("wvo", [P, KC, D])
        bvo = k.sb("bvo", [1, D])
        kvs = k.sb("kvs", [P, MH, KC, D + 1])
        eq = k.sb("eq", [P, 4, 4, TN])
        rz = k.sb("rz", [TN, MH])
        acc = k.sb("acc", [TN, 2, D])
        bo = k.sb("bo", [TN, D])
        sidx = k.sb("sidx", [P, 2, CNT_G], I32)
        srec = k.sb("srec", [P, 2, CNT_G], I32)
        p_u = [k.ps(f"p_u{i}") for i in range(2)]
        p_g = [k.ps(f"p_g{i}") for i in range(4)]
        p_s = [k.ps(f"p_s{i}") for i in range(2)]

        s_const = k.sem("mx_const")
        s_ones = k.sem("mx_ones")
        s_bsq = k.sem("mx_bsq")
        s_w = [k.sem(f"mx_w{i}") for i in range(2)]
        s_dve = k.sem("mx_dve")
        s_crow = k.sem("mx_crow")
        s_cpart = k.sem("mx_cpart")
        s_cdram = k.sem("mx_cdram")
        s_caug = k.sem("mx_caug")
        s_fold = k.sem("mx_fold")
        s_folded = k.sem("mx_folded")
        s_cs = k.sem("mx_cs")
        s_zero = k.sem("mx_zero")
        s_xs = k.sem("mx_xs")
        s_cross = k.sem("mx_cross")
        s_q = k.sem("mx_q")
        s_qfree = k.sem("mx_qfree")
        s_s54 = k.sem("mx_s54")
        s_st = k.sem("mx_st")
        s_aug = k.sem("mx_aug")
        s_u = k.sem("mx_u")
        s_e = k.sem("mx_e")
        s_efree = k.sem("mx_efree")
        s_gs = k.sem("mx_gs")
        s_vo = k.sem("mx_vo")
        s_voc = k.sem("mx_voc")
        s_kdiag = k.sem("mx_kdiag")
        s_gt = k.sem("mx_gt")
        s_gtc = k.sem("mx_gtc")
        s_kv = k.sem("mx_kv")
        s_kvs = k.sem("mx_kvs")
        s_uq = k.sem("mx_uq")
        s_eq = k.sem("mx_eq")
        s_eps = k.sem("mx_eps")
        s_n = k.sem("mx_n")
        s_rz = k.sem("mx_rz")
        s_nfree = k.sem("mx_nfree")
        s_y = k.sem("mx_y")
        s_step = k.sem("mx_step")
        s_idx = k.sem("mx_idx")
        s_scat = [k.sem(f"mx_scat{i}") for i in range(2)]
        block = ctx.enter_context(nc.Block())
        SQ0 = NT
        KEY0 = NT * (1 + 2 * NW)

        @block.sync
        def _(sp):
            sp.dma_start(pb[:, :, :], a["m_pb"]).then_inc(s_const, 16)
            sp.dma_start(augw[:, :, :], a["m_sel"]).then_inc(s_const, 16)
            sp.dma_start(bo[:, :], row(a["m_bo"], TN)).then_inc(s_const, 16)

            def load(n, slot):
                sp.dma_start(wring[:, slot:slot + 1, :], a["m_w"][:, bass.ds(n, 1), :]).then_inc(s_w[slot], 16)
            for n in range(2):
                load(n, n)
            sp.wait_ge(s_cpart, 1)
            sp.dma_start(scr["cpart"].rearrange("h (r m) -> h r m", r=PARTS), cpart[:, :, :]).then_inc(s_cdram, 16)
            sp.wait_ge(s_cdram, 16)
            sp.wait_ge(s_const, 48)
            for i in range(2):
                sp.dma_start(augw[PARTS * MH:AUG, i, :].rearrange("r (h m) -> r h m", h=MH),
                             scr["cpart"][i * MH:(i + 1) * MH, :].rearrange("h (r m) -> r h m", r=PARTS)).then_inc(s_caug, 16)
            for n in range(2, MH + 2):
                sp.wait_ge(s_fold, n - 1)
                load(n, n % 2)
            for w in range(2, 2 * NW + 2):
                sp.wait_ge(s_q, 2 + NT * (w - 1))
                load(MH + w, w % 2)
            for h in range(2, MH):
                sp.wait_ge(s_vo, h - 1)
                load(MH + 2 * NW + h, h % 2)

        @block.gpsimd
        def _(pool):
            pool.memset(ones[:, :], 1.0).then_inc(s_ones, 1)
            pool.memset(eones[:, :], 16e-6).then_inc(s_ones, 1)
            pool.sem_inc(s_y, 2)

            def scatter(n, slot):
                if not isinstance(n, int) or n >= 2:
                    pool.wait_ge(s_scat[slot], (n - slot) * 8 * (EC // CNT_T))
                cols = bass.ds(n * CNT_G, CNT_G)
                pool.tensor_copy(sidx[:, slot, :], g["scat_idx"][:, cols]).then_inc(s_idx, 1)
                pool.tensor_copy(srec[:, slot, :], g["record"][:, cols]).then_inc(s_idx, 1)
                hold(pool, s_step, s_idx, 2 * n + 2)
                for j in range(CNT_G):
                    pool.indirect_dma_start(out=scr["table"], out_offset=bass.IndirectOffsetOnAxis(ap=sidx[:, slot, j:j + 1], axis=0),
                                            in_=srec[:, slot, j:j + 1], in_offset=None).then_inc(s_scat[slot], 16)
            scatter(0, 0)
            scatter(1, 1)
            with pool.Fori(1, CNT_T // 2) as i:
                scatter(2 * i, 0)
                scatter(2 * i + 1, 1)
            scatter(CNT_T - 1, 0)
            pool.wait_ge(s_const, 48)
            pool.wait_ge(s_kvs, MH + 1)

            def output(t, slot):
                pool.wait_ge(s_nfree, 8 * t + 10)
                pool.tensor_tensor(acc[:, slot, :], acc[:, slot, :], bo[:, :], ALU.add).then_inc(s_idx, 1)
                hold(pool, s_step, s_idx, 2 * CNT_T + t + 1)
                pool.tensor_tensor(g["xn"][:, bass.ds(t, 1), 0:D], g["xn"][:, bass.ds(t, 1), 0:D],
                                   acc[:, slot:slot + 1, :], ALU.add).then_inc(s_y, 1)
            paired(pool, NT, output)
            pool.wait_ge(s_scat[0], 16 * CNT_G * (CNT_T - CNT_T // 2))
            pool.wait_ge(s_scat[1], 16 * CNT_G * (CNT_T // 2))

        @block.tensor
        def _(pe):
            pe.wait_ge(s_const, 48)
            pe.wait_ge(s_ones, 2)
            for c in range(KC):
                pe.matmul(p_s[0][0:NB, 0:D], pb[:, c, D:D + NB], pb[:, c, 0:D], start=c == 0, stop=c == 1)
            pe.wait_ge(s_bsq, 1)
            for c in range(KC):
                ins = pe.matmul(p_s[1][0:TN, 0:NB], ones[:, 0:TN], bsq[:, c, :], start=c == 0, stop=c == 1)
            ins.then_inc(s_crow, 1)

            def fold(h, slot):
                pe.wait_ge(s_w[slot], 8 * (h - slot) + 16)
                pe.wait_ge(s_folded, 2 * h + 2)
                w = wring[:, slot, 0:4 * D].rearrange("p (i c d) -> p i c d", i=2, c=KC)
                for i in range(2):
                    for dc in range(KC):
                        for c in range(KC):
                            ins = pe.matmul(p_g[2 * i + dc][:, 0:D + NB], w[:, i, c, dc * P:(dc + 1) * P], pb[:, c, :],
                                            start=c == 0, stop=c == KC - 1)
                ins.then_inc(s_fold, 1)
            paired(pe, MH, fold)

            pe.wait_ge(s_cs, 1)
            with pe.Fori(0, NT) as t:
                pe.matmul(p_s[0][:, 0:D + 1], eones[0:TN, :], g["xn"][:, bass.ds(t, 1), :], start=False, stop=False,
                          skip_group_check=True).then_inc(s_cs, 1)

            pe.wait_ge(s_folded, 2 * MH + 2)
            pe.wait_ge(s_zero, 1)
            pe.sem_inc(s_cross, 2)

            def cross(t, slot):
                pe.wait_ge(s_xs, t + 1)
                for c in range(KC):
                    ins = pe.matmul(p_s[1][0:TN, bass.ds(t * NB, NB)], xs[:, slot, c, :], w2[:, c, :],
                                    start=False, stop=False, skip_group_check=True)
                ins.then_inc(s_cross, 1)
            paired(pe, NT, cross)
            pe.sem_inc(s_q, 2)

            with pe.Fori(0, NW) as wp2:
                for wslot in range(2):
                    w = wp2 * 2 + wslot

                    def square(t, slot):
                        n = w * NT + t
                        pe.wait_ge(s_w[wslot], 16 * wp2 + (8 * MH + 16))
                        pe.wait_ge(s_xs, n + (SQ0 + 1))
                        pe.wait_ge(s_qfree, n + 1)
                        for c in range(KC):
                            ins = pe.matmul(p_u[slot][0:TN, :], xs[:, slot, c, :],
                                            wring[:, wslot, c * 2 * D:(c + 1) * 2 * D], start=c == 0, stop=c == KC - 1)
                        ins.then_inc(s_q, 1)
                    flipped(pe, NT, 1 - wslot, square)

            pe.wait_ge(s_qfree, 2 + 2 * NW * NT)
            pe.sem_inc(s_st, 2)

            def spread(t, slot):
                pe.wait_ge(s_s54, t + 1)
                pe.wait_ge(s_aug, t + 1)
                for i in range(2):
                    ins = pe.transpose(p_u[slot][:, :].bitcast(BF16)[0:AUG, i * P:i * P + TN],
                                       s54s[:, slot, i * AUG:(i + 1) * AUG], g["ident_b"][0:TN, 0:TN])
                ins.then_inc(s_st, 1)
            paired(pe, NT, spread)
            pe.wait_ge(s_aug, NT + 2)
            pe.wait_ge(s_caug, 32)
            pe.sem_inc(s_u, 2)
            pe.sem_inc(s_efree, 2)
            pe.sem_inc(s_gt, 1)

            with pe.Fori(0, NW // 2) as hq:
                for odd in range(2):
                    hp = hq * 2 + odd
                    first = (1 + odd) % 2
                    pe.wait_ge(s_zero, hp + 1)

                    def keys(t, slot):
                        n = hp * NT + t
                        pe.wait_ge(s_xs, n + (KEY0 + 1))
                        pe.wait_ge(s_efree, n + 1)
                        cols = bass.ds(hp * 2 * D, 2 * D)
                        for c in range(KC):
                            pe.matmul(p_u[slot][0:TN, :], xs[:, slot, c, :], wp[:, 1, c, cols], start=c == 0, stop=False)
                        pe.matmul(p_u[slot][0:TN, :], augs[:, slot, :], augw[:, 1, cols], start=False, stop=True).then_inc(s_u, 1)

                    def accumulate(t, slot):
                        pe.wait_ge(s_e, hp * NT + t + 1)
                        for m in range(4):
                            ins = pe.matmul(p_g[m][:, 0:D + 1], ek[:, slot, m * P:(m + 1) * P],
                                            g["xn"][:, bass.ds(t, 1), :], start=False, stop=False, skip_group_check=True)
                        ins.then_inc(s_efree, 1)

                    keys(0, first)
                    with pe.Fori(0, NT // 2) as i:
                        keys(2 * i + 1, 1 - first)
                        accumulate(2 * i, first)
                        keys(2 * i + 2, first)
                        accumulate(2 * i + 1, 1 - first)
                    accumulate(NT - 1, first)
                    for j in range(2):
                        h = hp * 2 + j
                        w = wring[:, j, 0:4 * D].rearrange("p (i c d) -> p i c d", i=2, c=KC)
                        pe.wait_ge(s_w[j], 16 * hp + 8 * (MH + 2 * NW) + 16)
                        pe.wait_ge(s_kvs, h + 1)
                        for dc in range(KC):
                            for c in range(KC):
                                pe.matmul(p_s[0][:, dc * D:(dc + 1) * D], w[:, 0, c, dc * P:(dc + 1) * P], w[:, 1, c, :],
                                          start=c == 0, stop=c == KC - 1)
                        for c in range(KC):
                            ins = pe.matmul(p_s[1][0:1, 0:D], wring[:, j, 4 * D + c:4 * D + c + 1], w[:, 1, c, :],
                                            start=c == 0, stop=c == KC - 1)
                        ins.then_inc(s_vo, 1)
                        pe.wait_ge(s_gs, hp + 1)
                        for mc in range(KC):
                            for dc in range(KC):
                                pe.transpose(p_u[0][:, dc * D + mc * P:dc * D + (mc + 1) * P],
                                             gs[:, 2 * j + mc, dc * P:(dc + 1) * P], g["ident"][:, :])
                            ins = pe.transpose(p_u[1][0:1, mc * P:(mc + 1) * P], gs[:, 2 * j + mc, D:D + 1], g["ident"][:, :])
                        ins.then_inc(s_gt, 1)
                        pe.wait_ge(s_voc, h + 1)
                        pe.wait_ge(s_gtc, h + 1)
                        for mc in range(KC):
                            for dc in range(KC):
                                pe.matmul(p_s[0][:, mc * D:(mc + 1) * D], gt[:, dc, mc * P:(mc + 1) * P], wvo[:, dc, :],
                                          start=dc == 0, stop=False)
                            ins = pe.matmul(p_s[0][:, mc * D:(mc + 1) * D], kst[:, mc * P:(mc + 1) * P], bvo[:, :],
                                            start=False, stop=True)
                        ins.then_inc(s_kv, 1)
            pe.wait_ge(s_kvs, MH + 1)
            pe.sem_inc(s_n, MH)

            def features(t, q):
                tile = bass.ds(t * TN, TN)
                pe.wait_ge(s_eq, 4 * t + (q + 1))
                for m in range(4):
                    f = slice((4 * q + m) * P, (4 * q + m + 1) * P)
                    out = p_g[q % 2][:, m * TN:(m + 1) * TN]
                    for c in range(KC):
                        pe.matmul(out, wp[:, 0, c, f], g["xn_t"][:, c, tile], start=c == 0, stop=False)
                    ins = pe.matmul(out, augw[:, 0, f], augx[:, 0, tile], start=False, stop=True)
                ins.then_inc(s_uq, 1)

            def heads(t, q):
                pe.wait_ge(s_eps, 4 * t + (q + 1))
                for j in range(2):
                    h = 2 * q + j
                    pe.wait_ge(s_nfree, 8 * t + (h + 1))
                    for mc in range(KC):
                        ins = pe.matmul(p_u[j][0:TN, 0:D + 1], eq[:, q, 2 * j + mc, :], kvs[:, h, mc, :],
                                        start=mc == 0, stop=mc == KC - 1)
                    ins.then_inc(s_n, 1)

            def queries(t, last):
                features(t, 1)
                heads(t, 0)
                features(t, 2)
                heads(t, 1)
                features(t, 3)
                heads(t, 2)
                if not last:
                    features(t + 1, 0)
                heads(t, 3)
            features(0, 0)
            with pe.Fori(0, NT - 1) as t:
                queries(t, False)
            queries(NT - 1, True)

        @block.scalar
        def _(act):
            act.sem_inc(s_folded, 1)
            act.sem_inc(s_kvs, 1)

            def folded(h, slot):
                act.wait_ge(s_fold, h + 1)
                for dc in range(KC):
                    act.activation(wp[:, 1, dc, bass.ds(h * D, D)], p_g[2 + dc][:, 0:D], ACT.Copy, scale=MSCALE)
                act.copy(w2[:, 0, bass.ds(h + MH, 1)], p_g[2][:, bass.ds(h + (D + MH), 1)])
                act.copy(w2[:, 1, bass.ds(h + MH, 1)], p_g[3][:, bass.ds(h + (D + MH), 1)]).then_inc(s_folded, 1)
            paired(act, MH, folded)
            act.sem_inc(s_qfree, 2)

            with act.Fori(0, NW) as wp2:
                for wslot in range(2):
                    w = wp2 * 2 + wslot

                    def square(t, slot):
                        n = w * NT + t
                        act.wait_ge(s_q, n + 3)
                        act.wait_ge(s_qfree, n + 1)
                        for j in range(2):
                            ins = act.activation(junk[:, slot, j, :], p_u[slot][0:TN, j * D:(j + 1) * D], ACT.Square,
                                                 accum_out=sq[:, bass.ds(t * NB + 2 * w + j, 1)])
                        ins.then_inc(s_qfree, 1)
                    flipped(act, NT, 1 - wslot, square)
            act.sem_inc(s_aug, 2)

            def spread(t, slot):
                act.wait_ge(s_st, t + 3)
                act.copy(augx[:, :, bass.ds(t * TN, TN)],
                         p_u[slot][:, :].bitcast(BF16)[0:AUG, 0:2 * P].rearrange("p (i n) -> p i n", i=2)[:, :, 0:TN]).then_inc(s_aug, 1)
            paired(act, NT, spread)

            with act.Fori(0, NW // 2) as hq:
                for odd in range(2):
                    hp = hq * 2 + odd

                    def keys(t, slot):
                        n = hp * NT + t
                        act.wait_ge(s_u, n + 3)
                        act.wait_ge(s_efree, n + 1)
                        act.activation(ek[:, slot, :], p_u[slot][0:TN, :], ACT.Exp).then_inc(s_e, 1)
                    flipped(act, NT, (1 + odd) % 2, keys)
                    for j in range(2):
                        h = hp * 2 + j
                        act.wait_ge(s_vo, h + 1)
                        act.copy(wvo[:, :, :], p_s[0][:, :].rearrange("p (c d) -> p c d", c=KC))
                        act.copy(bvo[:, :], p_s[1][0:1, 0:D]).then_inc(s_voc, 1)
                        act.wait_ge(s_kv, h + 1)
                        act.copy(kvs[:, bass.ds(h, 1), :, 0:D],
                                 p_s[0][:, :].rearrange("p (o c d) -> p o c d", o=1, c=KC)).then_inc(s_kvs, 1)
            act.sem_inc(s_eq, 2)

            with act.Fori(0, NT) as t:
                for q in range(4):
                    act.wait_ge(s_uq, 4 * t + (q + 1))
                    act.wait_ge(s_n, 8 * t + (2 * q + 2))
                    act.activation(eq[:, q, :, :], p_g[q % 2][:, 0:4 * TN].rearrange("p (m n) -> p m n", m=4),
                                   ACT.Exp).then_inc(s_eq, 1)

        @block.vector
        def _(v):
            c = Steps(v, s_dve)
            v.wait_ge(s_const, 48)
            v.tensor_tensor(bsq[:, :, :], pb[:, :, D:D + NB], pb[:, :, D:D + NB], ALU.mult).then_inc(s_bsq, 1)
            v.wait_ge(s_crow, 1)
            c.done(v.tensor_copy(c0[:, :], p_s[1][0:TN, 0:NB]))
            c.link(v.tensor_scalar(crow[:, :], p_s[0][0:NB, 0:D], MSCALE, None, ALU.mult))
            for r in range(PARTS):
                c.link(v.tensor_copy(cpart[:, r, :], crow[:, :]))
                if r < PARTS - 1:
                    c.link(v.tensor_tensor(crow[:, :], crow[:, :], cpart[:, r, :], ALU.subtract))
            v.sem_inc(s_cpart, 1)
            v.memset(p_s[0][:, :], 0.0).then_inc(s_cs, 1)
            c.done(v.memset(s54[:, :, :], 1.0))
            v.sem_inc(s_folded, 1)

            def folded(h, slot):
                v.wait_ge(s_fold, h + 1)
                for dc in range(KC):
                    v.tensor_scalar(wp[:, 0, dc, bass.ds(h * D, D)], p_g[dc][:, 0:D], MSCALE, None, ALU.mult)
                v.tensor_copy(w2[:, 0, bass.ds(h, 1)], p_g[0][:, bass.ds(h + D, 1)])
                v.tensor_copy(w2[:, 1, bass.ds(h, 1)], p_g[1][:, bass.ds(h + D, 1)]).then_inc(s_folded, 1)
            paired(v, MH, folded)
            v.wait_ge(s_cs, NT + 1)
            c.link(v.tensor_copy(csum[:, :], p_s[0][:, 0:D + 1]))
            v.wait_ge(s_folded, 2 * MH + 2)
            for b in p_g:
                v.memset(b[:, :], 0.0)
            v.memset(p_s[1][:, :], 0.0).then_inc(s_zero, 1)

            def stage(t, slot):
                return v.tensor_scalar(xs[:, slot, :, :], g["xn_t"][:, :, bass.ds(t * TN, TN)], 1.0, None, ALU.mult)

            def stage_cross(t, slot):
                v.wait_ge(s_cross, t + 1)
                stage(t, slot).then_inc(s_xs, 1)
            paired(v, NT, stage_cross)
            v.wait_ge(s_cross, NT + 2)
            with v.Fori(0, NW) as wp2:
                for wslot in range(2):
                    def stage_square(t, slot):
                        v.wait_ge(s_q, (wp2 * 2 + wslot) * NT + t + 1)
                        stage(t, slot).then_inc(s_xs, 1)
                    flipped(v, NT, 1 - wslot, stage_square)
            v.wait_ge(s_qfree, 2 + 2 * NW * NT)
            c.link(v.scalar_tensor_tensor(out=sqp[:, :].rearrange("p (t n) -> p t n", t=NT),
                                          in0=p_s[1][0:TN, 0:NT * NB].rearrange("p (t n) -> p t n", t=NT), scalar=2.0,
                                          in1=c0[:, :].rearrange("p (o n) -> p o n", o=1).to_broadcast([TN, NT, NB]),
                                          op0=ALU.mult, op1=ALU.add))
            c.link(v.tensor_tensor(sqp[:, :], sqp[:, :], sq[:, :], ALU.add))
            c.link(v.tensor_scalar(sqp[:, :], sqp[:, :], -0.5 * MSCALE * MSCALE, None, ALU.mult))
            left = sqp[:, :].rearrange("p (t i h) -> p t i h", t=NT, i=2)
            for r in range(PARTS):
                part = s54[:, :, :].rearrange("p t (i q) -> p t i q", i=2)[:, :, :, r * MH:(r + 1) * MH]
                c.link(v.tensor_copy(part, left))
                if r < PARTS - 1:
                    c.link(v.tensor_tensor(left, left, part, ALU.subtract))

            def stage_parts(t, slot):
                v.wait_ge(s_st, t + 1)
                v.tensor_scalar(s54s[:, slot:slot + 1, :], s54[:, bass.ds(t, 1), :], 1.0, None, ALU.mult).then_inc(s_s54, 1)
            paired(v, NT, stage_parts)
            v.wait_ge(s_aug, NT + 2)
            with v.Fori(0, NW // 2) as hq:
                for odd in range(2):
                    hp = hq * 2 + odd

                    def stage_key(t, slot):
                        v.wait_ge(s_u, hp * NT + t + 1)
                        v.tensor_scalar(augs[:, slot, :], augx[:, 1, bass.ds(t * TN, TN)], 1.0, None, ALU.mult)
                        stage(t, slot).then_inc(s_xs, 1)
                    flipped(v, NT, (1 + odd) % 2, stage_key)
                    v.wait_ge(s_efree, hp * NT + (NT + 2))
                    v.wait_ge(s_gt, 2 * hp + 1)
                    for m in range(4):
                        ins = v.tensor_tensor(gs[:, m, :], p_g[m][:, 0:D + 1], csum[:, :], ALU.add)
                    ins.then_inc(s_gs, 1)
                    v.wait_ge(s_gs, hp + 1)
                    v.tensor_copy(kvs[:, bass.ds(hp * 2, 2), :, D],
                                  gs[:, :, D].rearrange("p (j m) -> p j m", j=2)).then_inc(s_kdiag, 1)
                    for b in p_g:
                        ins = v.memset(b[:, :], 0.0)
                    ins.then_inc(s_zero, 1)
                    for j in range(2):
                        v.wait_ge(s_gt, hp * 2 + (j + 2))
                        v.tensor_copy(gt[:, :, :], p_u[0][:, :].rearrange("p (c d) -> p c d", c=KC))
                        v.tensor_copy(kst[:, :], p_u[1][0:1, 0:D]).then_inc(s_gtc, 1)
            v.sem_inc(s_nfree, 2)

            def add_eps(t, q):
                v.wait_ge(s_eq, 4 * t + (q + 3))
                v.tensor_scalar(eq[:, q, :, :], eq[:, q, :, :], 16e-6, None, ALU.add).then_inc(s_eps, 1)

            def add_heads(t, q, slot):
                for j in range(2):
                    h = 2 * q + j
                    n = p_u[j][0:TN, :]
                    v.wait_ge(s_n, 8 * t + (MH + h + 1))
                    v.reciprocal(rz[:, h:h + 1], n[:, D:D + 1]).then_inc(s_rz, 1)
                    v.wait_ge(s_rz, 8 * t + (h + 1))
                    if h == 0:
                        v.wait_ge(s_y, t + 1)
                        v.tensor_scalar(acc[:, slot, :], n[:, 0:D], rz[:, 0:1], None, ALU.mult).then_inc(s_nfree, 1)
                    else:
                        v.wait_ge(s_nfree, 8 * t + (h + 2))
                        v.scalar_tensor_tensor(out=acc[:, slot, :], in0=n[:, 0:D], scalar=rz[:, h:h + 1],
                                               in1=acc[:, slot, :], op0=ALU.mult, op1=ALU.add).then_inc(s_nfree, 1)

            def queries(t, slot, last=False):
                add_eps(t, 1)
                add_heads(t, 0, slot)
                add_eps(t, 2)
                add_heads(t, 1, slot)
                add_eps(t, 3)
                add_heads(t, 2, slot)
                if not last:
                    add_eps(t + 1, 0)
                add_heads(t, 3, slot)
            add_eps(0, 0)
            with v.Fori(0, NT // 2) as i:
                queries(2 * i, 0)
                queries(2 * i + 1, 1)
            queries(NT - 1, 0, last=True)


class Mlp:

    def __init__(self, k, name, chunks, func):
        self.chunks, self.func = chunks, func
        self.xin = k.sb(name + "_xin", [TN, 2, D])
        self.xt = k.sb(name + "_xt", [P, 2, KC, TN])
        self.ht = k.sb(name + "_ht", [P, 2, chunks, TN])
        self.w1 = k.sb(name + "_w1", [P, KC, chunks * P])
        self.w2 = k.sb(name + "_w2", [P, chunks, D])
        self.b1 = k.sb(name + "_b1", [P, chunks])
        self.banks = -(-chunks // 4)
        self.p_x = [k.ps(f"{name}_px{i}") for i in range(2)]
        self.p_h = [[k.ps(f"{name}_ph{i}{j}") for j in range(self.banks)] for i in range(2)]
        self.p_y = [k.ps(f"{name}_py{i}") for i in range(2)]
        self.s_w = k.sem(name + "_w")
        self.s_in = k.sem(name + "_in")
        self.s_tr = k.sem(name + "_tr")
        self.s_xt = k.sem(name + "_xt")
        self.s_h = k.sem(name + "_h")
        self.s_ht = k.sem(name + "_ht")
        self.s_y = k.sem(name + "_y")
        self.s_take = k.sem(name + "_take")

    def load(self, sp, w1, w2, b1):
        sp.dma_start(self.w1[:, :, :], w1).then_inc(self.s_w, 16)
        sp.dma_start(self.w2[:, :, :], w2).then_inc(self.s_w, 16)
        sp.dma_start(self.b1[:, :], b1).then_inc(self.s_w, 16)

    def schedule(self, eng, ahead, mid, behind):
        ahead(0, 0)
        ahead(1, 1)
        mid(0, 0)

        def pair(i):
            ahead(2 * i + 2, 0)
            mid(2 * i + 1, 1)
            behind(2 * i, 0)
            ahead(2 * i + 3, 1)
            mid(2 * i + 2, 0)
            behind(2 * i + 1, 1)
        pair(0)
        with eng.Fori(1, (NT - 3) // 2) as i:
            pair(i)
        ahead(NT - 1, 0)
        mid(NT - 2, 1)
        behind(NT - 3, 0)
        mid(NT - 1, 0)
        behind(NT - 2, 1)
        behind(NT - 1, 0)

    def on_pe(self, pe, ident):
        for s in (self.s_tr, self.s_h, self.s_y):
            pe.sem_inc(s, 2)
        pe.wait_ge(self.s_w, 48)

        def transpose(t, slot):
            pe.wait_ge(self.s_in, t + 1)
            pe.wait_ge(self.s_xt, t + 1)
            for c in range(KC):
                ins = pe.transpose(self.p_x[slot][:, c * TN:(c + 1) * TN], self.xin[:, slot, c * P:(c + 1) * P],
                                   ident[0:TN, 0:TN])
            ins.then_inc(self.s_tr, 1)

        def hidden(t, slot):
            pe.wait_ge(self.s_xt, t + 3)
            pe.wait_ge(self.s_ht, t + 1)
            for f in range(self.chunks):
                out = self.p_h[slot][f // 4][:, (f % 4) * TN:(f % 4 + 1) * TN]
                for c in range(KC):
                    ins = pe.matmul(out, self.w1[:, c, f * P:(f + 1) * P], self.xt[:, slot, c, :], start=c == 0, stop=c == KC - 1)
            ins.then_inc(self.s_h, 1)

        def output(t, slot):
            pe.wait_ge(self.s_ht, t + 3)
            pe.wait_ge(self.s_take, t + 1)
            for f in range(self.chunks):
                ins = pe.matmul(self.p_y[slot][0:TN, 0:D], self.ht[:, slot, f, :], self.w2[:, f, :],
                                start=f == 0, stop=f == self.chunks - 1)
            ins.then_inc(self.s_y, 1)
        self.schedule(pe, transpose, hidden, output)

    def on_act(self, act):
        act.sem_inc(self.s_xt, 2)
        act.sem_inc(self.s_ht, 2)

        def copy(t, slot):
            act.wait_ge(self.s_tr, t + 3)
            act.wait_ge(self.s_h, t + 1)
            act.copy(self.xt[:, slot, :, :], self.p_x[slot][:, 0:KC * TN].rearrange("p (c n) -> p c n", c=KC)).then_inc(self.s_xt, 1)

        def function(t, slot):
            act.wait_ge(self.s_h, t + 3)
            act.wait_ge(self.s_y, t + 1)
            for f in range(self.chunks):
                ins = act.activation(self.ht[:, slot, f, :], self.p_h[slot][f // 4][:, (f % 4) * TN:(f % 4 + 1) * TN],
                                     self.func, bias=self.b1[:, f:f + 1])
            ins.then_inc(self.s_ht, 1)
        self.schedule(act, copy, function, lambda t, slot: None)

    def on_dve(self, v, put, take):
        v.sem_inc(self.s_take, 2)

        def inward(t, slot):
            v.wait_ge(self.s_tr, t + 1)
            put(t, slot, self.xin[:, slot, :]).then_inc(self.s_in, 1)

        def outward(t, slot):
            v.wait_ge(self.s_y, t + 3)
            take(t, slot, self.p_y[slot][0:TN, 0:D]).then_inc(self.s_take, 1)
        self.schedule(v, inward, lambda t, slot: None, outward)


def affine(eng, go, sem, base, x, gain, bias, ready=None):
    with eng.Fori(0, NT) as t:
        tile = x[:, bass.ds(t, 1), 0:D]
        if ready is not None:
            hold(eng, go, ready[0], t + ready[1])
        eng.tensor_tensor(tile, tile, gain.rearrange("p (o d) -> p o d", o=1), ALU.mult).then_inc(sem, 1)
        hold(eng, go, sem, 2 * t + (base + 1))
        eng.tensor_tensor(tile, tile, bias.rearrange("p (o d) -> p o d", o=1), ALU.add).then_inc(sem, 1)


def mix_out(nc, a, g, scr):
    with ExitStack() as ctx:
        k = Kit(nc, ctx)
        mlp = Mlp(k, "mm", KC, ACT.Relu)
        norm = Norm(k, "mn")
        rows = k.sb("mrows", [TN, 5, D])
        s_rows = k.sem("mo_rows")
        s_dve = k.sem("mo_dve")
        s_ap = k.sem("mo_ap")
        s_pool = k.sem("mo_pool")
        s_put = k.sem("mo_put")
        s_go = k.sem("mo_go")
        block = ctx.enter_context(nc.Block())
        xn = g["xn"]

        @block.sync
        def _(sp):
            sp.dma_start(rows[:, :, :].rearrange("p r d -> p (r d)"), row(a["m_rows"], TN)).then_inc(s_rows, 16)
            mlp.load(sp, a["m_w1"], a["m_w2"], a["m_b1"])

        @block.tensor
        def _(pe):
            mlp.on_pe(pe, g["ident"])

        @block.scalar
        def _(act):
            mlp.on_act(act)

        @block.gpsimd
        def _(pool):
            pool.wait_ge(s_rows, 16)
            affine(pool, s_go, s_pool, 0, xn, rows[:, 0, :], rows[:, 1, :], ready=(s_ap, 1))
            affine(pool, s_go, s_pool, 2 * NT, xn, rows[:, 3, :], rows[:, 4, :], ready=(s_ap, NT + 1))
            with pool.Fori(0, NT) as t:
                hold(pool, s_go, s_pool, 2 * t + (2 * NT + 2))
                acc = g["xacc"][:, bass.ds(t, 1), :]
                pool.tensor_tensor(acc, acc, xn[:, bass.ds(t, 1), 0:D], ALU.add)

        @block.vector
        def _(v):
            c = Steps(v, s_dve)
            norm.moments(v, c, xn, 1e-6)
            with v.Fori(0, NT) as t:
                norm.apply(v, xn[:, bass.ds(t, 1), 0:D], xn[:, bass.ds(t, 1), 0:D], t).then_inc(s_ap, 1)
            v.wait_ge(s_rows, 16)

            def put(t, slot, xin):
                v.wait_ge(s_pool, 2 * t + 2)
                return v.tensor_scalar(xin.rearrange("p (o d) -> p o d", o=1), xn[:, bass.ds(t, 1), 0:D], 1.0, None, ALU.mult)

            def take(t, slot, y):
                tile = xn[:, bass.ds(t, 1), 0:D]
                v.tensor_tensor(tile, tile, y.rearrange("p (o d) -> p o d", o=1), ALU.add).then_inc(s_put, 1)
                v.wait_ge(s_put, t + 1)
                return v.tensor_tensor(tile, tile, rows[:, 2:3, :], ALU.add)
            mlp.on_dve(v, put, take)
            v.wait_ge(mlp.s_take, NT + 2)
            norm.moments(v, c, xn, 1e-6)
            with v.Fori(0, NT) as t:
                norm.apply(v, xn[:, bass.ds(t, 1), 0:D], xn[:, bass.ds(t, 1), 0:D], t).then_inc(s_ap, 1)


def gnn(nc, a, g, scr):
    with ExitStack() as ctx:
        k = Kit(nc, ctx)
        NG = ETILES // GRP
        SL = 4
        hid, agg = g["xn"], g["xn_t"]
        q_sb = k.sb("q_sb", [TN, NT * D])
        cnt_t = k.sb("cnt_t", [N_ET, NT * TN])
        target = k.sb("target", [P, ETILES], I32)
        source = k.sb("source", [P, ETILES])
        wo = k.sb("wo", [P, KC, D])
        et = k.sb("et_t", [P, KC, N_ET])
        ewo = k.sb("ewo", [N_ET, D])
        rows = k.sb("grows", [TN, 6, D])
        xt = k.sb("gxt", [P, 2, KC, TN])
        idx = k.sb("idx", [P, SL, GRP], I32)
        kv = k.sb("kv", [P, SL, GRP, 2 * D])
        prod = k.sb("prod", [P, GRP, GH * GH * GD])
        flat, used = prod[:, :, :].rearrange("p j m -> p (j m)"), 0

        def share(parts, a_, b_):
            nonlocal used
            used += a_ * b_
            assert used <= GRP * GH * GH * GD
            return flat[0:parts, used - a_ * b_:used].rearrange("p (a b) -> p a b", a=a_)
        kvst = share(TN, 2, 2 * D)
        wqkv = share(P, KC, 3 * D)
        win = share(P, KC, D)
        hs = share(TN, 2, D)
        bin_ = share(TN, 1, D)
        cs = share(N_ET, 2, TN)
        sc = k.sb("sc", [P, GRP * GH * GH])
        mx = k.sb("mx", [P, GRP * GH])
        sm = k.sb("sm", [P, GRP * GH])
        ex = k.sb("ex", [P, GRP * GH * GH])
        attn = k.sb("attn", [P, 2, GRP, GH * GH])
        wv = k.sb("wv", [P, GRP, GH, D])
        table = wv[:, :, :, :].rearrange("p j g d -> p (j g d)")[:, 0:TCOLS].bitcast(I32)
        q_last = k.sb("q_last", [P, D])
        oh = k.sb("oh", [P, SL, GRP, TN])
        oht = k.sb("oht", [TN, 2, GRP, P])
        norm = Norm(k, "gn")
        p_q = [k.ps(f"p_q{i}") for i in range(2)]
        p_a = [k.ps(f"p_a{i}") for i in range(4)]
        p_t = k.ps("p_t")
        p_o = k.ps("p_o")

        s_const = k.sem("gn_const")
        s_edge = k.sem("gn_edge")
        s_w = k.sem("gn_w")
        s_rows = k.sem("gn_rows")
        s_hs = k.sem("gn_hs")
        s_tr = k.sem("gn_tr")
        s_xt = k.sem("gn_xt")
        s_qkv = k.sem("gn_qkv")
        s_kvst = k.sem("gn_kvst")
        s_kvd = [k.sem(f"gn_kvd{i}") for i in range(2)]
        s_h0 = k.sem("gn_h0")
        s_ewo = k.sem("gn_ewo")
        s_ewoc = k.sem("gn_ewoc")
        s_start = k.sem("gn_start")
        s_vgo = k.sem("gn_vgo")
        s_pgo = k.sem("gn_pgo")
        s_go = k.sem("gn_go")
        s_azero = k.sem("gn_azero")
        s_idx = k.sem("gn_idx")
        s_kv = [k.sem(f"gn_kv{i}") for i in range(SL)]
        s_oh = k.sem("gn_oh")
        s_t = k.sem("gn_t")
        s_tc = k.sem("gn_tc")
        s_qe = k.sem("gn_qe")
        s_pk = k.sem("gn_pk")
        s_ql = k.sem("gn_ql")
        s_pp = k.sem("gn_pp")
        s_chain = k.sem("gn_chain")
        s_ex = k.sem("gn_ex")
        s_attn = k.sem("gn_attn")
        s_wv = k.sem("gn_wv")
        s_wa = k.sem("gn_wa")
        s_agg = k.sem("gn_agg")
        s_acc = k.sem("gn_acc")
        s_os = k.sem("gn_os")
        s_o = k.sem("gn_o")
        s_hm = k.sem("gn_hm")
        s_dve = k.sem("gn_dve")
        s_ap = k.sem("gn_ap")
        s_pool = k.sem("gn_pool")
        s_relu = k.sem("gn_relu")
        block = ctx.enter_context(nc.Block())
        NORM_STEPS = NT + 22
        per = NG * GRP
        ACT_G = (2, 1, 2, 1)
        assert NG % (2 * SL) == 0 and GRP == 4
        p_qt = [p_q[0][:, 0:D], p_q[0][:, D:2 * D], p_q[1][:, 0:D], p_o[:, 0:D]]

        def gathered(l, i):
            return (l * (NG // SL) + i + 1) * (16 * GRP)

        def edge_loop(eng, body):
            for u in range(SL):
                body(u, u, 0, lambda d, u=u: u + d >= 0)
            with eng.Fori(1, NG // SL - 1) as i:
                for u in range(SL):
                    body(i * SL + u, u, i, lambda d: True)
            for u in range(SL):
                body(NG - SL + u, u, NG // SL - 1, lambda d, u=u: u + d < SL)

        def buckets(eng, kk):
            word = eng.value_load(g["tab"][0:1, bass.ds(kk, 1)], min_val=0, max_val=(1 << 20) - 1)
            return [nc.s_assert_within((word >> (5 * j)) & 31, 0, NT - 1,
                                       skip_runtime_bounds_check_because="the table's buckets are at most NT - 1")
                    for j in range(GRP)]

        @block.sync
        def _(sp):
            sp.dma_start(table[:, :], scr["table"].rearrange("(p c) o -> p (c o)", p=P)).then_inc(s_const, 16)
            sp.dma_start(cnt_t[:, :].rearrange("e (b n) -> e b n", b=NT), scr["counts"].rearrange("(b e) n -> e b n", e=N_ET)).then_inc(s_const, 16)
            sp.dma_start(win[:, :, :], a["g_win"]).then_inc(s_kvd[0], 16)
            sp.dma_start(bin_[:, :, :], row(a["g_bin"], TN).rearrange("p (o d) -> p o d", o=1)).then_inc(s_kvd[1], 16)
            with sp.Fori(0, LAYERS) as l:
                sp.wait_ge(s_relu, l * NT + 1)
                one = bass.ds(l, 1)
                sp.dma_start(wqkv[:, :, :].rearrange("p (o c) d -> p o (c d)", o=1), a["g_wqkv"][:, one, :]).then_inc(s_w, 16)
                sp.dma_start(wo[:, :, :].rearrange("p (o c) d -> p o (c d)", o=1), a["g_wo"][:, one, :]).then_inc(s_w, 16)
                sp.dma_start(et[:, :, :].rearrange("p (o c) d -> p o (c d)", o=1), a["g_et"][:, one, :]).then_inc(s_w, 16)
                sp.dma_start(rows[:, :, :].rearrange("p (o r) d -> p o (r d)", o=1),
                             a["g_rows"][one, :].rearrange("o (x d) -> x o d", x=1).to_broadcast([TN, 1, 6 * D])).then_inc(s_w, 16)

                def store(t, slot):
                    sp.wait_ge(s_kvst, l * NT + t + (NT + 3))
                    sp.dma_start(scr["kv"][bass.ds(t * TN, TN), :], kvst[:, slot, :]).then_inc(s_kvd[slot], 16)
                with sp.Fori(0, NT // 2) as i:
                    store(2 * i, 0)
                    store(2 * i + 1, 1)
                store(NT - 1, 0)

        @block.tensor
        def _(pe):
            pe.wait_ge(s_const, 32)
            pe.wait_ge(s_kvd[0], 16)
            pe.sem_inc(s_h0, 2)

            def first(t, slot):
                pe.wait_ge(s_hs, t + 1)
                pe.wait_ge(s_kvst, t + 1)
                for c in range(KC):
                    ins = pe.matmul(p_q[slot][0:TN, 0:D], xt[:, slot, c, :], win[:, c, :], start=c == 0, stop=c == KC - 1)
                ins.then_inc(s_h0, 1)
            paired(pe, NT, first)
            pe.sem_inc(s_tr, 2)
            pe.sem_inc(s_qkv, 2)
            pe.sem_inc(s_o, 2)
            with pe.Fori(0, LAYERS) as l:
                node = l * NT
                pe.wait_ge(s_w, 64 * l + 64)
                for c in range(KC):
                    ins = pe.matmul(p_o[0:N_ET, 0:D], et[:, c, :], wo[:, c, :], start=c == 0, stop=c == KC - 1)
                ins.then_inc(s_ewo, 1)

                def transpose(t, slot):
                    pe.wait_ge(s_hs, node + t + (NT + 1))
                    pe.wait_ge(s_xt, node + t + 1)
                    for c in range(KC):
                        ins = pe.transpose(p_q[slot][:, c * TN:(c + 1) * TN], hs[:, slot, c * P:(c + 1) * P], g["ident"][0:TN, 0:TN])
                    ins.then_inc(s_tr, 1)

                def qkv(t, slot):
                    pe.wait_ge(s_xt, node + t + 3)
                    pe.wait_ge(s_kvst, node + t + (NT + 1))
                    for c in range(KC):
                        pe.matmul(p_a[2 * slot][0:TN, :], xt[:, slot, c, :], wqkv[:, c, 0:2 * D], start=c == 0, stop=c == KC - 1)
                    for c in range(KC):
                        ins = pe.matmul(p_a[2 * slot + 1][0:TN, 0:D], xt[:, slot, c, :], wqkv[:, c, 2 * D:3 * D], start=c == 0, stop=c == KC - 1)
                    ins.then_inc(s_qkv, 1)
                transpose(0, 0)
                with pe.Fori(0, NT // 2) as i:
                    transpose(2 * i + 1, 1)
                    qkv(2 * i, 0)
                    transpose(2 * i + 2, 0)
                    qkv(2 * i + 1, 1)
                qkv(NT - 1, 0)
                pe.wait_ge(s_kvst, node + (2 * NT + 2))

                def spread(kk, u):
                    pe.wait_ge(s_oh, l * NG + kk + 1)
                    for j in range(GRP):
                        ins = pe.transpose(p_t[0:TN, j * P:(j + 1) * P], oh[:, u, j, :], g["ident"][:, :])
                    ins.then_inc(s_t, 1)

                def sources(kk, u, guard):
                    bucket = buckets(pe, kk)
                    pe.wait_ge(s_tc, l * NG + kk + 1)
                    for j in range(GRP):
                        if guard and j in (0, 2):
                            pe.wait_ge(s_pk, (l * NG + kk) * (GRP - 1) + (2 - GRP + 1 if j == 0 else 0))
                        elif guard and j == GRP - 1:
                            pe.wait_ge(s_ql, l * NG + kk)
                        pe.matmul(p_qt[j], oht[:, u % 2, j, :],
                                  q_sb[:, bass.ds(bucket[j] * D, D)], start=True, stop=True).then_inc(s_qe, 1)

                def sums(kk, u, j, guard):
                    out = p_a[2 * (u % 2) + j // 2]
                    n = l * per + GRP * kk
                    pe.wait_ge(s_wv, n + (j + 1))
                    pe.wait_ge(s_wa, n + (j + 1))
                    if guard:
                        pe.wait_ge(s_acc, n + (j // 2 * 2 + 2 - 2 * GRP))
                    for c in range(KC):
                        for h in range(GH):
                            ins = pe.matmul(out[:, (j % 2) * 2 * TN + c * TN:(j % 2) * 2 * TN + (c + 1) * TN],
                                            wv[:, j, h, c * P:(c + 1) * P], oh[:, u, j, :], start=h == 0, stop=h == GH - 1)
                    ins.then_inc(s_agg, 1)

                spread(0, 0)
                sources(0, 0, False)

                def body(kk, u, i, has):
                    if has(1):
                        spread(kk + 1, (u + 1) % SL)
                        sources(kk + 1, (u + 1) % SL, True)
                    if has(-1):
                        sums(kk - 1, (u - 1) % SL, 0, has(-3))
                        sums(kk - 1, (u - 1) % SL, 1, has(-3))
                        sums(kk - 1, (u - 1) % SL, 2, has(-3))
                        sums(kk - 1, (u - 1) % SL, 3, has(-3))
                edge_loop(pe, body)
                for j in range(GRP):
                    sums(NG - 1, SL - 1, j, True)

                pe.wait_ge(s_ql, l * NG + NG)
                hold(pe, s_pgo, s_ewoc, l + 1)

                def project(t, slot):
                    pe.wait_ge(s_os, node + t + 2)
                    pe.wait_ge(s_hm, node + t + 1)
                    out = [p_t, p_o][slot][0:TN, 0:D]
                    for c in range(KC):
                        pe.matmul(out, xt[:, slot, c, :], wo[:, c, :], start=c == 0, stop=False)
                    pe.matmul(out, cs[:, slot, :], ewo[:, :], start=False, stop=True).then_inc(s_o, 1)
                paired(pe, NT, project)

        @block.scalar
        def _(act):
            act.sem_inc(s_xt, 2)
            act.sem_inc(s_os, 1)
            with act.Fori(0, LAYERS) as l:
                node = l * NT

                def copy(t, slot):
                    act.wait_ge(s_tr, node + t + 3)
                    act.wait_ge(s_qkv, node + t + 1)
                    act.copy(xt[:, slot, :, :], p_q[slot][:, 0:KC * TN].rearrange("p (c n) -> p c n", c=KC)).then_inc(s_xt, 1)
                paired(act, NT, copy)
                act.wait_ge(s_qkv, node + (NT + 2))

                def spread(kk, u, guard):
                    act.wait_ge(s_t, l * NG + kk + 1)
                    if guard:
                        act.wait_ge(s_qe, l * per + GRP * kk + (-GRP))
                    act.copy(oht[:, u % 2, :, :], p_t[0:TN, :].rearrange("p (j e) -> p j e", j=GRP)).then_inc(s_tc, 1)
                spread(0, 0, False)
                spread(1, 1, False)

                def last_q(kk, guard):
                    act.wait_ge(s_qe, l * per + GRP * kk + GRP)
                    if guard:
                        act.wait_ge(s_pp, l * NG + kk)
                    act.copy(q_last[:, :], p_qt[GRP - 1]).then_inc(s_ql, 1)
                last_q(0, False)

                def body(kk, u, i, has):
                    if has(1):
                        last_q(kk + 1, True)
                    act.wait_ge(s_chain, 5 * (l * NG + kk) + 3)
                    act.activation(ex[:, :], sc[:, :], ACT.Exp, scale=1.0 / 8.0).then_inc(s_ex, 1)
                    n = l * per + GRP * kk
                    act.wait_ge(s_kv[u], gathered(l, i))
                    act.wait_ge(s_attn, l * NG + kk + 1)
                    for j in range(GRP):
                        if has(-1):
                            act.wait_ge(s_agg, n + (j - GRP + 1))
                        for gg in range(GH - ACT_G[j], GH):
                            for h in range(GH):
                                ins = act.activation(wv[:, j, gg, h * GD:(h + 1) * GD], kv[:, u, j, D + gg * GD:D + (gg + 1) * GD],
                                                     ACT.Copy, scale=attn[:, u % 2, j, gg * GH + h:gg * GH + h + 1])
                        ins.then_inc(s_wa, 1)
                        if j == 1 and has(2):
                            spread(kk + 2, (u + 2) % SL, True)
                edge_loop(act, body)

                def staged(t, slot):
                    act.wait_ge(s_acc, l * per + per)
                    act.wait_ge(s_o, node + t + 1)
                    act.copy(xt[:, slot, :, :], agg[:, :, bass.ds(t * TN, TN)])
                    act.copy(cs[:, slot, :], cnt_t[:, bass.ds(t * TN, TN)]).then_inc(s_os, 1)
                paired(act, NT, staged)

        @block.gpsimd
        def _(pool):
            with pool.Fori(0, LAYERS) as l:
                pool.wait_ge(s_os, l * NT + 1)
                hold(pool, s_go, s_start, l + 1)
                pool.memset(agg[:, :, :], 0.0).then_inc(s_azero, 1)

                def columns(kk, slot):
                    pool.tensor_copy(idx[:, slot, :], target[:, bass.ds(GRP * kk, GRP)]).then_inc(s_idx, 1)

                def gather(slot, j):
                    pool.indirect_dma_start(out=kv[:, slot, j, :], out_offset=None, in_=scr["kv"],
                                            in_offset=bass.IndirectOffsetOnAxis(ap=idx[:, slot, j:j + 1], axis=0)).then_inc(s_kv[slot], 16)

                def product(kk, slot, i):
                    j = GRP - 1
                    pool.wait_ge(s_ql, l * NG + kk + 1)
                    pool.wait_ge(s_kv[slot], gathered(l, i))
                    pool.tensor_tensor(prod[:, j, :].rearrange("p (h g d) -> p h g d", h=GH, g=GH),
                                       q_last[:, :].rearrange("p (h o d) -> p h o d", h=GH, o=1).to_broadcast([P, GH, GH, GD]),
                                       kv[:, slot, j, 0:D].rearrange("p (o g d) -> p o g d", o=1, g=GH).to_broadcast([P, GH, GH, GD]),
                                       ALU.mult).then_inc(s_pp, 1)

                def values(kk, u, j, has):
                    m = GH - ACT_G[j]
                    if has(-1):
                        pool.wait_ge(s_agg, l * per + GRP * kk + (j - GRP + 1))
                    pool.tensor_tensor(wv[:, j, 0:m, :].rearrange("p g (h d) -> p g h d", h=GH),
                                       kv[:, u, j, D:D + m * GD].rearrange("p (g o d) -> p g o d", g=m, o=1).to_broadcast([P, m, GH, GD]),
                                       attn[:, u % 2, j, 0:m * GH].rearrange("p (g h o) -> p g h o", g=m, o=1).to_broadcast([P, m, GH, GD]),
                                       ALU.mult).then_inc(s_wv, 1)
                pool.wait_ge(s_edge, 1)
                pool.wait_ge(s_kvd[0], 16 * (NT - NT // 2) * (l + 1) + 16)
                pool.wait_ge(s_kvd[1], 16 * (NT // 2) * (l + 1) + 16)
                pool.sem_inc(s_go, 1)
                for slot in range(SL - 1):
                    columns(slot, slot)
                hold(pool, s_go, s_idx, NG * l + SL - 1)
                for slot in range(SL - 1):
                    for j in range(GRP):
                        gather(slot, j)
                product(0, 0, 0)

                def body(kk, u, i, has):
                    ahead = (u + 3) % SL
                    pool.wait_ge(s_kv[u], gathered(l, i))
                    pool.wait_ge(s_attn, l * NG + kk + 1)
                    if has(1):
                        product(kk + 1, (u + 1) % SL, i if u < SL - 1 else i + 1)
                    values(kk, u, 0, has)
                    if has(3):
                        columns(kk + 3, ahead)
                    values(kk, u, 1, has)
                    if has(3):
                        if has(-1):
                            pool.wait_ge(s_wv, l * per + GRP * kk)
                            pool.wait_ge(s_wa, l * per + GRP * kk)
                        hold(pool, s_go, s_idx, l * NG + kk + 4)
                        gather(ahead, 0)
                        gather(ahead, 1)
                    values(kk, u, 2, has)
                    values(kk, u, 3, has)
                    if has(3):
                        gather(ahead, 2)
                        gather(ahead, 3)
                edge_loop(pool, body)
                rowg, rowb = rows[:, 4:5, :], rows[:, 5:6, :]
                with pool.Fori(0, NT) as t:
                    tile = hid[:, bass.ds(t, 1), 0:D]
                    hold(pool, s_go, s_ap, l * NT + t + 1)
                    pool.tensor_tensor(tile, tile, rowg, ALU.mult).then_inc(s_pool, 1)
                    hold(pool, s_go, s_pool, 2 * l * NT + 2 * t + 1)
                    pool.tensor_tensor(tile, tile, rowb, ALU.add).then_inc(s_pool, 1)

        @block.vector
        def _(v):
            v.wait_ge(s_const, 32)
            v.wait_ge(s_kvd[1], 16)
            c = Steps(v, s_dve)
            c.link(v.tensor_scalar(target[:, :], table[:, 0:ETILES], (1 << NODE_BITS) - 1, None, ALU.bitwise_and))
            c.link(v.tensor_scalar(table[:, 0:ETILES], table[:, 0:ETILES], NODE_BITS, None, ALU.logical_shift_right))
            v.tensor_copy(source[:, :], table[:, 0:ETILES])
            v.sem_inc(s_edge, 1)
            v.sem_inc(s_kvst, 2)

            def stage0(t, slot):
                v.wait_ge(s_h0, t + 1)
                v.tensor_scalar(xt[:, slot, :, :], agg[:, :, bass.ds(t * TN, TN)], 1.0, None, ALU.mult).then_inc(s_hs, 1)

            def take0(t, slot):
                v.wait_ge(s_h0, t + 3)
                v.tensor_tensor(hid[:, bass.ds(t, 1), 0:D], p_q[slot][0:TN, 0:D].rearrange("p (o d) -> p o d", o=1),
                                bin_[:, :, :], ALU.add).then_inc(s_kvst, 1)
            stage0(0, 0)
            with v.Fori(0, NT // 2) as i:
                stage0(2 * i + 1, 1)
                take0(2 * i, 0)
                stage0(2 * i + 2, 0)
                take0(2 * i + 1, 1)
            take0(NT - 1, 0)
            v.wait_ge(s_kvst, NT + 2)
            v.sem_inc(s_hm, 2)
            v.sem_inc(s_relu, 1)
            with v.Fori(0, LAYERS) as l:
                node = l * NT
                v.sem_inc(s_start, 1)
                v.wait_ge(s_w, 64 * l + 64)
                v.wait_ge(s_ewo, l + 1)
                v.tensor_tensor(ewo[:, :], p_o[0:N_ET, 0:D], rows[0:N_ET, 3, :], ALU.add).then_inc(s_ewoc, 1)

                def stage(t, slot):
                    v.wait_ge(s_tr, node + t + 1)
                    v.tensor_scalar(hs[:, slot:slot + 1, :], hid[:, bass.ds(t, 1), 0:D], 1.0, None, ALU.mult).then_inc(s_hs, 1)

                def take(t, i, slot):
                    v.wait_ge(s_qkv, node + t + 3)
                    v.wait_ge(s_kvd[slot], 16 * ((NT - NT // 2 if slot == 0 else NT // 2) * l + i) + 16)
                    v.tensor_tensor(kvst[:, slot, :], p_a[2 * slot][0:TN, :], rows[:, 0:2, :].rearrange("p r d -> p (r d)"), ALU.add)
                    v.tensor_tensor(q_sb[:, bass.ds(t * D, D)], p_a[2 * slot + 1][0:TN, 0:D], rows[:, 2, :], ALU.add).then_inc(s_kvst, 1)
                stage(0, 0)
                with v.Fori(0, NT // 2) as i:
                    stage(2 * i + 1, 1)
                    take(2 * i, i, 0)
                    stage(2 * i + 2, 0)
                    take(2 * i + 1, i, 1)
                take(NT - 1, NT // 2, 0)
                v.wait_ge(s_azero, l + 1)

                def onehot(kk, u):
                    v.tensor_tensor(oh[:, u, :, :],
                                    source[:, bass.ds(GRP * kk, GRP)].rearrange("p (j o) -> p j o", o=1).to_broadcast([P, GRP, TN]),
                                    g["iota_n"][:, :].rearrange("p (o n) -> p o n", o=1).to_broadcast([P, GRP, TN]),
                                    ALU.is_equal).then_inc(s_oh, 1)

                def add_sum(kk, u, bucket, j):
                    n = l * per + GRP * kk
                    tile = agg[:, :, bass.ds(bucket[j] * TN, TN)]
                    v.wait_ge(s_agg, n + (j // 2 * 2 + 2))
                    if j or not isinstance(kk, int) or kk:
                        v.wait_ge(s_acc, n + j)
                    v.tensor_tensor(tile, tile, p_a[2 * (u % 2) + j // 2][:, (j % 2) * 2 * TN:(j % 2 + 1) * 2 * TN].rearrange("p (c n) -> p c n", c=KC),
                                    ALU.add).then_inc(s_acc, 1)

                def body(kk, u, i, has):
                    n = l * per + GRP * kk
                    grp = l * NG + kk
                    v.wait_ge(s_kv[u], gathered(l, i))
                    for j in range(GRP - 1):
                        v.wait_ge(s_qe, n + max(j + 1, 2))
                        v.tensor_tensor(prod[:, j, :].rearrange("p (h g d) -> p h g d", h=GH, g=GH),
                                        p_qt[j].rearrange("p (h o d) -> p h o d", h=GH, o=1).to_broadcast([P, GH, GH, GD]),
                                        kv[:, u, j, 0:D].rearrange("p (o g d) -> p o g d", o=1, g=GH).to_broadcast([P, GH, GH, GD]),
                                        ALU.mult).then_inc(s_pk, 1)
                    old, mod = kk - 2, (u - 2) % SL
                    bucket = buckets(v, old) if has(-2) else None
                    add = (lambda j: add_sum(old, mod, bucket, j)) if has(-2) else (lambda j: None)
                    steps = Steps(v, s_chain, 5 * grp)
                    v.wait_ge(s_pk, grp * (GRP - 1) + (GRP - 1))
                    v.wait_ge(s_pp, grp + 1)
                    steps.done(v.tensor_reduce(sc[:, :], prod[:, :, :].rearrange("p j (m d) -> p (j m) d", d=GD), AX.X, ALU.add))
                    add(0)
                    steps.wait()
                    scg = sc[:, :].rearrange("p (m g) -> p m g", g=GH)
                    steps.done(v.tensor_reduce(mx[:, :], scg, AX.X, ALU.max))
                    add(1)
                    steps.wait()
                    steps.done(v.tensor_tensor(scg, scg, mx[:, :].rearrange("p (m o) -> p m o", o=1).to_broadcast([P, GRP * GH, GH]), ALU.subtract))
                    add(2)
                    v.wait_ge(s_ex, grp + 1)
                    exg = ex[:, :].rearrange("p (m g) -> p m g", g=GH)
                    steps.done(v.tensor_reduce(sm[:, :], exg, AX.X, ALU.add))
                    add(3)
                    steps.wait()
                    steps.done(v.reciprocal(sm[:, :], sm[:, :]))
                    if has(2):
                        onehot(kk + 2, (u + 2) % SL)
                    steps.wait()
                    if has(-2):
                        v.wait_ge(s_wv, n - GRP)
                        v.wait_ge(s_wa, n - GRP)
                    v.tensor_tensor(attn[:, u % 2, :, :].rearrange("p j (g h) -> p j h g", g=GH),
                                    ex[:, :].rearrange("p (j h g) -> p j h g", j=GRP, h=GH),
                                    sm[:, :].rearrange("p (j h o) -> p j h o", j=GRP, o=1).to_broadcast([P, GRP, GH, GH]),
                                    ALU.mult).then_inc(s_attn, 1)
                    assert steps.n == 5

                onehot(0, 0)
                onehot(1, 1)
                edge_loop(v, body)
                for kk in (NG - 2, NG - 1):
                    bucket = buckets(v, kk)
                    for j in range(GRP):
                        add_sum(kk, kk % SL, bucket, j)

                def add_messages(t, slot):
                    v.wait_ge(s_o, node + t + 3)
                    tile = hid[:, bass.ds(t, 1), 0:D]
                    v.tensor_tensor(tile, tile, [p_t, p_o][slot][0:TN, 0:D].rearrange("p (o d) -> p o d", o=1), ALU.add).then_inc(s_hm, 1)
                paired(v, NT, add_messages)
                hold(v, s_vgo, s_hm, node + (NT + 2))
                c = Steps(v, s_dve, l * NORM_STEPS + 2)
                norm.moments(v, c, hid, 1e-5)
                assert c.n == NORM_STEPS, c.n
                with v.Fori(0, NT) as t:
                    norm.apply(v, hid[:, bass.ds(t, 1), 0:D], hid[:, bass.ds(t, 1), 0:D], t).then_inc(s_ap, 1)
                with v.Fori(0, NT) as t:
                    tile = hid[:, bass.ds(t, 1), 0:D]
                    v.wait_ge(s_pool, 2 * node + 2 * t + 2)
                    v.tensor_scalar(tile, tile, 0.0, None, ALU.max).then_inc(s_relu, 1)
                hold(v, s_vgo, s_relu, node + (NT + 1))


def gnn_out(nc, a, g, scr):
    with ExitStack() as ctx:
        k = Kit(nc, ctx)
        mlp = Mlp(k, "gm", KC, ACT.Relu)
        b2 = k.sb("gb2", [TN, D])
        s_b2 = k.sem("go_b2")
        s_put = k.sem("go_put")
        block = ctx.enter_context(nc.Block())

        @block.sync
        def _(sp):
            sp.dma_start(b2[:, :], row(a["g_b2"], TN)).then_inc(s_b2, 16)
            mlp.load(sp, a["g_w1"], a["g_w2"], a["g_b1"])

        @block.tensor
        def _(pe):
            mlp.on_pe(pe, g["ident"])

        @block.scalar
        def _(act):
            mlp.on_act(act)

        @block.vector
        def _(v):
            v.wait_ge(s_b2, 16)

            def put(t, slot, xin):
                return v.tensor_scalar(xin.rearrange("p (o d) -> p o d", o=1), g["xn"][:, bass.ds(t, 1), 0:D], 1.0, None, ALU.mult)

            def take(t, slot, y):
                tile = g["xacc"][:, bass.ds(t, 1), :]
                v.tensor_tensor(tile, tile, y.rearrange("p (o d) -> p o d", o=1), ALU.add).then_inc(s_put, 1)
                v.wait_ge(s_put, t + 1)
                return v.tensor_tensor(tile, tile, b2[:, :].rearrange("p (o d) -> p o d", o=1), ALU.add)
            mlp.on_dve(v, put, take)


def route(nc, a, g, scr):
    with ExitStack() as ctx:
        k = Kit(nc, ctx)
        xn, xn_t = g["xn"], g["xn_t"]
        norm = Norm(k, "fn")
        tin = k.sb("tin", [TN, 2, D])
        wr = k.sb("wr", [P, KC])
        wrr = k.sb("wrr", [P, KC, TN])
        br = k.sb("br", [TN, 1])
        one = k.sb("fone", [P, TN])
        wb = k.sb("wb", [TN, N_NODES])
        wc = k.sb("wc", [TN, NT])
        rank = k.sb("rank", [TN, 4, NT])
        cmp = k.sb("cmp", [TN, N_NODES], BF16)
        eqm = k.sb("eqm", [TN, TN])
        lower = k.sb("lower", [TN, TN])
        p_tr = [k.ps(f"f_tr{i}") for i in range(2)]
        p_w = [k.ps(f"f_w{i}") for i in range(2)]
        p_c = k.ps("f_c")
        s_const = k.sem("fw_const")
        s_dve = k.sem("fw_dve")
        s_wrr = k.sem("fw_wrr")
        s_in = k.sem("fw_in")
        s_tr = k.sem("fw_tr")
        s_xt = k.sem("fw_xt")
        s_pw = k.sem("fw_pw")
        s_wb = k.sem("fw_wb")
        s_wc = k.sem("fw_wc")
        s_go = k.sem("fw_go")
        block = ctx.enter_context(nc.Block())

        @block.sync
        def _(sp):
            sp.dma_start(wr[:, :], a["f_wr"]).then_inc(s_const, 16)
            sp.dma_start(br[:, :], row(a["f_br"], TN)).then_inc(s_const, 16)
            sp.dma_start(lower[:, :], a["c_lower"]).then_inc(s_const, 16)

        @block.tensor
        def _(pe):
            def step(t, slot):
                pe.wait_ge(s_in, t + 1)
                pe.wait_ge(s_xt, t + 1)
                for c in range(KC):
                    ins = pe.transpose(p_tr[slot][:, c * TN:(c + 1) * TN], tin[:, slot, c * P:(c + 1) * P], g["ident"][0:TN, 0:TN])
                ins.then_inc(s_tr, 1)
            paired(pe, NT, step)
            pe.wait_ge(s_xt, NT + 2)
            pe.wait_ge(s_wrr, 1)

            def weights(t, slot):
                pe.wait_ge(s_wb, t + 1)
                for c in range(KC):
                    ins = pe.matmul(p_w[slot][0:TN, 0:TN], wrr[:, c, :], xn_t[:, c, bass.ds(t * TN, TN)], start=c == 0, stop=c == KC - 1)
                ins.then_inc(s_pw, 1)
            paired(pe, NT, weights)
            pe.wait_ge(s_wb, NT + 2)
            for t in range(NT):
                ins = pe.transpose(p_c[0:TN, t:t + 1], wb[0:1, t * TN:(t + 1) * TN], g["ident"][0:1, 0:1])
            ins.then_inc(s_wc, 1)

        @block.scalar
        def _(act):
            act.sem_inc(s_xt, 2)

            def step(t, slot):
                act.wait_ge(s_tr, t + 1)
                act.copy(xn_t[:, :, bass.ds(t * TN, TN)], p_tr[slot][:, 0:KC * TN].rearrange("p (c n) -> p c n", c=KC)).then_inc(s_xt, 1)
            paired(act, NT, step)

        @block.gpsimd
        def _(pool):
            with pool.Fori(0, NT) as t:
                hold(pool, s_go, s_in, t + 1)
                tile = g["xacc"][:, bass.ds(t, 1), :]
                pool.tensor_tensor(tile, tile, xn[:, bass.ds(t, 1), 0:D], ALU.add)

        @block.vector
        def _(v):
            c = Steps(v, s_dve)
            v.wait_ge(s_const, 48)
            c.link(v.memset(one[:, :], 1.0))
            for kc in range(KC):
                ins = v.tensor_scalar(wrr[:, kc, :], one[:, :], wr[:, kc:kc + 1], None, ALU.mult)
            ins.then_inc(s_wrr, 1)
            norm.moments(v, c, g["xacc"], 1e-5)

            def normed(t, slot):
                v.wait_ge(s_xt, t + 1)
                norm.apply(v, xn[:, bass.ds(t, 1), 0:D], g["xacc"][:, bass.ds(t, 1), :], t)
                norm.apply(v, tin[:, slot:slot + 1, :], g["xacc"][:, bass.ds(t, 1), :], t).then_inc(s_in, 1)
            paired(v, NT, normed)
            v.sem_inc(s_wb, 2)

            def weights(t, slot):
                v.wait_ge(s_pw, t + 1)
                v.tensor_scalar(wb[:, bass.ds(t * TN, TN)], p_w[slot][0:TN, 0:TN], br[:, :], None, ALU.add).then_inc(s_wb, 1)
            paired(v, NT, weights)
            v.wait_ge(s_wb, NT + 2)
            v.wait_ge(s_wc, 1)
            c.link(v.tensor_copy(wc[:, :], p_c[0:TN, 0:NT]))
            c.link(v.memset(rank[:, :, :], 0.0))
            for t in range(NT):
                mine, lo, hi = wc[:, t:t + 1], t * TN, (t + 1) * TN
                if t:
                    c.link(v.tensor_scalar(cmp[:, 0:lo], wb[:, 0:lo], mine, None, ALU.is_ge, ALU.add, accum_out=rank[:, 0, t:t + 1]))
                c.link(v.tensor_scalar(cmp[:, lo:N_NODES], wb[:, lo:N_NODES], mine, None, ALU.is_gt, ALU.add, accum_out=rank[:, 1, t:t + 1]))
                c.link(v.scalar_tensor_tensor(out=eqm[:, :], in0=wb[:, lo:hi], scalar=mine, in1=lower[:, :], op0=ALU.is_equal, op1=ALU.mult))
                c.link(v.tensor_reduce(rank[:, 2, t:t + 1], eqm[:, :], AX.X, ALU.add))
            c.link(v.tensor_tensor(rank[:, 0, :], rank[:, 0, :], rank[:, 1, :], ALU.add))
            c.link(v.tensor_tensor(rank[:, 0, :], rank[:, 0, :], rank[:, 2, :], ALU.add))
            c.link(v.tensor_scalar(rank[:, 0, :], rank[:, 0, :], float(TOPK), None, ALU.is_lt))
            v.tensor_tensor(g["scale"][:, :], rank[:, 0, :], wc[:, :], ALU.mult)


def ffn(nc, a, g, scr, out):
    with ExitStack() as ctx:
        k = Kit(nc, ctx)
        mlp = Mlp(k, "fm", FF // P, ACT.Gelu_apprx_tanh)
        b2 = k.sb("fb2", [TN, D])
        res = k.sb("res", [TN, 2, D])
        s_b2 = k.sem("ff_b2")
        s_put = k.sem("ff_put")
        s_out = [k.sem(f"ff_out{i}") for i in range(2)]
        block = ctx.enter_context(nc.Block())
        out_t = out.rearrange("(t p) d -> p t d", p=TN)

        @block.sync
        def _(sp):
            sp.dma_start(b2[:, :], row(a["f_b2"], TN)).then_inc(s_b2, 16)
            mlp.load(sp, a["f_w1"], a["f_w2"], a["f_b1"])

            def store(t, slot):
                sp.wait_ge(mlp.s_take, t + 3)
                sp.dma_start(out_t[:, bass.ds(t, 1), :], res[:, slot:slot + 1, :]).then_inc(s_out[slot], 16)
            paired(sp, NT, store)
            sp.wait_ge(s_out[0], 16 * (NT - NT // 2))
            sp.wait_ge(s_out[1], 16 * (NT // 2))

        @block.tensor
        def _(pe):
            mlp.on_pe(pe, g["ident"])

        @block.scalar
        def _(act):
            mlp.on_act(act)

        @block.vector
        def _(v):
            v.wait_ge(s_b2, 16)

            def put(t, slot, xin):
                return v.tensor_scalar(xin.rearrange("p (o d) -> p o d", o=1), g["xn"][:, bass.ds(t, 1), 0:D], 1.0, None, ALU.mult)

            def take(t, slot, y):
                if not isinstance(t, int) or t >= 2:
                    v.wait_ge(s_out[slot], (t - slot) * 8)
                v.tensor_tensor(res[:, slot, :], y, b2[:, :], ALU.add).then_inc(s_put, 1)
                v.wait_ge(s_put, t + 1)
                return v.scalar_tensor_tensor(out=res[:, slot:slot + 1, :], in0=res[:, slot:slot + 1, :],
                                              scalar=g["scale"][:, bass.ds(t, 1)], in1=g["xacc"][:, bass.ds(t, 1), :],
                                              op0=ALU.mult, op1=ALU.add)
            mlp.on_dve(v, put, take)


def program(nc, a, out, stop=9):
    with ExitStack() as ctx:
        k = Kit(nc, ctx)
        scr = {
            "table": nc.dram_tensor("edge_table", [P * TCOLS, 1], I32).ap(),
            "counts": nc.dram_tensor("edge_counts", [NT * N_ET, TN], F32).ap(),
            "cpart": nc.dram_tensor("bias_parts", [2 * MH, PARTS * D], BF16).ap(),
            "kv": nc.dram_tensor("kv_rows", [N_NODES, 2 * D], F32).ap(),
        }
        g = {
            "xacc": k.sb("xacc", [TN, NT, D]),
            "ident": k.sb("ident", [P, P]),
            "ident_b": k.sb("ident_b", [P, P], BF16),
            "iota_n": k.sb("iota_n", [P, TN]),
            "tab": k.sb("tab", [1, ETILES // GRP], I32),
            "scale": k.sb("scale", [TN, NT]),
            "xn": k.sb("xn", [TN, NT, D + 1]),
            "xn_t": k.sb("xn_t", [P, KC, N_NODES]),
        }
        with ExitStack() as edges:
            k = Kit(nc, edges)
            g["scat_idx"] = k.sb("scat_idx", [P, EC], I32)
            g["record"] = k.sb("record", [P, EC], I32)
            prepare(nc, a, g, scr)
            if stop > 1:
                mix(nc, a, g, scr)
        if stop > 1:
            mix_out(nc, a, g, scr)
        if stop > 2:
            gnn(nc, a, g, scr)
            gnn_out(nc, a, g, scr)
        if stop > 3:
            route(nc, a, g, scr)
            ffn(nc, a, g, scr, out)


def layouts(inputs):
    import numpy as np

    f = {n: np.asarray(v) for n, v in inputs.items()}
    pad = N_PADDED - N_EDGES

    def edges(v, filler):
        return np.concatenate([v, np.full(pad, filler, v.dtype)]).reshape(P, EC)

    def lhs(w):
        w = w.reshape(w.shape[:-2] + (KC, P, w.shape[-1]))
        return np.moveaxis(w, -2, 0)

    wq, wk, wv = (f["L0_mix_" + n].transpose(1, 2, 0) for n in ("Wq", "Wk", "Wv"))
    flat = [f["L0_mix_" + n].reshape(D, HM) for n in ("Wq", "Wk")]
    bcols = [f["L0_mix_" + n].T for n in ("bq", "bk", "bv")]
    steps = [np.concatenate([lhs(wq[h]).reshape(P, -1), lhs(wk[h]).reshape(P, -1)], 1) for h in range(MH)]
    steps += [lhs(w[:, i:i + 2 * D]).reshape(P, -1) for w in flat for i in range(0, HM, 2 * D)]
    steps += [np.concatenate([lhs(wv[h]).reshape(P, -1), lhs(f["L0_mix_Wo"][h]).reshape(P, -1),
                              lhs(bcols[2][:, h:h + 1]).reshape(P, -1)], 1) for h in range(MH)]
    m_w = np.zeros((P, len(steps), 4 * D + KC), np.float32)
    for n, w in enumerate(steps):
        m_w[:, n, :w.shape[1]] = w
    sel = np.zeros((AUG, 2, HM), mybir.dt.np(BF16))
    for r in range(PARTS):
        for h in range(MH):
            sel[r * MH + h, :, h * D:(h + 1) * D] = 1
    def per_layer(w):
        return lhs(w).reshape(P, LAYERS, -1)

    G = {n: f["L0_gnn_" + n] for n in ("Win", "b_in", "Wq", "bq", "Wk", "bk", "Wv", "bv", "Eemb", "Wo", "bo",
                                       "ln_g", "ln_b", "W1", "b1", "W2", "b2")}
    tr = lambda w: np.swapaxes(w, -1, -2)
    gnn_in = {
        "g_win": lhs(tr(G["Win"])), "g_bin": G["b_in"],
        "g_wqkv": per_layer(np.concatenate([tr(G["Wk"]), tr(G["Wv"]), tr(G["Wq"])], -1)),
        "g_wo": per_layer(tr(G["Wo"])), "g_et": per_layer(tr(G["Eemb"])),
        "g_rows": np.concatenate([G["bk"], G["bv"], G["bq"], G["bo"], G["ln_g"], G["ln_b"]], 1),
        "g_w1": lhs(tr(G["W1"])), "g_w2": lhs(tr(G["W2"])), "g_b1": lhs(G["b1"][:, None])[:, :, 0], "g_b2": G["b2"],
        "f_wr": lhs(f["L0_ffn_wr"])[:, :, 0], "f_br": f["L0_ffn_br"], "f_w1": lhs(f["L0_ffn_w1"]),
        "f_w2": f["L0_ffn_w2"].reshape(FF // P, P, D).transpose(1, 0, 2),
        "f_b1": f["L0_ffn_b1"].reshape(FF // P, P).T, "f_b2": f["L0_ffn_b2"],
    }
    arr = {
        **gnn_in,
        "m_rows": np.concatenate([f["L0_mix_" + n] for n in ("g1", "beta1", "bias2", "g2", "beta2")]),
        "m_w1": lhs(f["L0_mix_W1"]), "m_w2": lhs(f["L0_mix_W2"]), "m_b1": lhs(f["L0_mix_bias1"][:, None])[:, :, 0],
        "c_lower": np.tril(np.ones((TN, TN), np.float32), -1),
        "m_w": m_w, "m_sel": sel, "m_bo": f["L0_mix_bo"],
        "m_pb": lhs(np.concatenate([f["L0_mix_proj"].T, bcols[0], bcols[1]], 1)),
        "x": f["x"],
        "src": edges(f["src"], N_NODES), "dst": edges(f["dst"], 0), "et": edges(f["edge_type_3"], 0),
        "c_ident": np.eye(P, dtype=np.float32),
        "c_tri": np.triu(np.ones((P, P), np.float32), 1),
        "c_iota_n": np.tile(np.arange(TN, dtype=np.float32), (P, 1)),
        "c_iota_e": np.tile(np.arange(TCOLS, dtype=np.float32), (P, 1)),
    }
    return {n: np.ascontiguousarray(v) for n, v in arr.items()}


def kernel(**inputs):
    import numpy as _np
    import concourse.bacc as _bacc
    from concourse import mybir as _mybir
    from concourse.bass_utils import run_bass_kernel_spmd as _run

    nc = _bacc.Bacc("TRN2", target_bir_lowering=False, num_devices=1)
    arrays = {"in_" + n: v for n, v in layouts(inputs).items()}
    aps = {n[3:]: nc.dram_tensor(n, v.shape, _mybir.dt.from_np(v.dtype), kind="ExternalInput").ap() for n, v in arrays.items()}
    out = nc.dram_tensor("out_0_dram", (N_NODES, D), _mybir.dt.float32, kind="ExternalOutput").ap()
    program(nc, aps, out)
    r = _run(nc, [arrays], core_ids=[0])
    return r.results[0]["out_0_dram"]
```

```python
from contextlib import ExitStack

import concourse.bass as bass
from concourse import mybir

F32 = mybir.dt.float32
I32 = mybir.dt.int32
BF16 = mybir.dt.bfloat16
ALU = mybir.AluOpType
ACT = mybir.ActivationFunctionType
AX = mybir.AxisListType

N_NODES = 3125
D = 256
P = 128
TN = 125
NT = N_NODES // TN
KC = D // P
N_EDGES = 50000
EC = 391
N_PADDED = P * EC
ET_MAX = (N_EDGES + NT * (P - 1)) // P
GRP = 4
ETILES = -(-ET_MAX // (2 * GRP)) * 2 * GRP
TRASH = ETILES * P
TCOLS = ETILES + -(-EC // P)
NODE_BITS = 12
EMPTY = 127 << NODE_BITS
N_ET = 3
LAYERS = 3
GH, GD = 4, 64
MH = 8
HM = MH * D
PARTS = 3
AUG = PARTS * (MH + 1)
MSCALE = 0.25
FF = 4 * D
TOPK = N_NODES // 2 - 1
WSTEPS = 2 * MH * D // (2 * D)
CNT_T = 23
CNT_G = EC // CNT_T


class Steps:

    def __init__(self, eng, sem, base=0):
        self.eng, self.sem, self.base, self.n = eng, sem, base, 0

    def done(self, ins):
        self.n += 1
        return ins.then_inc(self.sem, 1)

    def wait(self):
        self.eng.wait_ge(self.sem, self.base + self.n)

    def link(self, ins):
        self.done(ins)
        self.wait()


def paired(eng, n, step):
    with eng.Fori(0, n // 2) as i:
        step(2 * i, 0)
        step(2 * i + 1, 1)
    if n % 2:
        step(n - 1, 0)


def hold(eng, go, sem, value):
    eng.wait_ge(sem, value)
    eng.sem_inc(go, 1)


def row(ap, n):
    return ap.rearrange("(o d) -> o d", o=1).to_broadcast([n, ap.shape[0]])


def flipped(eng, n, first, step):
    with eng.Fori(0, n // 2) as i:
        step(2 * i, first)
        step(2 * i + 1, 1 - first)
    step(n - 1, first)


class Norm:

    def __init__(self, k, name):
        self.stats = k.sb(name + "_stats", [TN, NT, 6])
        self.mean = k.sb(name + "_mean", [TN, NT])
        self.rstd = k.sb(name + "_rstd", [TN, NT])
        self.var = k.sb(name + "_var", [TN, NT])
        self.tmp = k.sb(name + "_tmp", [TN, NT])
        self.bits = k.sb(name + "_bits", [TN, NT], I32)
        self.s_done = k.sem(name + "_done")

    def moments(self, v, c, x, eps):
        for t in range(NT):
            ins = v.bn_stats(self.stats[:, t, :], x[:, t, 0:D])
        c.link(ins)
        even, odd = self.stats[:, :, 1], self.stats[:, :, 4]
        var, tmp, y = self.var[:, :], self.tmp[:, :], self.rstd[:, :]
        c.done(v.tensor_tensor(self.mean[:, :], even, odd, ALU.add))
        c.done(v.tensor_tensor(tmp, even, odd, ALU.subtract))
        c.link(v.tensor_tensor(var, self.stats[:, :, 2], self.stats[:, :, 5], ALU.add))
        c.done(v.tensor_scalar(self.mean[:, :], self.mean[:, :], 0.5, None, ALU.mult))
        c.link(v.scalar_tensor_tensor(out=tmp, in0=tmp, scalar=D / 4.0, in1=tmp, op0=ALU.mult, op1=ALU.mult))
        c.link(v.tensor_tensor(var, var, tmp, ALU.add))
        c.link(v.tensor_scalar(var, var, 1.0 / D, eps, ALU.mult, ALU.add))
        c.link(v.tensor_scalar(self.bits[:, :], var.bitcast(I32), 1, None, ALU.logical_shift_right))
        c.link(v.tensor_scalar(y.bitcast(I32), self.bits[:, :], -1.0, float(0x5F3759DF), ALU.mult, ALU.add))
        c.link(v.tensor_scalar(var, var, -0.5, None, ALU.mult))
        for _ in range(4):
            c.wait()
            c.link(v.tensor_tensor(tmp, y, y, ALU.mult))
            c.link(v.tensor_tensor(tmp, tmp, var, ALU.mult))
            c.done(v.scalar_tensor_tensor(out=y, in0=tmp, scalar=1.5, in1=y, op0=ALU.add, op1=ALU.mult))
        hold(v, self.s_done, c.sem, c.base + c.n)

    def apply_all(self, v, x):
        for t in range(NT):
            ins = v.tensor_scalar(x[:, t, 0:D], x[:, t, 0:D], self.mean[:, t:t + 1], self.rstd[:, t:t + 1],
                                  ALU.subtract, ALU.mult)
        return ins

    def apply(self, v, out, x, t):
        return v.tensor_scalar(out, x, self.mean[:, bass.ds(t, 1)], self.rstd[:, bass.ds(t, 1)],
                               ALU.subtract, ALU.mult)


class Kit:

    def __init__(self, nc, ctx):
        self.nc, self.ctx = nc, ctx

    def sb(self, name, shape, dt=F32):
        return self.ctx.enter_context(self.nc.sbuf_tensor(name, shape, dt))

    def ps(self, name, shape=(P, 512), dt=F32):
        return self.ctx.enter_context(self.nc.psum_tensor(name, list(shape), dt))

    def sem(self, name):
        return self.ctx.enter_context(self.nc.semaphore(name))


def prepare(nc, a, g, scr):
    with ExitStack() as ctx:
        k = Kit(nc, ctx)
        src_i = k.sb("src_i", [P, EC], I32)
        dst_i = k.sb("dst_i", [P, EC], I32)
        et_i = k.sb("et_i", [P, EC], I32)
        src_f = k.sb("src_f", [P, EC])
        dst_f = k.sb("dst_f", [P, EC])
        et_f = k.sb("et_f", [P, EC])
        ge = k.sb("ge", [P, NT + 1, EC], BF16)
        boh = k.sb("boh", [P, NT, EC], BF16)
        eoh = k.sb("eoh", [P, N_ET, EC], BF16)
        run = k.sb("run", [P, NT * EC])
        runb = run[:, :].rearrange("p (b t) -> p b t", b=NT)
        local = k.sb("local", [P, EC])
        iota_e = k.sb("iota_e", [P, TCOLS])
        tri = k.sb("tri", [P, P])
        ones = k.sb("ones", [P, P])
        last = k.sb("last", [P, NT + 1])
        cnt = k.sb("cnt", [P, NT])
        cnt_i = k.sb("cnt_i", [P, NT], I32)
        tiles = k.sb("tiles", [P, NT])
        tend = k.sb("tend", [P, NT])
        off = k.sb("off", [P, NT])
        pos, pos_i, lo_i, hi_i = et_f, src_i, dst_i, et_i
        fill = k.sb("fill", [P, TCOLS], I32)
        bucket = k.sb("bucket", [1, ETILES])
        be = k.sb("be", [P, NT, N_ET, CNT_T], BF16)
        roh = k.sb("roh", [P, CNT_T, TN], BF16)
        counts = k.sb("counts", [NT * N_ET, TN])
        norm_x = Norm(k, "nx")
        stage = k.sb("stage", [TN, 2, D])
        wsq = k.sb("wsq", [P, 2, 4 * D])
        xs = k.sb("xs0", [P, 2, KC, TN])
        junk = k.sb("junk", [TN, 2, 2, D])
        p_tr = [k.ps(f"p_tr{i}") for i in range(2)]
        p_scan = k.ps("p_scan")
        p_cnt = k.ps("p_cnt")
        p_sq = [k.ps(f"p_sq{i}") for i in range(2)]

        s_x = k.sem("pr_x")
        s_const = k.sem("pr_const")
        s_edges = k.sem("pr_edges")
        s_dve = k.sem("pr_dve")
        s_xn = k.sem("pr_xn")
        s_tr = k.sem("pr_tr")
        s_xnt = k.sem("pr_xnt")
        s_c = k.sem("pr_c")
        s_off = k.sem("pr_off")
        s_oh = k.sem("pr_oh")
        s_ohu = k.sem("pr_ohu")
        s_cout = k.sem("pr_cout")
        s_fill = k.sem("pr_fill")
        s_out = k.sem("pr_out")
        s_ws = [k.sem(f"pr_ws{i}") for i in range(2)]
        s_xs = k.sem("pr_xs")
        s_q = k.sem("pr_q")
        s_qfree = k.sem("pr_qfree")
        s_go = k.sem("pr_go")
        block = ctx.enter_context(nc.Block())

        @block.sync
        def _(sp):
            sp.dma_start(g["xacc"][:, :, :], a["x"].rearrange("(t p) d -> p t d", p=TN)).then_inc(s_x, 16)
            sp.dma_start(src_i[:, :], a["src"]).then_inc(s_edges, 16)
            sp.dma_start(dst_i[:, :], a["dst"]).then_inc(s_edges, 16)
            sp.dma_start(et_i[:, :], a["et"]).then_inc(s_edges, 16)
            sp.dma_start(g["ident"][:, :], a["c_ident"]).then_inc(s_const, 16)
            sp.dma_start(tri[:, :], a["c_tri"]).then_inc(s_const, 16)
            sp.dma_start(g["iota_n"][:, :], a["c_iota_n"]).then_inc(s_const, 16)
            sp.dma_start(iota_e[:, :], a["c_iota_e"]).then_inc(s_const, 16)

            def load(w):
                sp.dma_start(wsq[:, w % 2, :], a["m_w"][:, 2 * MH + w, 0:4 * D]).then_inc(s_ws[w % 2], 16)
            load(0)
            load(1)
            sp.wait_ge(s_fill, 1)
            sp.dma_start(scr["table"].rearrange("(p c) o -> p (c o)", p=P), fill[:, :]).then_inc(s_out, 16)
            for w in range(2, WSTEPS):
                sp.wait_ge(s_q, 2 + NT * (w - 1))
                load(w)
            sp.wait_ge(s_cout, 1)
            sp.dma_start(scr["counts"], counts[:, :]).then_inc(s_out, 16)
            sp.wait_ge(s_out, 32)

        @block.scalar
        def _(act):
            act.sem_inc(s_xnt, 2)

            def step(t, slot):
                act.wait_ge(s_tr, t + 1)
                act.copy(g["xn_t"][:, :, bass.ds(t * TN, TN)],
                         p_tr[slot][:, 0:KC * TN].rearrange("p (c n) -> p c n", c=KC)).then_inc(s_xnt, 1)
            paired(act, NT, step)
            act.sem_inc(s_qfree, 2)
            with act.Fori(0, WSTEPS // 2) as wp2:
                for wslot in range(2):
                    w = wp2 * 2 + wslot

                    def square(t, slot):
                        n = w * NT + t
                        act.wait_ge(s_q, n + 3)
                        act.wait_ge(s_qfree, n + 1)
                        for j in range(2):
                            ins = act.activation(junk[:, slot, j, :], p_sq[slot][0:TN, j * D:(j + 1) * D], ACT.Square,
                                                 accum_out=g["sq"][:, bass.ds(t * (2 * MH) + 2 * w + j, 1)])
                        ins.then_inc(s_qfree, 1)
                    flipped(act, NT, wslot, square)

        @block.tensor
        def _(pe):
            pe.wait_ge(s_const, 64)

            def step(t, slot):
                pe.wait_ge(s_xn, t + 1)
                pe.wait_ge(s_xnt, t + 1)
                for c in range(KC):
                    ins = pe.transpose(p_tr[slot][:, c * TN:(c + 1) * TN],
                                       stage[:, slot, c * P:(c + 1) * P], g["ident"][0:TN, 0:TN])
                ins.then_inc(s_tr, 1)
            paired(pe, NT, step)
            pe.sem_inc(s_q, 2)
            pe.sem_inc(s_ohu, 1)

            def square(w, t, slot):
                n = t + w * NT
                pe.wait_ge(s_xs, n + 1)
                pe.wait_ge(s_qfree, n + 1)
                for c in range(KC):
                    ins = pe.matmul(p_sq[slot][0:TN, :], xs[:, slot, c, :], wsq[:, w % 2, c * 2 * D:(c + 1) * 2 * D],
                                    start=c == 0, stop=c == KC - 1)
                ins.then_inc(s_q, 1)

            def count(i):
                pe.wait_ge(s_oh, i + 1)
                for j in range(CNT_T):
                    ins = pe.matmul(p_cnt[0:NT * N_ET, 0:TN], be[:, :, :, j].rearrange("p b e -> p (b e)"),
                                    roh[:, j, :], start=False, stop=False, skip_group_check=True)
                ins.then_inc(s_ohu, 1)

            def squares(w, counts=range(0)):
                pe.wait_ge(s_ws[w % 2], 16 * (w // 2 + 1))
                if counts:
                    with pe.Fori(0, len(counts)) as i:
                        count(i + counts[0])
                        for q in range(4):
                            square(w, 4 * i + q, (w + q) % 2)
                if 4 * len(counts) < NT - 1:
                    with pe.Fori(2 * len(counts), NT // 2) as i:
                        square(w, 2 * i, w % 2)
                        square(w, 2 * i + 1, (w + 1) % 2)
                square(w, NT - 1, w % 2)
            squares(0)
            pe.wait_ge(s_c, 1)
            pe.matmul(p_scan[:, 0:NT], tri[:, :], cnt[:, :], start=True, stop=True)
            pe.matmul(p_scan[:, NT:2 * NT], ones[:, :], cnt[:, :], start=True, stop=True).then_inc(s_off, 1)
            squares(1)
            counted, most = 0, NT // 4
            for w in range(2, WSTEPS):
                now = min(most, CNT_G - counted)
                squares(w, range(counted, counted + now))
                counted += now
            assert counted == CNT_G

        @block.gpsimd
        def _(pool):
            pool.memset(fill[:, :], EMPTY).then_inc(s_fill, 1)
            pool.wait_ge(s_xnt, NT + 2)
            with pool.Fori(0, WSTEPS // 2) as wp2:
                for wslot in range(2):
                    def stage_square(t, slot):
                        hold(pool, s_go, s_q, (wp2 * 2 + wslot) * NT + t + 1)
                        pool.tensor_copy(xs[:, slot, :, :], g["xn_t"][:, :, bass.ds(t * TN, TN)]).then_inc(s_xs, 1)
                    flipped(pool, NT, wslot, stage_square)

        @block.vector
        def _(v):
            c = Steps(v, s_dve)
            v.memset(ones[:, :], 1.0)
            v.memset(last[:, 0:1], 0.0)
            v.memset(g["xn"][:, :, D:D + 1], 1.0)
            v.wait_ge(s_x, 16)
            norm_x.moments(v, c, g["xacc"], 1e-5)

            def norm(t, slot):
                v.wait_ge(s_xnt, t + 1)
                norm_x.apply(v, g["xn"][:, bass.ds(t, 1), 0:D], g["xacc"][:, bass.ds(t, 1), :], t)
                norm_x.apply(v, stage[:, slot, :], g["xacc"][:, bass.ds(t, 1), :], t).then_inc(s_xn, 1)
            paired(v, NT, norm)
            v.wait_ge(s_edges, 48)
            v.wait_ge(s_const, 64)
            v.tensor_copy(g["ident_b"][:, :], g["ident"][:, :])
            c.done(v.tensor_copy(src_f[:, :], src_i[:, :]))
            c.done(v.tensor_copy(dst_f[:, :], dst_i[:, :]))
            c.link(v.tensor_copy(et_f[:, :], et_i[:, :]))
            for b in range(NT + 1):
                c.done(v.tensor_scalar(ge[:, b, :], src_f[:, :], float(TN * b), None, ALU.is_ge))
            for e in range(N_ET):
                c.done(v.tensor_scalar(eoh[:, e, :], et_f[:, :], float(e), None, ALU.is_equal))
            c.wait()
            c.done(v.tensor_tensor(boh[:, :, :], ge[:, 0:NT, :], ge[:, 1:NT + 1, :], ALU.subtract))
            c.link(v.tensor_reduce(local[:, :], ge[:, 1:NT, :].rearrange("p b t -> p t b"), AX.X, ALU.add))
            c.done(v.scalar_tensor_tensor(out=local[:, :], in0=local[:, :], scalar=-float(TN), in1=src_f[:, :],
                                          op0=ALU.mult, op1=ALU.add))
            flat = boh[:, :, :].rearrange("p b t -> p (b t)")
            c.link(v.tensor_tensor_scan(run[:, :], flat, flat, 0.0, ALU.add, ALU.max))
            c.link(v.tensor_copy(last[:, 1:NT + 1], runb[:, :, EC - 1]))
            c.link(v.tensor_tensor(cnt[:, :], last[:, 1:NT + 1], last[:, 0:NT], ALU.subtract))
            v.nop().then_inc(s_c, 1)
            v.wait_ge(s_off, 1)
            c.link(v.tensor_scalar(cnt_i[:, :], p_scan[:, NT:2 * NT], float(P - 1), None, ALU.add))
            c.link(v.tensor_scalar(cnt_i[:, :], cnt_i[:, :], 7, None, ALU.logical_shift_right))
            c.link(v.tensor_copy(tiles[:, :], cnt_i[:, :]))
            c.link(v.tensor_tensor_scan(tend[:, :], tiles[:, :], tiles[:, :], 0.0, ALU.add, ALU.max))
            c.link(v.tensor_tensor(off[:, :], tend[:, :], tiles[:, :], ALU.subtract))
            c.link(v.tensor_scalar(off[:, :], off[:, :], float(P), -1.0, ALU.mult, ALU.add))
            c.link(v.tensor_tensor(off[:, :], off[:, :], p_scan[:, 0:NT], ALU.add))
            c.link(v.tensor_tensor(off[:, :], off[:, :], last[:, 0:NT], ALU.subtract))
            c.link(v.tensor_tensor(runb, runb, off[:, :].rearrange("p (b o) -> p b o", o=1).to_broadcast([P, NT, EC]), ALU.add))
            c.link(v.tensor_tensor(runb, runb, boh[:, :, :], ALU.mult))
            c.link(v.tensor_reduce(pos[:, :], runb.rearrange("p b t -> p t b"), AX.X, ALU.add))
            c.link(v.scalar_tensor_tensor(out=src_f[:, :], in0=iota_e[:, 0:EC], scalar=float(TRASH), in1=ge[:, NT, :],
                                          op0=ALU.add, op1=ALU.mult))
            c.link(v.tensor_tensor(pos_i[:, :], pos[:, :], src_f[:, :], ALU.add))
            c.done(v.tensor_scalar(lo_i[:, :], pos_i[:, :], P - 1, None, ALU.bitwise_and))
            c.link(v.tensor_scalar(hi_i[:, :], pos_i[:, :], 7, None, ALU.logical_shift_right))
            c.done(v.scalar_tensor_tensor(out=g["scat_idx"][:, :], in0=lo_i[:, :], scalar=float(TCOLS), in1=hi_i[:, :],
                                          op0=ALU.mult, op1=ALU.add))
            c.done(v.scalar_tensor_tensor(out=g["record"][:, :], in0=local[:, :], scalar=float(1 << NODE_BITS),
                                          in1=dst_f[:, :], op0=ALU.mult, op1=ALU.add))
            cmp = run[0:1, 0:ETILES * NT // 2].rearrange("p (j b) -> p j b", b=NT)
            half = ETILES // 2
            for h in range(2):
                c.link(v.tensor_tensor(cmp, iota_e[0:1, h * half:(h + 1) * half].rearrange("p (j o) -> p j o", o=1).to_broadcast([1, half, NT]),
                                       tend[0:1, :].rearrange("p (o b) -> p o b", o=1).to_broadcast([1, half, NT]), ALU.is_ge))
                c.link(v.tensor_reduce(bucket[0:1, h * half:(h + 1) * half], cmp, AX.X, ALU.add))
            c.link(v.tensor_scalar(bucket[:, :], bucket[:, :], float(NT - 1), None, ALU.min))
            b4 = bucket[:, :].rearrange("p (g j) -> p g j", j=GRP)
            for j in range(1, GRP):
                c.link(v.scalar_tensor_tensor(out=b4[:, :, 0] if j < GRP - 1 else g["tab"][:, :], in0=b4[:, :, j],
                                              scalar=float(32 ** j), in1=b4[:, :, 0], op0=ALU.mult, op1=ALU.add))
            c.link(v.memset(p_cnt[:, :], 0.0))
            with v.Fori(0, CNT_G) as i:
                v.wait_ge(s_ohu, i + 1)
                cols = bass.ds(i * CNT_T, CNT_T)
                v.tensor_tensor(be[:, :, :, :],
                                boh[:, :, cols].rearrange("p (b o) t -> p b o t", o=1).to_broadcast([P, NT, N_ET, CNT_T]),
                                eoh[:, :, cols].rearrange("p (o e) t -> p o e t", o=1).to_broadcast([P, NT, N_ET, CNT_T]),
                                ALU.mult)
                v.tensor_tensor(roh[:, :, :],
                                local[:, cols].rearrange("p (t o) -> p t o", o=1).to_broadcast([P, CNT_T, TN]),
                                g["iota_n"][:, :].rearrange("p (o n) -> p o n", o=1).to_broadcast([P, CNT_T, TN]),
                                ALU.is_equal).then_inc(s_oh, 1)
            v.wait_ge(s_ohu, CNT_G + 1)
            v.tensor_copy(counts[:, :], p_cnt[0:NT * N_ET, 0:TN]).then_inc(s_cout, 1)


def mix(nc, a, g, scr):
    with ExitStack() as ctx:
        k = Kit(nc, ctx)
        NB = 2 * MH
        NW = HM // (2 * D)
        WCOLS = 4 * D + KC
        wring = k.sb("wring", [P, 2, WCOLS])
        pb = k.sb("pb", [P, KC, D + NB])
        bsq = k.sb("bsq", [P, KC, NB])
        ones = k.sb("mones", [P, P])
        eones = k.sb("eones", [P, P])
        wp = k.sb("wp", [P, 2, KC, HM])
        w2 = k.sb("w2", [P, KC, NB])
        crow = k.sb("crow", [NB, D])
        cpart = k.sb("cpart", [NB, PARTS, D], BF16)
        augw = k.sb("augw", [AUG, 2, HM], BF16)
        augx = k.sb("augx", [AUG, 2, N_NODES], BF16)
        c0 = k.sb("c0", [TN, NB])
        sqp = k.sb("sqp", [TN, NT * NB])
        s54 = k.sb("s54", [TN, NT, 2 * AUG], BF16)
        s54s = k.sb("s54s", [TN, 2, 2 * AUG], BF16)
        xs = k.sb("xs", [P, 2, KC, TN])
        augs = k.sb("augs", [AUG, 2, TN], BF16)
        ek = k.sb("ek", [TN, 2, 2 * D])
        csum = k.sb("csum", [P, D + 1])
        gs = k.sb("gs", [P, 4, D + 1])
        gt = k.sb("gt", [P, KC, D])
        kst = k.sb("kst", [1, D])
        wvo = k.sb("wvo", [P, KC, D])
        bvo = k.sb("bvo", [1, D])
        kvs = k.sb("kvs", [P, MH, KC, D + 1])
        eq = k.sb("eq", [P, 4, 4, TN])
        rz = k.sb("rz", [TN, MH])
        acc = k.sb("acc", [TN, 2, D])
        bo = k.sb("bo", [TN, D])
        sidx = k.sb("sidx", [P, 2, CNT_G], I32)
        srec = k.sb("srec", [P, 2, CNT_G], I32)
        p_u = [k.ps(f"p_u{i}") for i in range(2)]
        p_g = [k.ps(f"p_g{i}") for i in range(4)]
        p_s = [k.ps(f"p_s{i}") for i in range(2)]

        s_const = k.sem("mx_const")
        s_ones = k.sem("mx_ones")
        s_bsq = k.sem("mx_bsq")
        s_w = [k.sem(f"mx_w{i}") for i in range(2)]
        s_dve = k.sem("mx_dve")
        s_crow = k.sem("mx_crow")
        s_cpart = k.sem("mx_cpart")
        s_cdram = k.sem("mx_cdram")
        s_caug = k.sem("mx_caug")
        s_fold = k.sem("mx_fold")
        s_folded = k.sem("mx_folded")
        s_cs = k.sem("mx_cs")
        s_zero = k.sem("mx_zero")
        s_xs = k.sem("mx_xs")
        s_cross = k.sem("mx_cross")
        s_xacc = k.sem("mx_xacc")
        s_s54 = k.sem("mx_s54")
        s_st = k.sem("mx_st")
        s_aug = k.sem("mx_aug")
        s_u = k.sem("mx_u")
        s_e = k.sem("mx_e")
        s_efree = k.sem("mx_efree")
        s_gs = k.sem("mx_gs")
        s_vo = k.sem("mx_vo")
        s_voc = k.sem("mx_voc")
        s_kdiag = k.sem("mx_kdiag")
        s_gt = k.sem("mx_gt")
        s_gtc = k.sem("mx_gtc")
        s_kv = k.sem("mx_kv")
        s_kvs = k.sem("mx_kvs")
        s_uq = k.sem("mx_uq")
        s_eq = k.sem("mx_eq")
        s_eps = k.sem("mx_eps")
        s_n = k.sem("mx_n")
        s_rz = k.sem("mx_rz")
        s_nfree = k.sem("mx_nfree")
        s_y = k.sem("mx_y")
        s_step = k.sem("mx_step")
        s_idx = k.sem("mx_idx")
        s_scat = [k.sem(f"mx_scat{i}") for i in range(2)]
        block = ctx.enter_context(nc.Block())
        KEY0 = NT

        @block.sync
        def _(sp):
            sp.dma_start(pb[:, :, :], a["m_pb"]).then_inc(s_const, 16)
            sp.dma_start(augw[:, :, :], a["m_sel"]).then_inc(s_const, 16)
            sp.dma_start(bo[:, :], row(a["m_bo"], TN)).then_inc(s_const, 16)

            def load(n, slot):
                sp.dma_start(wring[:, slot:slot + 1, :], a["m_w"][:, bass.ds(n, 1), :]).then_inc(s_w[slot], 16)
            for n in range(2):
                load(n, n)
            sp.wait_ge(s_cpart, 1)
            sp.dma_start(scr["cpart"].rearrange("h (r m) -> h r m", r=PARTS), cpart[:, :, :]).then_inc(s_cdram, 16)
            sp.wait_ge(s_cdram, 16)
            sp.wait_ge(s_const, 48)
            for i in range(2):
                sp.dma_start(augw[PARTS * MH:AUG, i, :].rearrange("r (h m) -> r h m", h=MH),
                             scr["cpart"][i * MH:(i + 1) * MH, :].rearrange("h (r m) -> r h m", r=PARTS)).then_inc(s_caug, 16)
            for n in range(2, MH + 2):
                sp.wait_ge(s_fold, n - 1)
                load(n, n % 2)
            for h in range(2, MH):
                sp.wait_ge(s_vo, h - 1)
                load(MH + h, h % 2)

        @block.gpsimd
        def _(pool):
            pool.memset(ones[:, :], 1.0).then_inc(s_ones, 1)
            pool.memset(eones[:, :], 16e-6).then_inc(s_ones, 1)
            pool.sem_inc(s_y, 2)

            def scatter(n, slot):
                if not isinstance(n, int) or n >= 2:
                    pool.wait_ge(s_scat[slot], (n - slot) * 8 * (EC // CNT_T))
                cols = bass.ds(n * CNT_G, CNT_G)
                pool.tensor_copy(sidx[:, slot, :], g["scat_idx"][:, cols]).then_inc(s_idx, 1)
                pool.tensor_copy(srec[:, slot, :], g["record"][:, cols]).then_inc(s_idx, 1)
                hold(pool, s_step, s_idx, 2 * n + 2)
                for j in range(CNT_G):
                    pool.indirect_dma_start(out=scr["table"], out_offset=bass.IndirectOffsetOnAxis(ap=sidx[:, slot, j:j + 1], axis=0),
                                            in_=srec[:, slot, j:j + 1], in_offset=None).then_inc(s_scat[slot], 16)
            scatter(0, 0)
            scatter(1, 1)
            with pool.Fori(1, CNT_T // 2) as i:
                scatter(2 * i, 0)
                scatter(2 * i + 1, 1)
            scatter(CNT_T - 1, 0)
            pool.tensor_tensor(g["xacc"][:, :, :], g["xacc"][:, :, :], g["xn"][:, :, 0:D], ALU.add).then_inc(s_xacc, 1)
            pool.wait_ge(s_xacc, 1)
            pool.wait_ge(s_const, 48)
            pool.wait_ge(s_kvs, MH + 1)

            def output(t, slot):
                pool.wait_ge(s_nfree, 8 * t + 10)
                pool.tensor_tensor(acc[:, slot, :], acc[:, slot, :], bo[:, :], ALU.add).then_inc(s_idx, 1)
                hold(pool, s_step, s_idx, 2 * CNT_T + t + 1)
                pool.tensor_tensor(g["xn"][:, bass.ds(t, 1), 0:D], g["xn"][:, bass.ds(t, 1), 0:D],
                                   acc[:, slot:slot + 1, :], ALU.add).then_inc(s_y, 1)
            paired(pool, NT, output)
            pool.wait_ge(s_scat[0], 16 * CNT_G * (CNT_T - CNT_T // 2))
            pool.wait_ge(s_scat[1], 16 * CNT_G * (CNT_T // 2))

        @block.tensor
        def _(pe):
            pe.wait_ge(s_const, 48)
            pe.wait_ge(s_ones, 2)
            for c in range(KC):
                pe.matmul(p_s[0][0:NB, 0:D], pb[:, c, D:D + NB], pb[:, c, 0:D], start=c == 0, stop=c == 1)
            pe.wait_ge(s_bsq, 1)
            for c in range(KC):
                ins = pe.matmul(p_s[1][0:TN, 0:NB], ones[:, 0:TN], bsq[:, c, :], start=c == 0, stop=c == 1)
            ins.then_inc(s_crow, 1)

            def fold(h, slot):
                pe.wait_ge(s_w[slot], 8 * (h - slot) + 16)
                pe.wait_ge(s_folded, 2 * h + 2)
                w = wring[:, slot, 0:4 * D].rearrange("p (i c d) -> p i c d", i=2, c=KC)
                for i in range(2):
                    for dc in range(KC):
                        for c in range(KC):
                            ins = pe.matmul(p_g[2 * i + dc][:, 0:D + NB], w[:, i, c, dc * P:(dc + 1) * P], pb[:, c, :],
                                            start=c == 0, stop=c == KC - 1)
                ins.then_inc(s_fold, 1)
            paired(pe, MH, fold)

            pe.wait_ge(s_cs, 1)
            with pe.Fori(0, NT) as t:
                pe.matmul(p_s[0][:, 0:D + 1], eones[0:TN, :], g["xn"][:, bass.ds(t, 1), :], start=False, stop=False,
                          skip_group_check=True).then_inc(s_cs, 1)

            pe.wait_ge(s_folded, 2 * MH + 2)
            pe.wait_ge(s_zero, 1)
            pe.sem_inc(s_cross, 2)

            def cross(t, slot):
                pe.wait_ge(s_xs, t + 1)
                for c in range(KC):
                    ins = pe.matmul(p_s[1][0:TN, bass.ds(t * NB, NB)], xs[:, slot, c, :], w2[:, c, :],
                                    start=False, stop=False, skip_group_check=True)
                ins.then_inc(s_cross, 1)
            paired(pe, NT, cross)

            pe.sem_inc(s_st, 2)

            def spread(t, slot):
                pe.wait_ge(s_s54, t + 1)
                pe.wait_ge(s_aug, t + 1)
                for i in range(2):
                    ins = pe.transpose(p_u[slot][:, :].bitcast(BF16)[0:AUG, i * P:i * P + TN],
                                       s54s[:, slot, i * AUG:(i + 1) * AUG], g["ident_b"][0:TN, 0:TN])
                ins.then_inc(s_st, 1)
            paired(pe, NT, spread)
            pe.wait_ge(s_aug, NT + 2)
            pe.wait_ge(s_caug, 32)
            pe.sem_inc(s_u, 2)
            pe.sem_inc(s_efree, 2)
            pe.sem_inc(s_gt, 1)

            with pe.Fori(0, NW // 2) as hq:
                for odd in range(2):
                    hp = hq * 2 + odd
                    first = (1 + odd) % 2
                    pe.wait_ge(s_zero, hp + 1)

                    def keys(t, slot):
                        n = hp * NT + t
                        pe.wait_ge(s_xs, n + (KEY0 + 1))
                        pe.wait_ge(s_efree, n + 1)
                        cols = bass.ds(hp * 2 * D, 2 * D)
                        for c in range(KC):
                            pe.matmul(p_u[slot][0:TN, :], xs[:, slot, c, :], wp[:, 1, c, cols], start=c == 0, stop=False)
                        pe.matmul(p_u[slot][0:TN, :], augs[:, slot, :], augw[:, 1, cols], start=False, stop=True).then_inc(s_u, 1)

                    def accumulate(t, slot):
                        pe.wait_ge(s_e, hp * NT + t + 1)
                        for m in range(4):
                            ins = pe.matmul(p_g[m][:, 0:D + 1], ek[:, slot, m * P:(m + 1) * P],
                                            g["xn"][:, bass.ds(t, 1), :], start=False, stop=False, skip_group_check=True)
                        ins.then_inc(s_efree, 1)

                    keys(0, first)
                    with pe.Fori(0, NT // 2) as i:
                        keys(2 * i + 1, 1 - first)
                        accumulate(2 * i, first)
                        keys(2 * i + 2, first)
                        accumulate(2 * i + 1, 1 - first)
                    accumulate(NT - 1, first)
                    for j in range(2):
                        h = hp * 2 + j
                        w = wring[:, j, 0:4 * D].rearrange("p (i c d) -> p i c d", i=2, c=KC)
                        pe.wait_ge(s_w[j], 16 * hp + 8 * MH + 16)
                        pe.wait_ge(s_kvs, h + 1)
                        for dc in range(KC):
                            for c in range(KC):
                                pe.matmul(p_s[0][:, dc * D:(dc + 1) * D], w[:, 0, c, dc * P:(dc + 1) * P], w[:, 1, c, :],
                                          start=c == 0, stop=c == KC - 1)
                        for c in range(KC):
                            ins = pe.matmul(p_s[1][0:1, 0:D], wring[:, j, 4 * D + c:4 * D + c + 1], w[:, 1, c, :],
                                            start=c == 0, stop=c == KC - 1)
                        ins.then_inc(s_vo, 1)
                        pe.wait_ge(s_gs, hp + 1)
                        for mc in range(KC):
                            for dc in range(KC):
                                pe.transpose(p_u[0][:, dc * D + mc * P:dc * D + (mc + 1) * P],
                                             gs[:, 2 * j + mc, dc * P:(dc + 1) * P], g["ident"][:, :])
                            ins = pe.transpose(p_u[1][0:1, mc * P:(mc + 1) * P], gs[:, 2 * j + mc, D:D + 1], g["ident"][:, :])
                        ins.then_inc(s_gt, 1)
                        pe.wait_ge(s_voc, h + 1)
                        pe.wait_ge(s_gtc, h + 1)
                        for mc in range(KC):
                            for dc in range(KC):
                                pe.matmul(p_s[0][:, mc * D:(mc + 1) * D], gt[:, dc, mc * P:(mc + 1) * P], wvo[:, dc, :],
                                          start=dc == 0, stop=False)
                            ins = pe.matmul(p_s[0][:, mc * D:(mc + 1) * D], kst[:, mc * P:(mc + 1) * P], bvo[:, :],
                                            start=False, stop=True)
                        ins.then_inc(s_kv, 1)
            pe.wait_ge(s_kvs, MH + 1)
            pe.sem_inc(s_n, MH)

            def features(t, q):
                tile = bass.ds(t * TN, TN)
                pe.wait_ge(s_eq, 4 * t + (q + 1))
                for m in range(4):
                    f = slice((4 * q + m) * P, (4 * q + m + 1) * P)
                    out = p_g[q % 2][:, m * TN:(m + 1) * TN]
                    for c in range(KC):
                        pe.matmul(out, wp[:, 0, c, f], g["xn_t"][:, c, tile], start=c == 0, stop=False)
                    ins = pe.matmul(out, augw[:, 0, f], augx[:, 0, tile], start=False, stop=True)
                ins.then_inc(s_uq, 1)

            def heads(t, q):
                pe.wait_ge(s_eps, 4 * t + (q + 1))
                for j in range(2):
                    h = 2 * q + j
                    pe.wait_ge(s_nfree, 8 * t + (h + 1))
                    for mc in range(KC):
                        ins = pe.matmul(p_u[j][0:TN, 0:D + 1], eq[:, q, 2 * j + mc, :], kvs[:, h, mc, :],
                                        start=mc == 0, stop=mc == KC - 1)
                    ins.then_inc(s_n, 1)

            def queries(t, last):
                features(t, 1)
                heads(t, 0)
                features(t, 2)
                heads(t, 1)
                features(t, 3)
                heads(t, 2)
                if not last:
                    features(t + 1, 0)
                heads(t, 3)
            features(0, 0)
            with pe.Fori(0, NT - 1) as t:
                queries(t, False)
            queries(NT - 1, True)

        @block.scalar
        def _(act):
            act.sem_inc(s_folded, 1)
            act.sem_inc(s_kvs, 1)

            def folded(h, slot):
                act.wait_ge(s_fold, h + 1)
                for dc in range(KC):
                    act.activation(wp[:, 1, dc, bass.ds(h * D, D)], p_g[2 + dc][:, 0:D], ACT.Copy, scale=MSCALE)
                act.copy(w2[:, 0, bass.ds(h + MH, 1)], p_g[2][:, bass.ds(h + (D + MH), 1)])
                act.copy(w2[:, 1, bass.ds(h + MH, 1)], p_g[3][:, bass.ds(h + (D + MH), 1)]).then_inc(s_folded, 1)
            paired(act, MH, folded)
            act.sem_inc(s_aug, 2)

            def spread(t, slot):
                act.wait_ge(s_st, t + 3)
                act.copy(augx[:, :, bass.ds(t * TN, TN)],
                         p_u[slot][:, :].bitcast(BF16)[0:AUG, 0:2 * P].rearrange("p (i n) -> p i n", i=2)[:, :, 0:TN]).then_inc(s_aug, 1)
            paired(act, NT, spread)

            with act.Fori(0, NW // 2) as hq:
                for odd in range(2):
                    hp = hq * 2 + odd

                    def keys(t, slot):
                        n = hp * NT + t
                        act.wait_ge(s_u, n + 3)
                        act.wait_ge(s_efree, n + 1)
                        act.activation(ek[:, slot, :], p_u[slot][0:TN, :], ACT.Exp).then_inc(s_e, 1)
                    flipped(act, NT, (1 + odd) % 2, keys)
                    for j in range(2):
                        h = hp * 2 + j
                        act.wait_ge(s_vo, h + 1)
                        act.copy(wvo[:, :, :], p_s[0][:, :].rearrange("p (c d) -> p c d", c=KC))
                        act.copy(bvo[:, :], p_s[1][0:1, 0:D]).then_inc(s_voc, 1)
                        act.wait_ge(s_kv, h + 1)
                        act.copy(kvs[:, bass.ds(h, 1), :, 0:D],
                                 p_s[0][:, :].rearrange("p (o c d) -> p o c d", o=1, c=KC)).then_inc(s_kvs, 1)
            act.sem_inc(s_eq, 2)

            with act.Fori(0, NT) as t:
                for q in range(4):
                    act.wait_ge(s_uq, 4 * t + (q + 1))
                    act.wait_ge(s_n, 8 * t + (2 * q + 2))
                    act.activation(eq[:, q, :, :], p_g[q % 2][:, 0:4 * TN].rearrange("p (m n) -> p m n", m=4),
                                   ACT.Exp).then_inc(s_eq, 1)

        @block.vector
        def _(v):
            c = Steps(v, s_dve)
            v.wait_ge(s_const, 48)
            v.tensor_tensor(bsq[:, :, :], pb[:, :, D:D + NB], pb[:, :, D:D + NB], ALU.mult).then_inc(s_bsq, 1)
            v.wait_ge(s_crow, 1)
            c.done(v.tensor_copy(c0[:, :], p_s[1][0:TN, 0:NB]))
            c.link(v.tensor_scalar(crow[:, :], p_s[0][0:NB, 0:D], MSCALE, None, ALU.mult))
            for r in range(PARTS):
                c.link(v.tensor_copy(cpart[:, r, :], crow[:, :]))
                if r < PARTS - 1:
                    c.link(v.tensor_tensor(crow[:, :], crow[:, :], cpart[:, r, :], ALU.subtract))
            v.sem_inc(s_cpart, 1)
            v.memset(p_s[0][:, :], 0.0).then_inc(s_cs, 1)
            c.done(v.memset(s54[:, :, :], 1.0))
            v.sem_inc(s_folded, 1)

            def folded(h, slot):
                v.wait_ge(s_fold, h + 1)
                for dc in range(KC):
                    v.tensor_scalar(wp[:, 0, dc, bass.ds(h * D, D)], p_g[dc][:, 0:D], MSCALE, None, ALU.mult)
                v.tensor_copy(w2[:, 0, bass.ds(h, 1)], p_g[0][:, bass.ds(h + D, 1)])
                v.tensor_copy(w2[:, 1, bass.ds(h, 1)], p_g[1][:, bass.ds(h + D, 1)]).then_inc(s_folded, 1)
            paired(v, MH, folded)
            v.wait_ge(s_cs, NT + 1)
            c.link(v.tensor_copy(csum[:, :], p_s[0][:, 0:D + 1]))
            v.wait_ge(s_folded, 2 * MH + 2)
            for b in p_g:
                v.memset(b[:, :], 0.0)
            v.memset(p_s[1][:, :], 0.0).then_inc(s_zero, 1)

            def stage(t, slot):
                return v.tensor_scalar(xs[:, slot, :, :], g["xn_t"][:, :, bass.ds(t * TN, TN)], 1.0, None, ALU.mult)

            def stage_cross(t, slot):
                v.wait_ge(s_cross, t + 1)
                stage(t, slot).then_inc(s_xs, 1)
            paired(v, NT, stage_cross)
            v.wait_ge(s_cross, NT + 2)
            c.link(v.scalar_tensor_tensor(out=sqp[:, :].rearrange("p (t n) -> p t n", t=NT),
                                          in0=p_s[1][0:TN, 0:NT * NB].rearrange("p (t n) -> p t n", t=NT), scalar=2.0,
                                          in1=c0[:, :].rearrange("p (o n) -> p o n", o=1).to_broadcast([TN, NT, NB]),
                                          op0=ALU.mult, op1=ALU.add))
            c.link(v.tensor_tensor(sqp[:, :], sqp[:, :], g["sq"][:, :], ALU.add))
            c.link(v.tensor_scalar(sqp[:, :], sqp[:, :], -0.5 * MSCALE * MSCALE, None, ALU.mult))
            left = sqp[:, :].rearrange("p (t i h) -> p t i h", t=NT, i=2)
            for r in range(PARTS):
                part = s54[:, :, :].rearrange("p t (i q) -> p t i q", i=2)[:, :, :, r * MH:(r + 1) * MH]
                c.link(v.tensor_copy(part, left))
                if r < PARTS - 1:
                    c.link(v.tensor_tensor(left, left, part, ALU.subtract))

            def stage_parts(t, slot):
                v.wait_ge(s_st, t + 1)
                v.tensor_scalar(s54s[:, slot:slot + 1, :], s54[:, bass.ds(t, 1), :], 1.0, None, ALU.mult).then_inc(s_s54, 1)
            paired(v, NT, stage_parts)
            v.wait_ge(s_aug, NT + 2)
            with v.Fori(0, NW // 2) as hq:
                for odd in range(2):
                    hp = hq * 2 + odd

                    def stage_key(t, slot):
                        v.wait_ge(s_u, hp * NT + t + 1)
                        v.tensor_scalar(augs[:, slot, :], augx[:, 1, bass.ds(t * TN, TN)], 1.0, None, ALU.mult)
                        stage(t, slot).then_inc(s_xs, 1)
                    flipped(v, NT, (1 + odd) % 2, stage_key)
                    v.wait_ge(s_efree, hp * NT + (NT + 2))
                    v.wait_ge(s_gt, 2 * hp + 1)
                    for m in range(4):
                        ins = v.tensor_tensor(gs[:, m, :], p_g[m][:, 0:D + 1], csum[:, :], ALU.add)
                    ins.then_inc(s_gs, 1)
                    v.wait_ge(s_gs, hp + 1)
                    v.tensor_copy(kvs[:, bass.ds(hp * 2, 2), :, D],
                                  gs[:, :, D].rearrange("p (j m) -> p j m", j=2)).then_inc(s_kdiag, 1)
                    for b in p_g:
                        ins = v.memset(b[:, :], 0.0)
                    ins.then_inc(s_zero, 1)
                    for j in range(2):
                        v.wait_ge(s_gt, hp * 2 + (j + 2))
                        v.tensor_copy(gt[:, :, :], p_u[0][:, :].rearrange("p (c d) -> p c d", c=KC))
                        v.tensor_copy(kst[:, :], p_u[1][0:1, 0:D]).then_inc(s_gtc, 1)
            v.sem_inc(s_nfree, 2)

            def add_eps(t, q):
                v.wait_ge(s_eq, 4 * t + (q + 3))
                v.tensor_scalar(eq[:, q, :, :], eq[:, q, :, :], 16e-6, None, ALU.add).then_inc(s_eps, 1)

            def add_heads(t, q, slot):
                for j in range(2):
                    h = 2 * q + j
                    n = p_u[j][0:TN, :]
                    v.wait_ge(s_n, 8 * t + (MH + h + 1))
                    v.reciprocal(rz[:, h:h + 1], n[:, D:D + 1]).then_inc(s_rz, 1)
                    v.wait_ge(s_rz, 8 * t + (h + 1))
                    if h == 0:
                        v.wait_ge(s_y, t + 1)
                        v.tensor_scalar(acc[:, slot, :], n[:, 0:D], rz[:, 0:1], None, ALU.mult).then_inc(s_nfree, 1)
                    else:
                        v.wait_ge(s_nfree, 8 * t + (h + 2))
                        v.scalar_tensor_tensor(out=acc[:, slot, :], in0=n[:, 0:D], scalar=rz[:, h:h + 1],
                                               in1=acc[:, slot, :], op0=ALU.mult, op1=ALU.add).then_inc(s_nfree, 1)

            def queries(t, slot, last=False):
                add_eps(t, 1)
                add_heads(t, 0, slot)
                add_eps(t, 2)
                add_heads(t, 1, slot)
                add_eps(t, 3)
                add_heads(t, 2, slot)
                if not last:
                    add_eps(t + 1, 0)
                add_heads(t, 3, slot)
            add_eps(0, 0)
            with v.Fori(0, NT // 2) as i:
                queries(2 * i, 0)
                queries(2 * i + 1, 1)
            queries(NT - 1, 0, last=True)


class Mlp:

    def __init__(self, k, name, chunks, func):
        self.chunks, self.func = chunks, func
        self.xin = k.sb(name + "_xin", [TN, 2, D])
        self.xt = k.sb(name + "_xt", [P, 2, KC, TN])
        self.ht = k.sb(name + "_ht", [P, 2, chunks, TN])
        self.w1 = k.sb(name + "_w1", [P, KC, chunks * P])
        self.w2 = k.sb(name + "_w2", [P, chunks, D])
        self.b1 = k.sb(name + "_b1", [P, chunks])
        self.banks = -(-chunks // 4)
        self.p_x = [k.ps(f"{name}_px{i}") for i in range(2)]
        self.p_h = [[k.ps(f"{name}_ph{i}{j}") for j in range(self.banks)] for i in range(2)]
        self.p_y = [k.ps(f"{name}_py{i}") for i in range(2)]
        self.s_w = k.sem(name + "_w")
        self.s_in = k.sem(name + "_in")
        self.s_tr = k.sem(name + "_tr")
        self.s_xt = k.sem(name + "_xt")
        self.s_h = k.sem(name + "_h")
        self.s_ht = k.sem(name + "_ht")
        self.s_y = k.sem(name + "_y")
        self.s_take = k.sem(name + "_take")

    def load(self, sp, w1, w2, b1):
        sp.dma_start(self.w1[:, :, :], w1).then_inc(self.s_w, 16)
        sp.dma_start(self.w2[:, :, :], w2).then_inc(self.s_w, 16)
        sp.dma_start(self.b1[:, :], b1).then_inc(self.s_w, 16)

    def schedule(self, eng, ahead, mid, behind):
        ahead(0, 0)
        ahead(1, 1)
        mid(0, 0)

        def pair(i):
            ahead(2 * i + 2, 0)
            mid(2 * i + 1, 1)
            behind(2 * i, 0)
            ahead(2 * i + 3, 1)
            mid(2 * i + 2, 0)
            behind(2 * i + 1, 1)
        pair(0)
        with eng.Fori(1, (NT - 3) // 2) as i:
            pair(i)
        ahead(NT - 1, 0)
        mid(NT - 2, 1)
        behind(NT - 3, 0)
        mid(NT - 1, 0)
        behind(NT - 2, 1)
        behind(NT - 1, 0)

    def on_pe(self, pe, ident):
        for s in (self.s_tr, self.s_h, self.s_y):
            pe.sem_inc(s, 2)
        pe.wait_ge(self.s_w, 48)

        def transpose(t, slot):
            pe.wait_ge(self.s_in, t + 1)
            pe.wait_ge(self.s_xt, t + 1)
            for c in range(KC):
                ins = pe.transpose(self.p_x[slot][:, c * TN:(c + 1) * TN], self.xin[:, slot, c * P:(c + 1) * P],
                                   ident[0:TN, 0:TN])
            ins.then_inc(self.s_tr, 1)

        def hidden(t, slot):
            pe.wait_ge(self.s_xt, t + 3)
            pe.wait_ge(self.s_ht, t + 1)
            for f in range(self.chunks):
                out = self.p_h[slot][f // 4][:, (f % 4) * TN:(f % 4 + 1) * TN]
                for c in range(KC):
                    ins = pe.matmul(out, self.w1[:, c, f * P:(f + 1) * P], self.xt[:, slot, c, :], start=c == 0, stop=c == KC - 1)
            ins.then_inc(self.s_h, 1)

        def output(t, slot):
            pe.wait_ge(self.s_ht, t + 3)
            pe.wait_ge(self.s_take, t + 1)
            for f in range(self.chunks):
                ins = pe.matmul(self.p_y[slot][0:TN, 0:D], self.ht[:, slot, f, :], self.w2[:, f, :],
                                start=f == 0, stop=f == self.chunks - 1)
            ins.then_inc(self.s_y, 1)
        self.schedule(pe, transpose, hidden, output)

    def on_act(self, act):
        act.sem_inc(self.s_xt, 2)
        act.sem_inc(self.s_ht, 2)

        def copy(t, slot):
            act.wait_ge(self.s_tr, t + 3)
            act.wait_ge(self.s_h, t + 1)
            act.copy(self.xt[:, slot, :, :], self.p_x[slot][:, 0:KC * TN].rearrange("p (c n) -> p c n", c=KC)).then_inc(self.s_xt, 1)

        def function(t, slot):
            act.wait_ge(self.s_h, t + 3)
            act.wait_ge(self.s_y, t + 1)
            for f in range(self.chunks):
                ins = act.activation(self.ht[:, slot, f, :], self.p_h[slot][f // 4][:, (f % 4) * TN:(f % 4 + 1) * TN],
                                     self.func, bias=self.b1[:, f:f + 1])
            ins.then_inc(self.s_ht, 1)
        self.schedule(act, copy, function, lambda t, slot: None)

    def on_dve(self, v, put, take):
        v.sem_inc(self.s_take, 2)

        def inward(t, slot):
            v.wait_ge(self.s_tr, t + 1)
            put(t, slot, self.xin[:, slot, :]).then_inc(self.s_in, 1)

        def outward(t, slot):
            v.wait_ge(self.s_y, t + 3)
            take(t, slot, self.p_y[slot][0:TN, 0:D]).then_inc(self.s_take, 1)

        def pair(i):
            inward(2 * i + 3, 1)
            outward(2 * i, 0)
            inward(2 * i + 4, 0)
            outward(2 * i + 1, 1)
        for t in range(3):
            inward(t, t % 2)
        pair(0)
        with v.Fori(1, (NT - 3) // 2) as i:
            pair(i)
        for t in range(NT - 3, NT):
            outward(t, t % 2)


AFF_T = 5


def affine(v, done, wait, x, gain, bias):
    def over(r):
        return r.rearrange("p (o d) -> p o d", o=1).to_broadcast([TN, AFF_T, D])
    chunks = [x[:, t:t + AFF_T, 0:D] for t in range(0, NT, AFF_T)]
    for tiles in chunks:
        done(v.tensor_tensor(tiles, tiles, over(gain), ALU.mult))
    for c, tiles in enumerate(chunks):
        wait(c + 1)
        done(v.tensor_tensor(tiles, tiles, over(bias), ALU.add))


def mix_out(nc, a, g, scr):
    with ExitStack() as ctx:
        k = Kit(nc, ctx)
        mlp = Mlp(k, "mm", KC, ACT.Relu)
        norm = Norm(k, "mn")
        rows = k.sb("mrows", [TN, 5, D])
        s_rows = k.sem("mo_rows")
        s_dve = k.sem("mo_dve")
        s_ap = k.sem("mo_ap")
        s_aff = k.sem("mo_aff")
        s_put = k.sem("mo_put")
        block = ctx.enter_context(nc.Block())
        xn = g["xn"]

        @block.sync
        def _(sp):
            sp.dma_start(rows[:, :, :].rearrange("p r d -> p (r d)"), row(a["m_rows"], TN)).then_inc(s_rows, 16)
            mlp.load(sp, a["m_w1"], a["m_w2"], a["m_b1"])

        @block.tensor
        def _(pe):
            mlp.on_pe(pe, g["ident"])

        @block.scalar
        def _(act):
            mlp.on_act(act)

        @block.vector
        def _(v):
            c = Steps(v, s_dve)
            norm.moments(v, c, xn, 1e-6)
            norm.apply_all(v, xn).then_inc(s_ap, 1)
            v.wait_ge(s_rows, 16)
            v.wait_ge(s_ap, 1)
            aff = 2 * (NT // AFF_T)
            affine(v, lambda ins: ins.then_inc(s_aff, 1), lambda n: v.wait_ge(s_aff, n), xn, rows[:, 0, :], rows[:, 1, :])
            v.wait_ge(s_aff, aff)

            def put(t, slot, xin):
                return v.tensor_scalar(xin.rearrange("p (o d) -> p o d", o=1), xn[:, bass.ds(t, 1), 0:D], 1.0, None, ALU.mult)

            def take(t, slot, y):
                tile = xn[:, bass.ds(t, 1), 0:D]
                v.tensor_tensor(tile, tile, y.rearrange("p (o d) -> p o d", o=1), ALU.add).then_inc(s_put, 1)
                v.wait_ge(s_put, t + 1)
                return v.tensor_tensor(tile, tile, rows[:, 2:3, :], ALU.add)
            mlp.on_dve(v, put, take)
            v.wait_ge(mlp.s_take, NT + 2)
            norm.moments(v, c, xn, 1e-6)
            norm.apply_all(v, xn).then_inc(s_ap, 1)
            v.wait_ge(s_ap, 2)
            affine(v, lambda ins: ins.then_inc(s_aff, 1), lambda n: v.wait_ge(s_aff, aff + n), xn, rows[:, 3, :], rows[:, 4, :])
            v.wait_ge(s_aff, 2 * aff)
            v.tensor_tensor(g["xacc"][:, :, :], g["xacc"][:, :, :], xn[:, :, 0:D], ALU.add)


def gnn(nc, a, g, scr):
    with ExitStack() as ctx:
        k = Kit(nc, ctx)
        NG = ETILES // GRP
        SL = 4
        PQ = 1
        hid, agg = g["xn"], g["xn_t"]
        q_sb = k.sb("q_sb", [TN, NT * D])
        cnt_t = k.sb("cnt_t", [N_ET, NT * TN])
        target = k.sb("target", [P, ETILES], I32)
        source = k.sb("source", [P, ETILES])
        wo = k.sb("wo", [P, KC, D])
        et = k.sb("et_t", [P, KC, N_ET])
        ewo = k.sb("ewo", [N_ET, D])
        rows = k.sb("grows", [TN, 6, D])
        xt = k.sb("gxt", [P, 2, KC, TN])
        idx = k.sb("idx", [P, SL, GRP], I32)
        kv = k.sb("kv", [P, SL, GRP, 2 * D])
        prod = k.sb("prod", [P, GRP, GH * GH * GD])
        flat, used = prod[:, :, :].rearrange("p j m -> p (j m)"), 0

        def share(parts, a_, b_):
            nonlocal used
            used += a_ * b_
            assert used <= GRP * GH * GH * GD
            return flat[0:parts, used - a_ * b_:used].rearrange("p (a b) -> p a b", a=a_)
        kvst = share(TN, 2, 2 * D)
        wqkv = share(P, KC, 3 * D)
        win = share(P, KC, D)
        hs = share(TN, 2, D)
        bin_ = share(TN, 1, D)
        cs = share(N_ET, 2, TN)
        sc = k.sb("sc", [P, GRP * GH * GH])
        mx = k.sb("mx", [P, GRP * GH])
        sm = k.sb("sm", [P, GRP * GH])
        ex = k.sb("ex", [P, GRP * GH * GH])
        attn = k.sb("attn", [P, 2, GRP, GH * GH])
        wv = k.sb("wv", [P, GRP, GH, D])
        table = wv[:, :, :, :].rearrange("p j g d -> p (j g d)")[:, 0:TCOLS].bitcast(I32)
        q_last = k.sb("q_last", [P, D + PQ * GD])
        oh = k.sb("oh", [P, SL, GRP, TN])
        oht = k.sb("oht", [TN, 2, GRP, P])
        norm = Norm(k, "gn")
        p_q = [k.ps(f"p_q{i}") for i in range(2)]
        p_a = [k.ps(f"p_a{i}") for i in range(4)]
        p_t = k.ps("p_t")
        p_o = k.ps("p_o")

        s_const = k.sem("gn_const")
        s_edge = k.sem("gn_edge")
        s_w = k.sem("gn_w")
        s_rows = k.sem("gn_rows")
        s_hs = k.sem("gn_hs")
        s_tr = k.sem("gn_tr")
        s_xt = k.sem("gn_xt")
        s_qkv = k.sem("gn_qkv")
        s_kvst = k.sem("gn_kvst")
        s_kvd = [k.sem(f"gn_kvd{i}") for i in range(2)]
        s_h0 = k.sem("gn_h0")
        s_ewo = k.sem("gn_ewo")
        s_ewoc = k.sem("gn_ewoc")
        s_start = k.sem("gn_start")
        s_vgo = k.sem("gn_vgo")
        s_pgo = k.sem("gn_pgo")
        s_go = k.sem("gn_go")
        s_azero = k.sem("gn_azero")
        s_idx = k.sem("gn_idx")
        s_kv = [k.sem(f"gn_kv{i}") for i in range(SL)]
        s_oh = k.sem("gn_oh")
        s_t = k.sem("gn_t")
        s_tc = k.sem("gn_tc")
        s_qe = k.sem("gn_qe")
        s_pk = k.sem("gn_pk")
        s_ql = k.sem("gn_ql")
        s_pp = k.sem("gn_pp")
        s_chain = k.sem("gn_chain")
        s_ex = k.sem("gn_ex")
        s_attn = k.sem("gn_attn")
        s_wv = k.sem("gn_wv")
        s_wa = k.sem("gn_wa")
        s_agg = k.sem("gn_agg")
        s_acc = k.sem("gn_acc")
        s_os = k.sem("gn_os")
        s_o = k.sem("gn_o")
        s_hm = k.sem("gn_hm")
        s_dve = k.sem("gn_dve")
        s_ap = k.sem("gn_ap")
        s_aff = k.sem("gn_aff")
        s_relu = k.sem("gn_relu")
        block = ctx.enter_context(nc.Block())
        NORM_STEPS = 23
        per = NG * GRP
        ACT_G = (3, 2, 2, 2)
        assert NG % (2 * SL) == 0 and GRP == 4
        p_qt = [p_q[0][:, 0:D], p_q[0][:, D:2 * D], p_q[1][:, 0:D], p_o[:, 0:D]]

        def gathered(l, i):
            return (l * (NG // SL) + i + 1) * (16 * GRP)

        def edge_loop(eng, body):
            for u in range(SL):
                body(u, u, 0, lambda d, u=u: u + d >= 0)
            with eng.Fori(1, NG // SL - 1) as i:
                for u in range(SL):
                    body(i * SL + u, u, i, lambda d: True)
            for u in range(SL):
                body(NG - SL + u, u, NG // SL - 1, lambda d, u=u: u + d < SL)

        def buckets(eng, kk, stride):
            word = eng.value_load(g["tab"][0:1, bass.ds(kk, 1)], min_val=0, max_val=(1 << 20) - 1)
            return [nc.s_assert_within(eng.snap(((word >> (5 * j)) & 31) * stride), 0, (NT - 1) * stride,
                                       skip_runtime_bounds_check_because="the table's buckets are at most NT - 1")
                    for j in range(GRP)]

        @block.sync
        def _(sp):
            sp.dma_start(table[:, :], scr["table"].rearrange("(p c) o -> p (c o)", p=P)).then_inc(s_const, 16)
            sp.dma_start(cnt_t[:, :].rearrange("e (b n) -> e b n", b=NT), scr["counts"].rearrange("(b e) n -> e b n", e=N_ET)).then_inc(s_const, 16)
            sp.dma_start(win[:, :, :], a["g_win"]).then_inc(s_kvd[0], 16)
            sp.dma_start(bin_[:, :, :], row(a["g_bin"], TN).rearrange("p (o d) -> p o d", o=1)).then_inc(s_kvd[1], 16)
            with sp.Fori(0, LAYERS) as l:
                sp.wait_ge(s_relu, l * NT + 1)
                one = bass.ds(l, 1)
                sp.dma_start(wqkv[:, :, :].rearrange("p (o c) d -> p o (c d)", o=1), a["g_wqkv"][:, one, :]).then_inc(s_w, 16)
                sp.dma_start(wo[:, :, :].rearrange("p (o c) d -> p o (c d)", o=1), a["g_wo"][:, one, :]).then_inc(s_w, 16)
                sp.dma_start(et[:, :, :].rearrange("p (o c) d -> p o (c d)", o=1), a["g_et"][:, one, :]).then_inc(s_w, 16)
                sp.dma_start(rows[:, :, :].rearrange("p (o r) d -> p o (r d)", o=1),
                             a["g_rows"][one, :].rearrange("o (x d) -> x o d", x=1).to_broadcast([TN, 1, 6 * D])).then_inc(s_w, 16)

                def store(t, slot):
                    sp.wait_ge(s_kvst, l * NT + t + (NT + 3))
                    sp.dma_start(scr["kv"][bass.ds(t * TN, TN), :], kvst[:, slot, :]).then_inc(s_kvd[slot], 16)
                with sp.Fori(0, NT // 2) as i:
                    store(2 * i, 0)
                    store(2 * i + 1, 1)
                store(NT - 1, 0)

        @block.tensor
        def _(pe):
            pe.wait_ge(s_const, 32)
            pe.wait_ge(s_kvd[0], 16)
            pe.sem_inc(s_h0, 2)

            def first(t, slot):
                pe.wait_ge(s_hs, t + 1)
                pe.wait_ge(s_kvst, t + 1)
                for c in range(KC):
                    ins = pe.matmul(p_q[slot][0:TN, 0:D], xt[:, slot, c, :], win[:, c, :], start=c == 0, stop=c == KC - 1)
                ins.then_inc(s_h0, 1)
            paired(pe, NT, first)
            pe.sem_inc(s_tr, 2)
            pe.sem_inc(s_qkv, 2)
            pe.sem_inc(s_o, 2)
            with pe.Fori(0, LAYERS) as l:
                node = l * NT
                pe.wait_ge(s_w, 64 * l + 64)
                for c in range(KC):
                    ins = pe.matmul(p_o[0:N_ET, 0:D], et[:, c, :], wo[:, c, :], start=c == 0, stop=c == KC - 1)
                ins.then_inc(s_ewo, 1)

                def transpose(t, slot):
                    pe.wait_ge(s_hs, node + t + (NT + 1))
                    pe.wait_ge(s_xt, node + t + 1)
                    for c in range(KC):
                        ins = pe.transpose(p_q[slot][:, c * TN:(c + 1) * TN], hs[:, slot, c * P:(c + 1) * P], g["ident"][0:TN, 0:TN])
                    ins.then_inc(s_tr, 1)

                def qkv(t, slot):
                    pe.wait_ge(s_xt, node + t + 3)
                    pe.wait_ge(s_kvst, node + t + (NT + 1))
                    for c in range(KC):
                        pe.matmul(p_a[2 * slot][0:TN, :], xt[:, slot, c, :], wqkv[:, c, 0:2 * D], start=c == 0, stop=c == KC - 1)
                    for c in range(KC):
                        ins = pe.matmul(p_a[2 * slot + 1][0:TN, 0:D], xt[:, slot, c, :], wqkv[:, c, 2 * D:3 * D], start=c == 0, stop=c == KC - 1)
                    ins.then_inc(s_qkv, 1)
                transpose(0, 0)
                with pe.Fori(0, NT // 2) as i:
                    transpose(2 * i + 1, 1)
                    qkv(2 * i, 0)
                    transpose(2 * i + 2, 0)
                    qkv(2 * i + 1, 1)
                qkv(NT - 1, 0)
                pe.wait_ge(s_kvst, node + (2 * NT + 2))

                def spread(kk, u):
                    pe.wait_ge(s_oh, l * NG + kk + 1)
                    for j in range(GRP):
                        ins = pe.transpose(p_t[0:TN, j * P:(j + 1) * P], oh[:, u, j, :], g["ident"][:, :])
                    ins.then_inc(s_t, 1)

                def sources(kk, u, guard):
                    bucket = buckets(pe, kk, D)
                    pe.wait_ge(s_tc, l * NG + kk + 1)
                    for j in range(GRP):
                        if guard and j in (0, 2):
                            pe.wait_ge(s_pk, (l * NG + kk) * (GRP - 1) + (2 - GRP + 1 if j == 0 else 0))
                        elif guard and j == GRP - 1:
                            pe.wait_ge(s_ql, l * NG + kk)
                        pe.matmul(p_qt[j], oht[:, u % 2, j, :],
                                  q_sb[:, bass.ds(bucket[j], D)], start=True, stop=True).then_inc(s_qe, 1)

                def sums(kk, u, j, guard):
                    out = p_a[2 * (u % 2) + j // 2]
                    n = l * per + GRP * kk
                    pe.wait_ge(s_wv, n + (j + 1))
                    pe.wait_ge(s_wa, n + (j + 1))
                    if guard:
                        pe.wait_ge(s_acc, n + (j // 2 * 2 + 2 - 2 * GRP))
                    for c in range(KC):
                        for h in range(GH):
                            ins = pe.matmul(out[:, (j % 2) * 2 * TN + c * TN:(j % 2) * 2 * TN + (c + 1) * TN],
                                            wv[:, j, h, c * P:(c + 1) * P], oh[:, u, j, :], start=h == 0, stop=h == GH - 1)
                    ins.then_inc(s_agg, 1)

                spread(0, 0)
                sources(0, 0, False)

                def body(kk, u, i, has):
                    if has(1):
                        spread(kk + 1, (u + 1) % SL)
                        sources(kk + 1, (u + 1) % SL, True)
                    if has(-1):
                        sums(kk - 1, (u - 1) % SL, 0, has(-3))
                        sums(kk - 1, (u - 1) % SL, 1, has(-3))
                        sums(kk - 1, (u - 1) % SL, 2, has(-3))
                        sums(kk - 1, (u - 1) % SL, 3, has(-3))
                edge_loop(pe, body)
                for j in range(GRP):
                    sums(NG - 1, SL - 1, j, True)

                pe.wait_ge(s_ql, l * NG + NG)
                hold(pe, s_pgo, s_ewoc, l + 1)

                def project(t, slot):
                    pe.wait_ge(s_os, node + t + 2)
                    pe.wait_ge(s_hm, node + t + 1)
                    out = [p_t, p_o][slot][0:TN, 0:D]
                    for c in range(KC):
                        pe.matmul(out, xt[:, slot, c, :], wo[:, c, :], start=c == 0, stop=False)
                    pe.matmul(out, cs[:, slot, :], ewo[:, :], start=False, stop=True).then_inc(s_o, 1)
                paired(pe, NT, project)

        @block.scalar
        def _(act):
            act.sem_inc(s_xt, 2)
            act.sem_inc(s_os, 1)
            with act.Fori(0, LAYERS) as l:
                node = l * NT

                def copy(t, slot):
                    act.wait_ge(s_tr, node + t + 3)
                    act.wait_ge(s_qkv, node + t + 1)
                    act.copy(xt[:, slot, :, :], p_q[slot][:, 0:KC * TN].rearrange("p (c n) -> p c n", c=KC)).then_inc(s_xt, 1)
                paired(act, NT, copy)
                act.wait_ge(s_qkv, node + (NT + 2))

                def spread(kk, u, guard):
                    act.wait_ge(s_t, l * NG + kk + 1)
                    if guard:
                        act.wait_ge(s_qe, l * per + GRP * kk + (-GRP))
                    act.copy(oht[:, u % 2, :, :], p_t[0:TN, :].rearrange("p (j e) -> p j e", j=GRP)).then_inc(s_tc, 1)
                spread(0, 0, False)
                spread(1, 1, False)

                def last_q(kk, guard):
                    act.wait_ge(s_qe, l * per + GRP * kk + GRP)
                    if guard:
                        act.wait_ge(s_pp, l * NG + kk)
                    act.copy(q_last[:, 0:D], p_qt[GRP - 1])
                    act.copy(q_last[:, D:], p_qt[GRP - 2][:, D - PQ * GD:D]).then_inc(s_ql, 1)
                def exponentials(grp):
                    act.wait_ge(s_chain, 5 * grp + 3)
                    act.activation(ex[:, :], sc[:, :], ACT.Exp, scale=1.0 / 8.0).then_inc(s_ex, 1)

                def values(kk, u, j, has):
                    if has(-1):
                        act.wait_ge(s_agg, l * per + GRP * kk + (j - GRP + 1))
                    for gg in range(GH - ACT_G[j], GH):
                        for h in range(GH):
                            ins = act.activation(wv[:, j, gg, h * GD:(h + 1) * GD], kv[:, u, j, D + gg * GD:D + (gg + 1) * GD],
                                                 ACT.Copy, scale=attn[:, u % 2, j, gg * GH + h:gg * GH + h + 1])
                    ins.then_inc(s_wa, 1)
                last_q(0, False)
                last_q(1, True)
                exponentials(l * NG)

                def body(kk, u, i, has):
                    act.wait_ge(s_kv[u], gathered(l, i))
                    act.wait_ge(s_attn, l * NG + kk + 1)
                    values(kk, u, 0, has)
                    values(kk, u, 1, has)
                    if has(2):
                        spread(kk + 2, (u + 2) % SL, True)
                    values(kk, u, 2, has)
                    if has(2):
                        last_q(kk + 2, True)
                    if has(1):
                        exponentials(l * NG + kk + 1)
                    values(kk, u, 3, has)
                edge_loop(act, body)

                def staged(t, slot):
                    act.wait_ge(s_acc, l * per + per)
                    act.wait_ge(s_o, node + t + 1)
                    act.copy(xt[:, slot, :, :], agg[:, :, bass.ds(t * TN, TN)])
                    act.copy(cs[:, slot, :], cnt_t[:, bass.ds(t * TN, TN)]).then_inc(s_os, 1)
                paired(act, NT, staged)

        @block.gpsimd
        def _(pool):
            with pool.Fori(0, LAYERS) as l:
                pool.wait_ge(s_os, l * NT + 1)
                hold(pool, s_go, s_start, l + 1)
                pool.memset(agg[:, :, :], 0.0).then_inc(s_azero, 1)

                def columns(kk, slot):
                    pool.tensor_copy(idx[:, slot, :], target[:, bass.ds(GRP * kk, GRP)]).then_inc(s_idx, 1)

                def gather(slot, j):
                    pool.indirect_dma_start(out=kv[:, slot, j, :], out_offset=None, in_=scr["kv"],
                                            in_offset=bass.IndirectOffsetOnAxis(ap=idx[:, slot, j:j + 1], axis=0)).then_inc(s_kv[slot], 16)

                def product(kk, slot, i):
                    j = GRP - 1
                    pool.wait_ge(s_ql, l * NG + kk + 1)
                    pool.wait_ge(s_kv[slot], gathered(l, i))
                    pool.tensor_tensor(prod[:, j, :].rearrange("p (h g d) -> p h g d", h=GH, g=GH),
                                       q_last[:, 0:D].rearrange("p (h o d) -> p h o d", h=GH, o=1).to_broadcast([P, GH, GH, GD]),
                                       kv[:, slot, j, 0:D].rearrange("p (o g d) -> p o g d", o=1, g=GH).to_broadcast([P, GH, GH, GD]),
                                       ALU.mult)
                    pool.tensor_tensor(prod[:, j - 1, (GH - PQ) * D:].rearrange("p (h g d) -> p h g d", h=PQ, g=GH),
                                       q_last[:, D:].rearrange("p (h o d) -> p h o d", h=PQ, o=1).to_broadcast([P, PQ, GH, GD]),
                                       kv[:, slot, j - 1, 0:D].rearrange("p (o g d) -> p o g d", o=1, g=GH).to_broadcast([P, PQ, GH, GD]),
                                       ALU.mult).then_inc(s_pp, 1)

                def values(kk, u, j, has):
                    m = GH - ACT_G[j]
                    if has(-1):
                        pool.wait_ge(s_agg, l * per + GRP * kk + (j - GRP + 1))
                    pool.tensor_tensor(wv[:, j, 0:m, :].rearrange("p g (h d) -> p g h d", h=GH),
                                       kv[:, u, j, D:D + m * GD].rearrange("p (g o d) -> p g o d", g=m, o=1).to_broadcast([P, m, GH, GD]),
                                       attn[:, u % 2, j, 0:m * GH].rearrange("p (g h o) -> p g h o", g=m, o=1).to_broadcast([P, m, GH, GD]),
                                       ALU.mult).then_inc(s_wv, 1)
                pool.wait_ge(s_edge, 1)
                pool.wait_ge(s_kvd[0], 16 * (NT - NT // 2) * (l + 1) + 16)
                pool.wait_ge(s_kvd[1], 16 * (NT // 2) * (l + 1) + 16)
                pool.sem_inc(s_go, 1)
                for slot in range(SL - 1):
                    columns(slot, slot)
                hold(pool, s_go, s_idx, NG * l + SL - 1)
                for slot in range(SL - 1):
                    for j in range(GRP):
                        gather(slot, j)
                product(0, 0, 0)

                def body(kk, u, i, has):
                    ahead = (u + 3) % SL
                    pool.wait_ge(s_kv[u], gathered(l, i))
                    pool.wait_ge(s_attn, l * NG + kk + 1)
                    if has(1):
                        product(kk + 1, (u + 1) % SL, i if u < SL - 1 else i + 1)
                    values(kk, u, 0, has)
                    if has(3):
                        columns(kk + 3, ahead)
                    values(kk, u, 1, has)
                    if has(3):
                        if has(-1):
                            pool.wait_ge(s_wv, l * per + GRP * kk)
                            pool.wait_ge(s_wa, l * per + GRP * kk)
                        hold(pool, s_go, s_idx, l * NG + kk + 4)
                        gather(ahead, 0)
                        gather(ahead, 1)
                    values(kk, u, 2, has)
                    values(kk, u, 3, has)
                    if has(3):
                        gather(ahead, 2)
                        gather(ahead, 3)
                edge_loop(pool, body)

        @block.vector
        def _(v):
            v.wait_ge(s_const, 32)
            v.wait_ge(s_kvd[1], 16)
            c = Steps(v, s_dve)
            c.link(v.tensor_scalar(target[:, :], table[:, 0:ETILES], (1 << NODE_BITS) - 1, None, ALU.bitwise_and))
            c.link(v.tensor_scalar(table[:, 0:ETILES], table[:, 0:ETILES], NODE_BITS, None, ALU.logical_shift_right))
            v.tensor_copy(source[:, :], table[:, 0:ETILES])
            v.sem_inc(s_edge, 1)
            v.sem_inc(s_kvst, 2)

            def stage0(t, slot):
                v.wait_ge(s_h0, t + 1)
                v.tensor_scalar(xt[:, slot, :, :], agg[:, :, bass.ds(t * TN, TN)], 1.0, None, ALU.mult).then_inc(s_hs, 1)

            def take0(t, slot):
                v.wait_ge(s_h0, t + 3)
                v.tensor_tensor(hid[:, bass.ds(t, 1), 0:D], p_q[slot][0:TN, 0:D].rearrange("p (o d) -> p o d", o=1),
                                bin_[:, :, :], ALU.add).then_inc(s_kvst, 1)
            stage0(0, 0)
            with v.Fori(0, NT // 2) as i:
                stage0(2 * i + 1, 1)
                take0(2 * i, 0)
                stage0(2 * i + 2, 0)
                take0(2 * i + 1, 1)
            take0(NT - 1, 0)
            v.wait_ge(s_kvst, NT + 2)
            v.sem_inc(s_hm, 2)
            v.sem_inc(s_relu, 1)
            with v.Fori(0, LAYERS) as l:
                node = l * NT
                v.sem_inc(s_start, 1)
                v.wait_ge(s_w, 64 * l + 64)
                v.wait_ge(s_ewo, l + 1)
                v.tensor_tensor(ewo[:, :], p_o[0:N_ET, 0:D], rows[0:N_ET, 3, :], ALU.add).then_inc(s_ewoc, 1)

                def stage(t, slot):
                    v.wait_ge(s_tr, node + t + 1)
                    v.tensor_scalar(hs[:, slot:slot + 1, :], hid[:, bass.ds(t, 1), 0:D], 1.0, None, ALU.mult).then_inc(s_hs, 1)

                def take(t, i, slot):
                    v.wait_ge(s_qkv, node + t + 3)
                    v.wait_ge(s_kvd[slot], 16 * ((NT - NT // 2 if slot == 0 else NT // 2) * l + i) + 16)
                    v.tensor_tensor(kvst[:, slot, :], p_a[2 * slot][0:TN, :], rows[:, 0:2, :].rearrange("p r d -> p (r d)"), ALU.add)
                    v.tensor_tensor(q_sb[:, bass.ds(t * D, D)], p_a[2 * slot + 1][0:TN, 0:D], rows[:, 2, :], ALU.add).then_inc(s_kvst, 1)
                stage(0, 0)
                stage(1, 1)
                with v.Fori(0, NT // 2 - 1) as i:
                    stage(2 * i + 2, 0)
                    take(2 * i, i, 0)
                    stage(2 * i + 3, 1)
                    take(2 * i + 1, i, 1)
                stage(NT - 1, 0)
                take(NT - 3, NT // 2 - 1, 0)
                take(NT - 2, NT // 2 - 1, 1)
                take(NT - 1, NT // 2, 0)
                v.wait_ge(s_azero, l + 1)

                def onehot(kk, u):
                    v.tensor_tensor(oh[:, u, :, :],
                                    source[:, bass.ds(GRP * kk, GRP)].rearrange("p (j o) -> p j o", o=1).to_broadcast([P, GRP, TN]),
                                    g["iota_n"][:, :].rearrange("p (o n) -> p o n", o=1).to_broadcast([P, GRP, TN]),
                                    ALU.is_equal).then_inc(s_oh, 1)

                def add_sum(kk, u, bucket, j):
                    n = l * per + GRP * kk
                    tile = agg[:, :, bass.ds(bucket[j], TN)]
                    v.wait_ge(s_agg, n + (j // 2 * 2 + 2))
                    if j or not isinstance(kk, int) or kk:
                        v.wait_ge(s_acc, n + j)
                    v.tensor_tensor(tile, tile, p_a[2 * (u % 2) + j // 2][:, (j % 2) * 2 * TN:(j % 2 + 1) * 2 * TN].rearrange("p (c n) -> p c n", c=KC),
                                    ALU.add).then_inc(s_acc, 1)

                def body(kk, u, i, has):
                    n = l * per + GRP * kk
                    grp = l * NG + kk
                    places = {}

                    def add(d, j):
                        if has(-d):
                            if d not in places:
                                places[d] = buckets(v, kk - d, TN)
                            add_sum(kk - d, (u - d) % SL, places[d], j)
                    v.wait_ge(s_kv[u], gathered(l, i))
                    for j in range(GRP - 1):
                        v.wait_ge(s_qe, n + max(j + 1, 2))
                        m = GH if j < GRP - 2 else GH - PQ
                        if j == GRP - 2:
                            v.wait_ge(s_ql, grp + 1)
                        v.tensor_tensor(prod[:, j, 0:m * D].rearrange("p (h g d) -> p h g d", h=m, g=GH),
                                        p_qt[j][:, 0:m * GD].rearrange("p (h o d) -> p h o d", h=m, o=1).to_broadcast([P, m, GH, GD]),
                                        kv[:, u, j, 0:D].rearrange("p (o g d) -> p o g d", o=1, g=GH).to_broadcast([P, m, GH, GD]),
                                        ALU.mult).then_inc(s_pk, 1)
                        add(*[(3, 2), (3, 3), (2, 0)][j])
                    steps = Steps(v, s_chain, 5 * grp)
                    v.wait_ge(s_pk, grp * (GRP - 1) + (GRP - 1))
                    v.wait_ge(s_pp, grp + 1)
                    steps.done(v.tensor_reduce(sc[:, :], prod[:, :, :].rearrange("p j (m d) -> p (j m) d", d=GD), AX.X, ALU.add))
                    add(2, 1)
                    steps.wait()
                    scg = sc[:, :].rearrange("p (m g) -> p m g", g=GH)
                    steps.done(v.tensor_reduce(mx[:, :], scg, AX.X, ALU.max))
                    steps.wait()
                    steps.done(v.tensor_tensor(scg, scg, mx[:, :].rearrange("p (m o) -> p m o", o=1).to_broadcast([P, GRP * GH, GH]), ALU.subtract))
                    if has(2):
                        if has(-2):
                            v.wait_ge(s_agg, n - GRP)
                        onehot(kk + 2, (u + 2) % SL)
                    v.wait_ge(s_ex, grp + 1)
                    exg = ex[:, :].rearrange("p (m g) -> p m g", g=GH)
                    steps.done(v.tensor_reduce(sm[:, :], exg, AX.X, ALU.add))
                    steps.wait()
                    steps.link(v.reciprocal(sm[:, :], sm[:, :]))
                    if has(-2):
                        v.wait_ge(s_wv, n - GRP)
                        v.wait_ge(s_wa, n - GRP)
                    v.tensor_tensor(attn[:, u % 2, :, :].rearrange("p j (g h) -> p j h g", g=GH),
                                    ex[:, :].rearrange("p (j h g) -> p j h g", j=GRP, h=GH),
                                    sm[:, :].rearrange("p (j h o) -> p j h o", j=GRP, o=1).to_broadcast([P, GRP, GH, GH]),
                                    ALU.mult).then_inc(s_attn, 1)
                    assert steps.n == 5

                onehot(0, 0)
                onehot(1, 1)
                edge_loop(v, body)
                for kk in (NG - 3, NG - 2, NG - 1):
                    bucket = buckets(v, kk, TN)
                    for j in range(2 if kk == NG - 3 else 0, GRP):
                        add_sum(kk, kk % SL, bucket, j)

                def add_messages(t, slot):
                    v.wait_ge(s_o, node + t + 3)
                    tile = hid[:, bass.ds(t, 1), 0:D]
                    v.tensor_tensor(tile, tile, [p_t, p_o][slot][0:TN, 0:D].rearrange("p (o d) -> p o d", o=1), ALU.add).then_inc(s_hm, 1)
                paired(v, NT, add_messages)
                hold(v, s_vgo, s_hm, node + (NT + 2))
                c = Steps(v, s_dve, l * NORM_STEPS + 2)
                norm.moments(v, c, hid, 1e-5)
                assert c.n == NORM_STEPS, c.n
                norm.apply_all(v, hid).then_inc(s_ap, 1)
                hold(v, s_vgo, s_ap, l + 1)
                aff = 2 * (NT // AFF_T)
                affine(v, lambda ins: ins.then_inc(s_aff, 1), lambda n: v.wait_ge(s_aff, l * aff + n),
                       hid, rows[:, 4, :], rows[:, 5, :])
                for n, t in enumerate(range(0, NT, AFF_T)):
                    tiles = hid[:, t:t + AFF_T, 0:D]
                    v.wait_ge(s_aff, l * aff + (aff // 2 + n + 1))
                    v.tensor_scalar(tiles, tiles, 0.0, None, ALU.max).then_inc(s_relu, AFF_T)
                hold(v, s_vgo, s_relu, node + (NT + 1))


def gnn_out(nc, a, g, scr):
    with ExitStack() as ctx:
        k = Kit(nc, ctx)
        mlp = Mlp(k, "gm", KC, ACT.Relu)
        b2 = k.sb("gb2", [TN, D])
        s_b2 = k.sem("go_b2")
        s_put = k.sem("go_put")
        block = ctx.enter_context(nc.Block())

        @block.sync
        def _(sp):
            sp.dma_start(b2[:, :], row(a["g_b2"], TN)).then_inc(s_b2, 16)
            mlp.load(sp, a["g_w1"], a["g_w2"], a["g_b1"])

        @block.tensor
        def _(pe):
            mlp.on_pe(pe, g["ident"])

        @block.scalar
        def _(act):
            mlp.on_act(act)

        @block.vector
        def _(v):
            v.wait_ge(s_b2, 16)

            def put(t, slot, xin):
                return v.tensor_scalar(xin.rearrange("p (o d) -> p o d", o=1), g["xn"][:, bass.ds(t, 1), 0:D], 1.0, None, ALU.mult)

            def take(t, slot, y):
                tile = g["xacc"][:, bass.ds(t, 1), :]
                v.tensor_tensor(tile, tile, y.rearrange("p (o d) -> p o d", o=1), ALU.add).then_inc(s_put, 1)
                v.wait_ge(s_put, t + 1)
                return v.tensor_tensor(tile, tile, b2[:, :].rearrange("p (o d) -> p o d", o=1), ALU.add)
            mlp.on_dve(v, put, take)


def route(nc, a, g, scr):
    with ExitStack() as ctx:
        k = Kit(nc, ctx)
        xn, xn_t = g["xn"], g["xn_t"]
        norm = Norm(k, "fn")
        tin = k.sb("tin", [TN, 2, D])
        wr = k.sb("wr", [P, KC])
        wrr = k.sb("wrr", [P, KC, TN])
        br = k.sb("br", [TN, 1])
        one = k.sb("fone", [P, TN])
        wb = g["wb"]
        p_tr = [k.ps(f"f_tr{i}") for i in range(2)]
        p_w = [k.ps(f"f_w{i}") for i in range(2)]
        p_c = k.ps("f_c")
        s_const = k.sem("fw_const")
        s_dve = k.sem("fw_dve")
        s_wrr = k.sem("fw_wrr")
        s_in = k.sem("fw_in")
        s_tr = k.sem("fw_tr")
        s_xt = k.sem("fw_xt")
        s_pw = k.sem("fw_pw")
        s_wb = k.sem("fw_wb")
        s_wc = k.sem("fw_wc")
        s_go = k.sem("fw_go")
        block = ctx.enter_context(nc.Block())

        @block.sync
        def _(sp):
            sp.dma_start(wr[:, :], a["f_wr"]).then_inc(s_const, 16)
            sp.dma_start(br[:, :], row(a["f_br"], TN)).then_inc(s_const, 16)

        @block.tensor
        def _(pe):
            def step(t, slot):
                pe.wait_ge(s_in, t + 1)
                pe.wait_ge(s_xt, t + 1)
                for c in range(KC):
                    ins = pe.transpose(p_tr[slot][:, c * TN:(c + 1) * TN], tin[:, slot, c * P:(c + 1) * P], g["ident"][0:TN, 0:TN])
                ins.then_inc(s_tr, 1)
            paired(pe, NT, step)
            pe.wait_ge(s_xt, NT + 2)
            pe.wait_ge(s_wrr, 1)

            def weights(t, slot):
                pe.wait_ge(s_wb, t + 1)
                for c in range(KC):
                    ins = pe.matmul(p_w[slot][0:TN, 0:TN], wrr[:, c, :], xn_t[:, c, bass.ds(t * TN, TN)], start=c == 0, stop=c == KC - 1)
                ins.then_inc(s_pw, 1)
            paired(pe, NT, weights)
            pe.wait_ge(s_wb, NT + 2)
            for t in range(NT):
                ins = pe.transpose(p_c[0:TN, t:t + 1], wb[0:1, t * TN:(t + 1) * TN], g["ident"][0:1, 0:1])
            ins.then_inc(s_wc, 1)

        @block.scalar
        def _(act):
            act.sem_inc(s_xt, 2)

            def step(t, slot):
                act.wait_ge(s_tr, t + 1)
                act.copy(xn_t[:, :, bass.ds(t * TN, TN)], p_tr[slot][:, 0:KC * TN].rearrange("p (c n) -> p c n", c=KC)).then_inc(s_xt, 1)
            paired(act, NT, step)

        @block.gpsimd
        def _(pool):
            with pool.Fori(0, NT) as t:
                hold(pool, s_go, s_in, t + 1)
                tile = g["xacc"][:, bass.ds(t, 1), :]
                pool.tensor_tensor(tile, tile, xn[:, bass.ds(t, 1), 0:D], ALU.add)

        @block.vector
        def _(v):
            c = Steps(v, s_dve)
            v.wait_ge(s_const, 32)
            c.link(v.memset(one[:, :], 1.0))
            for kc in range(KC):
                ins = v.tensor_scalar(wrr[:, kc, :], one[:, :], wr[:, kc:kc + 1], None, ALU.mult)
            ins.then_inc(s_wrr, 1)
            norm.moments(v, c, g["xacc"], 1e-5)

            def normed(t, slot):
                v.wait_ge(s_xt, t + 1)
                norm.apply(v, xn[:, bass.ds(t, 1), 0:D], g["xacc"][:, bass.ds(t, 1), :], t)
                norm.apply(v, tin[:, slot:slot + 1, :], g["xacc"][:, bass.ds(t, 1), :], t).then_inc(s_in, 1)
            paired(v, NT, normed)
            v.sem_inc(s_wb, 2)

            def weights(t, slot):
                v.wait_ge(s_pw, t + 1)
                v.tensor_scalar(wb[:, bass.ds(t * TN, TN)], p_w[slot][0:TN, 0:TN], br[:, :], None, ALU.add).then_inc(s_wb, 1)
            paired(v, NT, weights)
            v.wait_ge(s_wb, NT + 2)
            v.wait_ge(s_wc, 1)
            v.tensor_copy(g["wc"][:, :], p_c[0:TN, 0:NT])


def ffn(nc, a, g, scr, out):
    with ExitStack() as ctx:
        k = Kit(nc, ctx)
        mlp = Mlp(k, "fm", FF // P, ACT.Gelu_apprx_tanh)
        b2 = k.sb("fb2", [TN, D])
        res = k.sb("res", [TN, 2, D])
        rank = k.sb("rank", [TN, 3, NT])
        place = k.sb("place", [TN, NT])
        scale = k.sb("scale", [TN, NT])
        cmp = k.sb("cmp", [TN, N_NODES], BF16)
        eqm = k.sb("eqm", [TN, TN])
        lower = k.sb("lower", [TN, TN])
        s_b2 = k.sem("ff_b2")
        s_dve = k.sem("ff_dve")
        s_out = [k.sem(f"ff_out{i}") for i in range(2)]
        block = ctx.enter_context(nc.Block())
        out_t = out.rearrange("(t p) d -> p t d", p=TN)

        @block.sync
        def _(sp):
            sp.dma_start(b2[:, :], row(a["f_b2"], TN)).then_inc(s_b2, 16)
            sp.dma_start(lower[:, :], a["c_lower"]).then_inc(s_b2, 16)
            mlp.load(sp, a["f_w1"], a["f_w2"], a["f_b1"])

            def store(t, slot):
                sp.wait_ge(mlp.s_take, t + 3)
                sp.dma_start(out_t[:, bass.ds(t, 1), :], res[:, slot:slot + 1, :]).then_inc(s_out[slot], 16)
            paired(sp, NT, store)
            sp.wait_ge(s_out[0], 16 * (NT - NT // 2))
            sp.wait_ge(s_out[1], 16 * (NT // 2))

        @block.tensor
        def _(pe):
            mlp.on_pe(pe, g["ident"])

        @block.scalar
        def _(act):
            mlp.on_act(act)

        @block.vector
        def _(v):
            c = Steps(v, s_dve)
            v.wait_ge(s_b2, 32)
            v.sem_inc(mlp.s_take, 2)
            wb, wc = g["wb"], g["wc"]

            def put(t):
                v.wait_ge(mlp.s_tr, t + 1)
                v.tensor_scalar(mlp.xin[:, t % 2, :], g["xn"][:, t, 0:D], 1.0, None, ALU.mult).then_inc(mlp.s_in, 1)

            def score(t):
                mine, lo, hi = wc[:, t:t + 1], t * TN, (t + 1) * TN
                c.done(v.scalar_tensor_tensor(out=eqm[:, :], in0=wb[:, lo:hi], scalar=mine, in1=lower[:, :], op0=ALU.is_equal, op1=ALU.mult))
                if t:
                    c.done(v.tensor_scalar(cmp[:, 0:lo], wb[:, 0:lo], mine, None, ALU.is_ge, ALU.add, accum_out=rank[:, 0, t:t + 1]))
                c.link(v.tensor_scalar(cmp[:, lo:N_NODES], wb[:, lo:N_NODES], mine, None, ALU.is_gt, ALU.add, accum_out=rank[:, 1, t:t + 1]))
                c.link(v.tensor_reduce(rank[:, 2, t:t + 1], eqm[:, :], AX.X, ALU.add))
                c.link(v.scalar_tensor_tensor(out=place[:, t:t + 1], in0=rank[:, 0, t:t + 1], scalar=rank[:, 1, t:t + 1],
                                              in1=rank[:, 2, t:t + 1], op0=ALU.add, op1=ALU.add))
                c.link(v.scalar_tensor_tensor(out=scale[:, t:t + 1], in0=place[:, t:t + 1], scalar=float(TOPK), in1=mine,
                                              op0=ALU.is_lt, op1=ALU.mult))

            def take(t):
                slot = t % 2
                v.wait_ge(mlp.s_y, t + 3)
                if t >= 2:
                    v.wait_ge(s_out[slot], 16 * (t // 2))
                c.link(v.tensor_tensor(res[:, slot, :], mlp.p_y[slot][0:TN, 0:D], b2[:, :], ALU.add))
                v.scalar_tensor_tensor(out=res[:, slot, :], in0=res[:, slot, :], scalar=scale[:, t:t + 1],
                                       in1=g["xacc"][:, t, :], op0=ALU.mult, op1=ALU.add).then_inc(mlp.s_take, 1)
            for t in range(3):
                put(t)
            c.link(v.memset(rank[:, :, :], 0.0))
            for t in range(NT):
                if t + 3 < NT:
                    put(t + 3)
                score(t)
                take(t)


def program(nc, a, out, stop=9):
    with ExitStack() as ctx:
        k = Kit(nc, ctx)
        scr = {
            "table": nc.dram_tensor("edge_table", [P * TCOLS, 1], I32).ap(),
            "counts": nc.dram_tensor("edge_counts", [NT * N_ET, TN], F32).ap(),
            "cpart": nc.dram_tensor("bias_parts", [2 * MH, PARTS * D], BF16).ap(),
            "kv": nc.dram_tensor("kv_rows", [N_NODES, 2 * D], F32).ap(),
        }
        g = {
            "xacc": k.sb("xacc", [TN, NT, D]),
            "ident": k.sb("ident", [P, P]),
            "ident_b": k.sb("ident_b", [P, P], BF16),
            "iota_n": k.sb("iota_n", [P, TN]),
            "tab": k.sb("tab", [1, ETILES // GRP], I32),
            "xn": k.sb("xn", [TN, NT, D + 1]),
            "xn_t": k.sb("xn_t", [P, KC, N_NODES]),
        }
        with ExitStack() as edges:
            ke = Kit(nc, edges)
            g["scat_idx"] = ke.sb("scat_idx", [P, EC], I32)
            g["record"] = ke.sb("record", [P, EC], I32)
            g["sq"] = ke.sb("sq", [TN, NT * 2 * MH])
            prepare(nc, a, g, scr)
            if stop > 1:
                mix(nc, a, g, scr)
        if stop > 1:
            mix_out(nc, a, g, scr)
        if stop > 2:
            gnn(nc, a, g, scr)
            gnn_out(nc, a, g, scr)
        if stop > 3:
            g["wb"] = k.sb("wb", [TN, N_NODES])
            g["wc"] = k.sb("wc", [TN, NT])
            route(nc, a, g, scr)
            ffn(nc, a, g, scr, out)


def layouts(inputs):
    import numpy as np

    f = {n: np.asarray(v) for n, v in inputs.items()}
    pad = N_PADDED - N_EDGES

    def edges(v, filler):
        return np.concatenate([v, np.full(pad, filler, v.dtype)]).reshape(P, EC)

    def lhs(w):
        w = w.reshape(w.shape[:-2] + (KC, P, w.shape[-1]))
        return np.moveaxis(w, -2, 0)

    wq, wk, wv = (f["L0_mix_" + n].transpose(1, 2, 0) for n in ("Wq", "Wk", "Wv"))
    flat = [f["L0_mix_" + n].reshape(D, HM) for n in ("Wq", "Wk")]
    bcols = [f["L0_mix_" + n].T for n in ("bq", "bk", "bv")]
    steps = [np.concatenate([lhs(wq[h]).reshape(P, -1), lhs(wk[h]).reshape(P, -1)], 1) for h in range(MH)]
    steps += [np.concatenate([lhs(wv[h]).reshape(P, -1), lhs(f["L0_mix_Wo"][h]).reshape(P, -1),
                              lhs(bcols[2][:, h:h + 1]).reshape(P, -1)], 1) for h in range(MH)]
    steps += [lhs(w[:, i:i + 2 * D]).reshape(P, -1) for w in flat for i in range(0, HM, 2 * D)]
    m_w = np.zeros((P, len(steps), 4 * D + KC), np.float32)
    for n, w in enumerate(steps):
        m_w[:, n, :w.shape[1]] = w
    sel = np.zeros((AUG, 2, HM), mybir.dt.np(BF16))
    for r in range(PARTS):
        for h in range(MH):
            sel[r * MH + h, :, h * D:(h + 1) * D] = 1
    def per_layer(w):
        return lhs(w).reshape(P, LAYERS, -1)

    G = {n: f["L0_gnn_" + n] for n in ("Win", "b_in", "Wq", "bq", "Wk", "bk", "Wv", "bv", "Eemb", "Wo", "bo",
                                       "ln_g", "ln_b", "W1", "b1", "W2", "b2")}
    tr = lambda w: np.swapaxes(w, -1, -2)
    gnn_in = {
        "g_win": lhs(tr(G["Win"])), "g_bin": G["b_in"],
        "g_wqkv": per_layer(np.concatenate([tr(G["Wk"]), tr(G["Wv"]), tr(G["Wq"])], -1)),
        "g_wo": per_layer(tr(G["Wo"])), "g_et": per_layer(tr(G["Eemb"])),
        "g_rows": np.concatenate([G["bk"], G["bv"], G["bq"], G["bo"], G["ln_g"], G["ln_b"]], 1),
        "g_w1": lhs(tr(G["W1"])), "g_w2": lhs(tr(G["W2"])), "g_b1": lhs(G["b1"][:, None])[:, :, 0], "g_b2": G["b2"],
        "f_wr": lhs(f["L0_ffn_wr"])[:, :, 0], "f_br": f["L0_ffn_br"], "f_w1": lhs(f["L0_ffn_w1"]),
        "f_w2": f["L0_ffn_w2"].reshape(FF // P, P, D).transpose(1, 0, 2),
        "f_b1": f["L0_ffn_b1"].reshape(FF // P, P).T, "f_b2": f["L0_ffn_b2"],
    }
    arr = {
        **gnn_in,
        "m_rows": np.concatenate([f["L0_mix_" + n] for n in ("g1", "beta1", "bias2", "g2", "beta2")]),
        "m_w1": lhs(f["L0_mix_W1"]), "m_w2": lhs(f["L0_mix_W2"]), "m_b1": lhs(f["L0_mix_bias1"][:, None])[:, :, 0],
        "c_lower": np.tril(np.ones((TN, TN), np.float32), -1),
        "m_w": m_w, "m_sel": sel, "m_bo": f["L0_mix_bo"],
        "m_pb": lhs(np.concatenate([f["L0_mix_proj"].T, bcols[0], bcols[1]], 1)),
        "x": f["x"],
        "src": edges(f["src"], N_NODES), "dst": edges(f["dst"], 0), "et": edges(f["edge_type_3"], 0),
        "c_ident": np.eye(P, dtype=np.float32),
        "c_tri": np.triu(np.ones((P, P), np.float32), 1),
        "c_iota_n": np.tile(np.arange(TN, dtype=np.float32), (P, 1)),
        "c_iota_e": np.tile(np.arange(TCOLS, dtype=np.float32), (P, 1)),
    }
    return {n: np.ascontiguousarray(v) for n, v in arr.items()}


def kernel(**inputs):
    import numpy as _np
    import concourse.bacc as _bacc
    from concourse import mybir as _mybir
    from concourse.bass_utils import run_bass_kernel_spmd as _run

    nc = _bacc.Bacc("TRN2", target_bir_lowering=False, num_devices=1)
    arrays = {"in_" + n: v for n, v in layouts(inputs).items()}
    aps = {n[3:]: nc.dram_tensor(n, v.shape, _mybir.dt.from_np(v.dtype), kind="ExternalInput").ap() for n, v in arrays.items()}
    out = nc.dram_tensor("out_0_dram", (N_NODES, D), _mybir.dt.float32, kind="ExternalOutput").ap()
    program(nc, aps, out)
    r = _run(nc, [arrays], core_ids=[0])
    return r.results[0]["out_0_dram"]
```
